# Optimizing a Trainium2 kernel written in Bass

```python
import numpy as np
import jax
import jax.numpy as jnp

def _softmax(x, axis=-1):
    return jax.nn.softmax(x, axis=axis)

def _gelu(x):
    return jax.nn.gelu(x, approximate=True)

def _silu(x):
    return jax.nn.silu(x)

def _sigmoid(x):
    return jax.nn.sigmoid(x)

def _layernorm(x, axis=-1, eps=1e-05):
    m = jnp.mean(x, axis=axis, keepdims=True)
    v = jnp.var(x, axis=axis, keepdims=True)
    return (x - m) / jnp.sqrt(v + eps)

def _scatter_add(tgt, idx, src, axis=0):
    return tgt.at[idx].add(src)

def _segment_sum(src, seg, n):
    return jax.ops.segment_sum(src, seg, n)
kernel_name = 'mk_prb_d2_jaxref_r8_c2f5c0'

def setup_inputs(seed: int=0):
    np.random.seed(seed)
    _w = jnp.asarray

    def _L0_attn_setup():
        import jax, jax.numpy as jnp
        import numpy as np
        D_MODEL = 256
        NUM_HEADS = 16
        D_K = D_MODEL // NUM_HEADS

        def _heads(t, B, S):
            return t.reshape(B, S, NUM_HEADS, D_K).transpose(0, 2, 1, 3)
        key = jax.random.key(seed)
        ks = jax.random.split(key, 9)
        s = 1.0 / np.sqrt(D_MODEL)
        x = jax.random.normal(ks[0], (4, 512, D_MODEL), dtype=jnp.float32)
        wq = jax.random.uniform(ks[1], (D_MODEL, D_MODEL), jnp.float32, -s, s)
        bq = jax.random.uniform(ks[2], (D_MODEL,), jnp.float32, -s, s)
        wk = jax.random.uniform(ks[3], (D_MODEL, D_MODEL), jnp.float32, -s, s)
        bk = jax.random.uniform(ks[4], (D_MODEL,), jnp.float32, -s, s)
        wv = jax.random.uniform(ks[5], (D_MODEL, D_MODEL), jnp.float32, -s, s)
        bv = jax.random.uniform(ks[6], (D_MODEL,), jnp.float32, -s, s)
        wo = jax.random.uniform(ks[7], (D_MODEL, D_MODEL), jnp.float32, -s, s)
        bo = jax.random.uniform(ks[8], (D_MODEL,), jnp.float32, -s, s)
        return {'x': x, 'wq': wq, 'bq': bq, 'wk': wk, 'bk': bk, 'wv': wv, 'bv': bv, 'wo': wo, 'bo': bo}
    _L0_attn_in = _L0_attn_setup()

    def _L0_ffn_setup():
        import jax, jax.numpy as jnp
        import numpy as np
        E = 32
        D = 256
        I = 176
        NG = 8
        TKG = 4
        TOPK = 8
        SCALE = 2.5
        SI = I * 2

        def _route(x, router_weight, e_bias):
            T = x.shape[0]
            scores = jax.nn.sigmoid(x @ router_weight.T)
            sfc = scores + e_bias[None, :]
            grp = sfc.reshape(T, NG, E // NG)
            top2, _ = jax.lax.top_k(grp, 2)
            group_scores = top2.sum(-1)
            _, gidx = jax.lax.top_k(group_scores, TKG)
            gmask = jnp.zeros((T, NG), sfc.dtype).at[jnp.arange(T)[:, None], gidx].set(1.0)
            smask = jnp.repeat(gmask, E // NG, axis=1)
            masked = jnp.where(smask > 0, sfc, 0.0)
            _, topk_idx = jax.lax.top_k(masked, TOPK)
            topk_w = jnp.take_along_axis(scores, topk_idx, axis=1)
            topk_w = topk_w / (topk_w.sum(-1, keepdims=True) + 1e-20)
            topk_w = topk_w * SCALE
            combine = jnp.zeros((T, E), scores.dtype).at[jnp.arange(T)[:, None], topk_idx].add(topk_w)
            return combine
        key = jax.random.key(seed)
        ks = jax.random.split(key, 8)
        s = 0.02
        return {'hidden_states': jax.random.normal(ks[0], (2, 256, D), jnp.float32), 'router_weight': jax.random.normal(ks[1], (E, D), jnp.float32) * s, 'e_bias': jnp.zeros((E,), jnp.float32), 'Wg': jax.random.normal(ks[2], (E, I, D), jnp.float32) * s, 'Wu': jax.random.normal(ks[3], (E, I, D), jnp.float32) * s, 'Wd': jax.random.normal(ks[4], (E, D, I), jnp.float32) * s, 'sWg': jax.random.normal(ks[5], (SI, D), jnp.float32) * s, 'sWu': jax.random.normal(ks[6], (SI, D), jnp.float32) * s, 'sWd': jax.random.normal(ks[7], (D, SI), jnp.float32) * s}
    _L0_ffn_in = _L0_ffn_setup()

    def _L1_attn_setup():
        import jax, jax.numpy as jnp
        import numpy as np
        B, L, H, NH = (2, 256, 256, 16)
        K = H // NH
        EPS = 1e-05
        SCALE = K ** (-0.5)

        def _gla(q, k, v, g):

            def step(S, xs):
                q_t, k_t, v_t, g_t = xs
                S = jnp.exp(g_t)[:, :, None] * S + k_t[:, :, None] * v_t[:, None, :]
                o_t = jnp.einsum('bk,bkv->bv', q_t, S)
                return (S, o_t)
            S0 = jnp.zeros((q.shape[0], q.shape[2], v.shape[2]), dtype=q.dtype)
            xs = (jnp.swapaxes(q, 0, 1), jnp.swapaxes(k, 0, 1), jnp.swapaxes(v, 0, 1), jnp.swapaxes(g, 0, 1))
            _, o = jax.lax.scan(step, S0, xs)
            return jnp.swapaxes(o, 0, 1)
        key = jax.random.key(seed)
        k0, k1, k2, k3, k4 = jax.random.split(key, 5)
        std = 0.02
        return {'hidden_states': jax.random.normal(k0, (B, L, H), dtype=jnp.float32), 'Wq': jax.random.normal(k1, (K, H), dtype=jnp.float32) * std, 'Wk': jax.random.normal(k2, (K, H), dtype=jnp.float32) * std, 'Wog': jax.random.normal(k3, (H, H), dtype=jnp.float32) * std, 'Wig': jax.random.normal(k4, (H, H), dtype=jnp.float32) * std, 'g_weight': jnp.ones((H,), dtype=jnp.float32)}
    _L1_attn_in = _L1_attn_setup()

    def _L1_ffn_setup():
        import jax, jax.numpy as jnp
        import numpy as np
        N_EXPERTS = 8
        TOP_K = 2
        N_GROUP = 4
        TOPK_GROUP = 2
        ROUTED_SCALE = 1.0

        def _group_limited_topk(scores):
            T, N = scores.shape
            E = N // N_GROUP
            group_scores = scores.reshape(T, N_GROUP, E).max(axis=-1)
            _, gidx = jax.lax.top_k(group_scores, TOPK_GROUP)
            gmask = jax.nn.one_hot(gidx, N_GROUP, dtype=scores.dtype).sum(1)
            smask = jnp.repeat(gmask, E, axis=1)
            masked = jnp.where(smask > 0, scores, jnp.zeros((), scores.dtype))
            topk_w, topk_i = jax.lax.top_k(masked, TOP_K)
            return (topk_w, topk_i)
        key = jax.random.key(seed)
        ks = jax.random.split(key, 8)
        B, S, H, F, FS, N = (2, 128, 256, 176, 352, N_EXPERTS)
        std = jnp.float32(0.02)
        return {'hidden_states': jax.random.normal(ks[0], (B, S, H), jnp.float32), 'gate_weight': jax.random.normal(ks[1], (N, H), jnp.float32) * std, 'gate_w': jax.random.normal(ks[2], (N, F, H), jnp.float32) * std, 'up_w': jax.random.normal(ks[3], (N, F, H), jnp.float32) * std, 'down_w': jax.random.normal(ks[4], (N, H, F), jnp.float32) * std, 'sh_gate_w': jax.random.normal(ks[5], (FS, H), jnp.float32) * std, 'sh_up_w': jax.random.normal(ks[6], (FS, H), jnp.float32) * std, 'sh_down_w': jax.random.normal(ks[7], (H, FS), jnp.float32) * std}
    _L1_ffn_in = _L1_ffn_setup()
    _d = {'L0_attn_x': _L0_attn_in['x'], 'L0_attn_wq': _L0_attn_in['wq'], 'L0_attn_bq': _L0_attn_in['bq'], 'L0_attn_wk': _L0_attn_in['wk'], 'L0_attn_bk': _L0_attn_in['bk'], 'L0_attn_wv': _L0_attn_in['wv'], 'L0_attn_bv': _L0_attn_in['bv'], 'L0_attn_wo': _L0_attn_in['wo'], 'L0_attn_bo': _L0_attn_in['bo'], 'L0_ffn_router_weight': _L0_ffn_in['router_weight'], 'L0_ffn_e_bias': _L0_ffn_in['e_bias'], 'L0_ffn_Wg': _L0_ffn_in['Wg'], 'L0_ffn_Wu': _L0_ffn_in['Wu'], 'L0_ffn_Wd': _L0_ffn_in['Wd'], 'L0_ffn_sWg': _L0_ffn_in['sWg'], 'L0_ffn_sWu': _L0_ffn_in['sWu'], 'L0_ffn_sWd': _L0_ffn_in['sWd'], 'L1_attn_Wq': _L1_attn_in['Wq'], 'L1_attn_Wk': _L1_attn_in['Wk'], 'L1_attn_Wog': _L1_attn_in['Wog'], 'L1_attn_Wig': _L1_attn_in['Wig'], 'L1_attn_g_weight': _L1_attn_in['g_weight'], 'L1_ffn_gate_weight': _L1_ffn_in['gate_weight'], 'L1_ffn_gate_w': _L1_ffn_in['gate_w'], 'L1_ffn_up_w': _L1_ffn_in['up_w'], 'L1_ffn_down_w': _L1_ffn_in['down_w'], 'L1_ffn_sh_gate_w': _L1_ffn_in['sh_gate_w'], 'L1_ffn_sh_up_w': _L1_ffn_in['sh_up_w'], 'L1_ffn_sh_down_w': _L1_ffn_in['sh_down_w']}
    _x0 = _d['L0_attn_x']
    _d['L0_attn_x'] = jax.random.normal(jax.random.fold_in(jax.random.key(seed), 1), (4, 512, 256), dtype=_x0.dtype)
    del _x0
    return _d

def reference(L0_attn_x, L0_attn_wq, L0_attn_bq, L0_attn_wk, L0_attn_bk, L0_attn_wv, L0_attn_bv, L0_attn_wo, L0_attn_bo, L0_ffn_router_weight, L0_ffn_e_bias, L0_ffn_Wg, L0_ffn_Wu, L0_ffn_Wd, L0_ffn_sWg, L0_ffn_sWu, L0_ffn_sWd, L1_attn_Wq, L1_attn_Wk, L1_attn_Wog, L1_attn_Wig, L1_attn_g_weight, L1_ffn_gate_weight, L1_ffn_gate_w, L1_ffn_up_w, L1_ffn_down_w, L1_ffn_sh_gate_w, L1_ffn_sh_up_w, L1_ffn_sh_down_w):

    def _L0_attn_ref(x, wq, bq, wk, bk, wv, bv, wo, bo):
        import jax, jax.numpy as jnp
        import numpy as np
        D_MODEL = 256
        NUM_HEADS = 16
        D_K = D_MODEL // NUM_HEADS

        def _heads(t, B, S):
            return t.reshape(B, S, NUM_HEADS, D_K).transpose(0, 2, 1, 3)
        B, S, _ = x.shape
        Q = _heads(x @ wq.T + bq, B, S)
        K = _heads(x @ wk.T + bk, B, S)
        V = _heads(x @ wv.T + bv, B, S)
        Q = jax.nn.elu(Q) + 1.0
        K = jax.nn.elu(K) + 1.0
        KV = jnp.einsum('bhsd,bhse->bhde', K, V)
        QKV = jnp.einsum('bhsd,bhde->bhse', Q, KV)
        K_sum = jnp.sum(K, axis=-2)
        QK_sum = jnp.einsum('bhsd,bhd->bhs', Q, K_sum)
        out = QKV / (QK_sum[..., None] + 1e-08)
        out = out.transpose(0, 2, 1, 3).reshape(B, S, D_MODEL)
        return out @ wo.T + bo

    def _L0_ffn_ref(hidden_states, router_weight, e_bias, Wg, Wu, Wd, sWg, sWu, sWd):
        import jax, jax.numpy as jnp
        import numpy as np
        E = 32
        D = 256
        I = 176
        NG = 8
        TKG = 4
        TOPK = 8
        SCALE = 2.5
        SI = I * 2

        def _route(x, router_weight, e_bias):
            T = x.shape[0]
            scores = jax.nn.sigmoid(x @ router_weight.T)
            sfc = scores + e_bias[None, :]
            grp = sfc.reshape(T, NG, E // NG)
            top2, _ = jax.lax.top_k(grp, 2)
            group_scores = top2.sum(-1)
            _, gidx = jax.lax.top_k(group_scores, TKG)
            gmask = jnp.zeros((T, NG), sfc.dtype).at[jnp.arange(T)[:, None], gidx].set(1.0)
            smask = jnp.repeat(gmask, E // NG, axis=1)
            masked = jnp.where(smask > 0, sfc, 0.0)
            _, topk_idx = jax.lax.top_k(masked, TOPK)
            topk_w = jnp.take_along_axis(scores, topk_idx, axis=1)
            topk_w = topk_w / (topk_w.sum(-1, keepdims=True) + 1e-20)
            topk_w = topk_w * SCALE
            combine = jnp.zeros((T, E), scores.dtype).at[jnp.arange(T)[:, None], topk_idx].add(topk_w)
            return combine
        orig = hidden_states.shape
        x = hidden_states.reshape(-1, orig[-1])
        combine = _route(x, router_weight, e_bias)

        def body(acc, ws):
            wg, wu, wd, cw = ws
            h = jax.nn.silu(x @ wg.T) * (x @ wu.T)
            return (acc + cw[:, None] * (h @ wd.T), None)
        acc, _ = jax.lax.scan(body, jnp.zeros_like(x), (Wg, Wu, Wd, combine.T))
        shared = jax.nn.silu(x @ sWg.T) * (x @ sWu.T) @ sWd.T
        return (acc + shared).reshape(orig)

    def _L1_attn_ref(hidden_states, Wq, Wk, Wog, Wig, g_weight):
        import jax, jax.numpy as jnp
        import numpy as np
        B, L, H, NH = (2, 256, 256, 16)
        K = H // NH
        EPS = 1e-05
        SCALE = K ** (-0.5)

        def _gla(q, k, v, g):

            def step(S, xs):
                q_t, k_t, v_t, g_t = xs
                S = jnp.exp(g_t)[:, :, None] * S + k_t[:, :, None] * v_t[:, None, :]
                o_t = jnp.einsum('bk,bkv->bv', q_t, S)
                return (S, o_t)
            S0 = jnp.zeros((q.shape[0], q.shape[2], v.shape[2]), dtype=q.dtype)
            xs = (jnp.swapaxes(q, 0, 1), jnp.swapaxes(k, 0, 1), jnp.swapaxes(v, 0, 1), jnp.swapaxes(g, 0, 1))
            _, o = jax.lax.scan(step, S0, xs)
            return jnp.swapaxes(o, 0, 1)
        x = hidden_states
        q = x @ Wq.T
        k_sig = jax.nn.sigmoid(x @ Wk.T)
        q = jax.nn.silu(q) * SCALE
        gf = jax.nn.log_sigmoid(-k_sig)
        o = _gla(q, k_sig, x, gf)
        go = o @ Wog.T + x @ Wig.T
        rms = o * jax.lax.rsqrt(jnp.mean(o * o, axis=-1, keepdims=True) + EPS) * g_weight
        return rms * go * jax.nn.sigmoid(go)

    def _L1_ffn_ref(hidden_states, gate_weight, gate_w, up_w, down_w, sh_gate_w, sh_up_w, sh_down_w):
        import jax, jax.numpy as jnp
        import numpy as np
        N_EXPERTS = 8
        TOP_K = 2
        N_GROUP = 4
        TOPK_GROUP = 2
        ROUTED_SCALE = 1.0

        def _group_limited_topk(scores):
            T, N = scores.shape
            E = N // N_GROUP
            group_scores = scores.reshape(T, N_GROUP, E).max(axis=-1)
            _, gidx = jax.lax.top_k(group_scores, TOPK_GROUP)
            gmask = jax.nn.one_hot(gidx, N_GROUP, dtype=scores.dtype).sum(1)
            smask = jnp.repeat(gmask, E, axis=1)
            masked = jnp.where(smask > 0, scores, jnp.zeros((), scores.dtype))
            topk_w, topk_i = jax.lax.top_k(masked, TOP_K)
            return (topk_w, topk_i)
        B, S, H = hidden_states.shape
        h = hidden_states.reshape(-1, H)
        logits = h.astype(jnp.float32) @ gate_weight.astype(jnp.float32).T
        scores = jax.nn.softmax(logits, axis=-1)
        topk_w, topk_i = _group_limited_topk(scores)
        topk_w = (topk_w * ROUTED_SCALE).astype(h.dtype)
        wmat = (jax.nn.one_hot(topk_i, N_EXPERTS, dtype=topk_w.dtype) * topk_w[..., None]).sum(axis=1)
        g = jnp.einsum('th,nfh->ntf', h, gate_w)
        u = jnp.einsum('th,nfh->ntf', h, up_w)
        e = jnp.einsum('ntf,nhf->nth', jax.nn.silu(g) * u, down_w)
        routed = jnp.einsum('nth,tn->th', e, wmat)
        sg = h @ sh_gate_w.T
        su = h @ sh_up_w.T
        shared = jax.nn.silu(sg) * su @ sh_down_w.T
        return (routed + shared).reshape(B, S, H)
    x = L0_attn_x
    xn = _layernorm(x, axis=-1)
    x = x + _L0_attn_ref(xn, L0_attn_wq, L0_attn_bq, L0_attn_wk, L0_attn_bk, L0_attn_wv, L0_attn_bv, L0_attn_wo, L0_attn_bo) + _L0_ffn_ref(xn, L0_ffn_router_weight, L0_ffn_e_bias, L0_ffn_Wg, L0_ffn_Wu, L0_ffn_Wd, L0_ffn_sWg, L0_ffn_sWu, L0_ffn_sWd)
    xn = _layernorm(x, axis=-1)
    x = x + _L1_attn_ref(xn, L1_attn_Wq, L1_attn_Wk, L1_attn_Wog, L1_attn_Wig, L1_attn_g_weight) + _L1_ffn_ref(xn, L1_ffn_gate_weight, L1_ffn_gate_w, L1_ffn_up_w, L1_ffn_down_w, L1_ffn_sh_gate_w, L1_ffn_sh_up_w, L1_ffn_sh_down_w)
    return x

_drawn_inputs = setup_inputs


def setup_inputs(seed=0):
    import zlib

    import numpy as np

    out = dict(_drawn_inputs(seed))
    spreads = {'L0_ffn_e_bias': (0.0, 0.627), 'L1_attn_g_weight': (1.0, 0.6)}
    factors = {'L0_attn_wq': 8.0,
     'L0_attn_bq': 41.237,
     'L0_attn_wk': 8.0,
     'L0_attn_bk': 121.826,
     'L0_attn_wv': 3.586,
     'L0_ffn_router_weight': 5.744,
     'L0_ffn_Wg': 4.211,
     'L0_ffn_Wu': 4.093,
     'L0_ffn_Wd': 4.12,
     'L1_attn_Wog': 19.961,
     'L1_ffn_gate_weight': 8.0,
     'L1_ffn_gate_w': 8.0,
     'L1_ffn_up_w': 8.0,
     'L1_ffn_down_w': 8.0,
     'L1_ffn_sh_gate_w': 2.95,
     'L1_ffn_sh_up_w': 2.925,
     'L1_ffn_sh_down_w': 2.926,
     'L1_attn_Wk': 7.5}
    for name, (base, spread) in spreads.items():
        noise = np.random.default_rng([zlib.crc32(name.encode()), seed]).standard_normal(out[name].shape)
        drawn = base * np.exp(spread * noise) if base else spread * noise
        out[name] = jnp.asarray(drawn.astype(out[name].dtype))
    for name, factor in factors.items():
        out[name] = (out[name] * factor).astype(out[name].dtype)
    return out
```

```python
from contextlib import ExitStack

import numpy as np

import concourse.bass as bass
from concourse import mybir

F32 = mybir.dt.float32
F32R = mybir.dt.float32r
ALU = mybir.AluOpType
ACT = mybir.ActivationFunctionType
AX_X = mybir.AxisListType.X

P = 128
D = 256
KD = D // P
BATCH, SEQ = 4, 512
T = BATCH * SEQ
BLK = 512
NBLK = T // BLK
NT = T // P
HEAD = 16
LN_EPS = 1e-5

E0, G0, F0 = 32, 8, 176
TOPG0, TOPK0, SCALE0 = 4, 8, 2.5
E1, G1, F1 = 8, 4, 176
TOPG1, TOPK1 = 2, 2
SHARED = 2 * F0
TILES0 = -(-(E0 * F0 + SHARED) // P)
TILES1 = -(-(E1 * F1 + SHARED) // P)
KC0, KC1 = 2 * E0 + 1, 2 * E1 + 1

CH = 32
NCH = SEQ // CH
GLA_SCALE = float(HEAD) ** -0.5

C_ID, C_HEADS, C_CAUSAL, C_START, C_TRI = 0, P, 2 * P, 3 * P, 3 * P + SEQ
C_ALL = C_TRI + G0 * G0 + G1 * G1 + E1 * E1 + 2
C_EPS, C_TINY = C_ALL - 2, C_ALL - 1
TINY = 1e-8

V_BQ, V_BO, V_GW, V_ROUTE0 = 0, 2, 4, 6
V_ROUTE1 = V_ROUTE0 + KD * E0
V_ALL = V_ROUTE1 + KD * E1
KV_RING = 3
R_BKV, R_EB = 0, 2 * D
R_ALL = R_EB + E0


class Phase:

    def __init__(self, layer, half, first):
        self.layer, self.half, self.first = layer, half, first
        self.tiles = (TILES0, TILES1)[layer]
        self.kc = (KC0, KC1)[layer]
        self.pairs = (self.tiles - 1) // 2
        self.rest = self.tiles - 2 * self.pairs
        self.peel = int(first == 0)
        self.last = first + self.tiles


PHASES = []
for _layer in range(2):
    for _half in range(2):
        PHASES.append(Phase(_layer, _half, PHASES[-1].last if PHASES else 0))
ALL_TILES = PHASES[-1].last


def needed(n):
    return not isinstance(n, int) or n > 0


def build(nc, x_t, w_attn, vecs, rows, consts, w_gla, moe0, moe1, expand0, expand1, out_t):
    with ExitStack() as ctx:
        def sb(name, shape, dt=F32):
            return ctx.enter_context(nc.sbuf_tensor(name, shape, dt))

        def sem(name):
            return ctx.enter_context(nc.semaphore(name))

        bank = [ctx.enter_context(nc.psum_tensor(f"bank{i}", [P, BLK], F32)) for i in range(8)]

        x = sb("x", [P, KD, T])
        xn = sb("xn", [P, KD, T])
        xn_hi = sb("xn_hi", [P, KD, T], F32R)
        xn_lo = sb("xn_lo", [P, KD, T], F32R)
        square = sb("square", [P, 2, KD, BLK])
        std = sb("std", [P, 2, BLK])

        cst = sb("cst", [P, C_ALL])
        vec = sb("vec", [P, V_ALL])
        row = sb("row", [P, R_ALL])
        mean_w = sb("mean_w", [P, P])

        a_hi = sb("a_hi", [P, KD, 2, BLK], F32R)
        a_lo = sb("a_lo", [P, KD, 2, BLK], F32R)
        wo_hi = sb("wo_hi", [P, KD, D], F32R)
        wo_lo = sb("wo_lo", [P, KD, D], F32R)

        w_raw = sb("w_raw", [P, 2, 3 * D])
        w_gu_hi = sb("w_gu_hi", [P, 2, 2 * D], F32R)
        w_gu_lo = sb("w_gu_lo", [P, 2, 2 * D], F32R)
        w_dn_hi = sb("w_dn_hi", [P, 2, D], F32R)
        w_dn_lo = sb("w_dn_lo", [P, 2, D], F32R)
        e_raw = sb("e_raw", [P, 2, P])
        e_sel = sb("e_sel", [P, 2, P], F32R)
        zero = sb("zero", [P, P], F32R)
        gate = sb("gate", [P, 2, BLK])
        h_hi = sb("h_hi", [P, 2, BLK], F32R)
        h_lo = sb("h_lo", [P, 2, BLK], F32R)
        q_exp = gate

        score = sb("score", [P, NT, E0])
        pick = sb("pick", [P, NT, E0])
        rep = sb("rep", [P, NT, E0])
        pair = [gate[:, n, :].rearrange("p (j t g a) -> p j t g a", j=2, t=NT, g=G0) for n in range(2)]
        group = sb("group", [P, NT, G0])
        compare = [square[:, n].rearrange("p k n -> p (k n)") for n in range(2)]
        rank = sb("rank", [P, NT, G0])
        top = sb("top", [P, NT, 8])
        tot = sb("tot", [P, NT, 1])
        comb = sb("comb", [P, NT, KC0])
        comb_t = sb("comb_t", [KC0, T], F32R)

        with ExitStack() as own0:
            def sb0(name, shape, dt=F32):
                return own0.enter_context(nc.sbuf_tensor(name, shape, dt))

            w0_raw = sb0("w0_raw", [P, KD, 4 * D])
            w0_hi = sb0("w0_hi", [P, KD, 3 * D], F32R)
            w0_lo = sb0("w0_lo", [P, KD, 3 * D], F32R)
            kv = sb0("kv", [P, 2, 2 * D])
            kv_exp = sb0("kv_exp", [P, 2, D])
            kv_hi = sb0("kv_hi", [P, KV_RING, 2 * D + 2], F32R)
            kv_lo = sb0("kv_lo", [P, KV_RING, 2 * D + 2], F32R)
            qf = sb0("qf", [P, 2, BLK])
            q_hi = sb0("q_hi", [P, 2, BLK], F32R)
            q_lo = sb0("q_lo", [P, 2, BLK], F32R)
            state = sb0("state", [P, 2, 2 * P])
            state_hi = sb0("state_hi", [P, 2, 2 * P], F32R)
            state_lo = sb0("state_lo", [P, 2, 2 * P], F32R)
            den = sb0("den", [P, 2, BLK])

        w1_raw = sb("w1_raw", [P, KD, 2 * HEAD + 2 * D])
        kq_hi = sb("kq_hi", [P, KD, 2, BATCH, P], F32R)
        kq_lo = sb("kq_lo", [P, KD, 2, BATCH, P], F32R)
        og_hi = sb("og_hi", [P, KD, 2 * D], F32R)
        og_lo = sb("og_lo", [P, KD, 2 * D], F32R)
        rec_q = sb("rec_q", [P, SEQ])
        rec_k = sb("rec_k", [P, SEQ])
        run = sb("run", [P, SEQ])
        q_bd = sb("q_bd", [P, NCH, BATCH, CH])
        k_bd = sb("k_bd", [P, NCH, BATCH, CH])
        e_bd = sb("e_bd", [P, NCH, BATCH, CH])
        x_chunk = sb("x_chunk", [P, 2, KD, BATCH, CH])
        sc = sb("sc", [P, 2, P])
        ke = sb("ke", [P, 2, P])
        v_nat = gate[:, 0, :].rearrange("p (j n) -> p j n", j=2)
        s_st = gate[:, 1, :].rearrange("p (j n) -> p j n", j=2)

        def f(ap):
            return ap.bitcast(F32)

        x_in = [sem(f"x_in{c}") for c in range(NBLK)]
        const_in = sem("const_in")
        small_in = sem("small_in")
        const_made = sem("const_made")
        raw_in = [sem(f"raw_in{b}") for b in range(2)]
        mean_done = sem("mean_done")
        centred = sem("centred")
        squared = sem("squared")
        var_done = sem("var_done")
        std_done = sem("std_done")
        normed = sem("normed")
        norm_hi = sem("norm_hi")
        norm_lo = sem("norm_lo")
        small_hi_done = sem("small_hi_done")
        small_lo_done = sem("small_lo_done")
        logits_done = sem("logits_done")
        score_done = sem("score_done")
        comb_done = sem("comb_done")
        comb_tp = sem("comb_tp")
        comb_t_done = sem("comb_t_done")
        kv_mm = sem("kv_mm")
        kv_biased = sem("kv_biased")
        kv_min = sem("kv_min")
        kv_exped = sem("kv_exped")
        kv_full = sem("kv_full")
        kv_hi_done = sem("kv_hi_done")
        kv_lo_done = sem("kv_lo_done")
        q_mm = sem("q_mm")
        q_biased = sem("q_biased")
        q_min = sem("q_min")
        q_exped = sem("q_exped")
        q_full = sem("q_full")
        q_hi_done = sem("q_hi_done")
        q_lo_done = sem("q_lo_done")
        state_mm = sem("state_mm")
        state_masked = sem("state_masked")
        state_hi_done = sem("state_hi_done")
        state_lo_done = sem("state_lo_done")
        ratio_mm = sem("ratio_mm")
        den_done = sem("den_done")
        attn_done = sem("attn_done")
        attn_hi_done = sem("attn_hi_done")
        attn_lo_done = sem("attn_lo_done")
        gu_hi_done = sem("gu_hi_done")
        gu_lo_done = sem("gu_lo_done")
        dn_hi_done = sem("dn_hi_done")
        dn_lo_done = sem("dn_lo_done")
        cw_mm = sem("cw_mm")
        gate_mm = sem("gate_mm")
        up_mm = sem("up_mm")
        down_mm = sem("down_mm")
        silu_done = sem("silu_done")
        weighted = sem("weighted")
        hid_done = sem("hid_done")
        h_hi_done = sem("h_hi_done")
        h_lo_done = sem("h_lo_done")
        acc_read = sem("acc_read")
        stored = sem("stored")
        gla_kq_mm = sem("gla_kq_mm")
        gla_act = sem("gla_act")
        gla_ready = sem("gla_ready")
        chunk_in = sem("chunk_in")
        v_tp = sem("v_tp")
        v_done = sem("v_done")
        sc_mm = sem("sc_mm")
        sc_done = sem("sc_done")
        ke_tp = sem("ke_tp")
        ke_done = sem("ke_done")
        upd_mm = sem("upd_mm")
        s_done = sem("s_done")
        o_mm = sem("o_mm")
        o_done = sem("o_done")
        o_hi_done = sem("o_hi_done")
        o_lo_done = sem("o_lo_done")
        osq_done = sem("osq_done")
        ms_mm = sem("ms_mm")
        rms_std = sem("rms_std")
        go_mm = sem("go_mm")
        go_silu = sem("go_silu")
        y_done = sem("y_done")
        chain = sem("chain")
        pool_chain = sem("pool_chain")

        block = ctx.enter_context(nc.Block())

        def blk(c):
            return slice(c * BLK, (c + 1) * BLK)

        @block.sync
        def _(sp):
            sp.dma_start(x[:, :, blk(0)], x_t[:, :, blk(0)]).then_inc(x_in[0], 16)
            sp.dma_start(cst[:], consts).then_inc(const_in, 16)
            sp.dma_start(vec[:], vecs).then_inc(const_in, 16)
            sp.dma_start(row[:], rows.partition_broadcast(P)).then_inc(const_in, 16)
            for c in range(1, NBLK):
                sp.dma_start(x[:, :, blk(c)], x_t[:, :, blk(c)]).then_inc(x_in[c], 16)
            sp.dma_start(w0_raw[:], w_attn).then_inc(small_in, 16)

            def load_tile(ph, n, m):
                src, sel = ((moe0, expand0), (moe1, expand1))[ph.layer]
                sp.dma_start(w_raw[:, n % 2, :], src[m]).then_inc(raw_in[n % 2], 16)
                sp.dma_start(e_raw[0:ph.kc, n % 2, :], sel[m]).then_inc(raw_in[n % 2], 16)

            for ph in PHASES:
                if ph.layer == 1 and ph.half == 0:
                    sp.wait_ge(attn_done, 2 * BATCH)
                    sp.dma_start(w1_raw[:], w_gla).then_inc(small_in, 16)
                for m in range(2):
                    n = ph.first + m
                    if n >= 2:
                        sp.wait_ge(dn_lo_done, n - 1)
                        sp.wait_ge(gu_lo_done, n - 1)
                    load_tile(ph, n, m)
                with sp.Fori(0, (ph.tiles - 2) // 2) as i:
                    for j in range(2):
                        n = ph.first + 2 + j
                        sp.wait_ge(dn_lo_done, 2 * i + (n - 1))
                        sp.wait_ge(gu_lo_done, 2 * i + (n - 1))
                        src, sel = ((moe0, expand0), (moe1, expand1))[ph.layer]
                        b = n % 2
                        sp.dma_start(w_raw[:, b, :], src[bass.ds(2 * i + (2 + j), 1), :, :]
                                     .rearrange("a p n -> p (a n)")).then_inc(raw_in[b], 16)
                        sp.dma_start(e_raw[0:ph.kc, b, :], sel[bass.ds(2 * i + (2 + j), 1), :, :]
                                     .rearrange("a p n -> p (a n)")).then_inc(raw_in[b], 16)
                if ph.tiles % 2:
                    n = ph.last - 1
                    sp.wait_ge(dn_lo_done, n - 1)
                    sp.wait_ge(gu_lo_done, n - 1)
                    load_tile(ph, n, ph.tiles - 1)
            for half in range(2):
                for a in range(4):
                    kd, c = a // 2, 2 * half + a % 2
                    sp.wait_ge(acc_read, 8 + 4 * half + a + 1)
                    sp.dma_start(out_t[:, kd, blk(c)], x[:, kd, blk(c)]).then_inc(stored, 16)
            sp.wait_ge(stored, 16 * 8)

        @block.gpsimd
        def _(pool):
            nc.gpsimd.memset(mean_w[:], 1.0 / D).then_inc(const_made, 1)
            nc.gpsimd.memset(f(kv_hi[:, :, 2 * D:2 * D + 2]), 1.0).then_inc(const_made, 1)
            nc.gpsimd.memset(f(kv_lo[:, :, 2 * D:2 * D + 2]), 0.0).then_inc(const_made, 1)
            nc.gpsimd.memset(f(zero[:]), 0.0).then_inc(const_made, 1)

            pool.wait_ge(small_hi_done, 2)
            nc.gpsimd.tensor_tensor(w0_lo[:], w0_raw[:, :, 0:3 * D], f(w0_hi[:]), ALU.subtract)\
                .then_inc(small_lo_done, 1)
            nc.gpsimd.tensor_tensor(wo_lo[:], w0_raw[:, :, 3 * D:4 * D], f(wo_hi[:]), ALU.subtract)\
                .then_inc(small_lo_done, 1)

            def kv_low(t):
                pool.wait_ge(kv_hi_done, t + 1)
                if t >= KV_RING:
                    pool.wait_ge(state_mm, t - KV_RING + 1)
                nc.gpsimd.tensor_tensor(kv_lo[:, t % KV_RING, 0:2 * D], kv[:, t % 2, :],
                                        f(kv_hi[:, t % KV_RING, 0:2 * D]), ALU.subtract).then_inc(kv_lo_done, 1)

            for b in range(BATCH):
                kv_low(4 * b)
                kv_low(4 * b + 1)
                for m in range(2):
                    u = 2 * b + m
                    pool.wait_ge(q_hi_done, u + 1)
                    if b >= 1:
                        pool.wait_ge(ratio_mm, 2 * (b - 1) + m + 1)
                    nc.gpsimd.tensor_tensor(q_lo[:, m, :], qf[:, m, :], f(q_hi[:, m, :]),
                                            ALU.subtract).then_inc(q_lo_done, 1)
                kv_low(4 * b + 2)
                kv_low(4 * b + 3)

            pool.wait_ge(attn_done, 2 * BATCH)
            for z in (q_bd[:], k_bd[:], e_bd[:], f(kq_hi[:]), f(kq_lo[:])):
                last = nc.gpsimd.memset(z, 0.0)
            last.then_inc(pool_chain, 1)
            pool.wait_ge(small_in, 32)
            nc.gpsimd.tensor_copy(og_hi[:], w1_raw[:, :, 2 * HEAD:]).then_inc(pool_chain, 1)
            pool.wait_ge(pool_chain, 2)
            raw = w1_raw[:, :, 0:2 * HEAD].rearrange("p k (w h) -> p k w h", w=2)
            for b in range(BATCH):
                own = (slice(None), slice(None), slice(None), b, slice(32 * b, 32 * b + HEAD))
                nc.gpsimd.tensor_copy(kq_hi[own], raw).then_inc(pool_chain, 1)
            nc.gpsimd.tensor_tensor(og_lo[:], w1_raw[:, :, 2 * HEAD:], f(og_hi[:]), ALU.subtract)\
                .then_inc(small_lo_done, 1)
            pool.wait_ge(pool_chain, 2 + BATCH)
            for b in range(BATCH):
                own = (slice(None), slice(None), slice(None), b, slice(32 * b, 32 * b + HEAD))
                nc.gpsimd.tensor_tensor(kq_lo[own], raw, f(kq_hi[own]), ALU.subtract).then_inc(small_lo_done, 1)

            pool.wait_ge(normed, 2 * NBLK)
            for i in range(NCH):
                if i >= 2:
                    pool.wait_ge(v_tp, i - 1)
                nc.gpsimd.tensor_copy(x_chunk[:, i % 2],
                                      xn[:].rearrange("p k (b c s) -> p c k b s", b=BATCH, s=CH)[:, i])\
                    .then_inc(chunk_in, 1)

        @block.tensor
        def _(pe):
            def three(out, w, wsl, m, msl, start, stop):
                (wh, wl), (mh, ml) = w, m
                pe.matmul(out, wh[wsl], mh[msl], start=start, stop=False, skip_group_check=True)
                pe.matmul(out, wh[wsl], ml[msl], start=False, stop=False, skip_group_check=True)
                return pe.matmul(out, wl[wsl], mh[msl], start=False, stop=stop, skip_group_check=True)

            XN = (xn_hi, xn_lo)
            W0, WO = (w0_hi, w0_lo), (wo_hi, wo_lo)
            KQ, OG = (kq_hi, kq_lo), (og_hi, og_lo)
            everything = slice(None)

            def norm_stats(layer):
                for c in range(NBLK):
                    if layer == 0:
                        pe.wait_ge(x_in[c], 16)
                        if c == 0:
                            pe.wait_ge(const_made, 1)
                    for k in range(KD):
                        mm = pe.matmul(bank[c][:], mean_w[:], x[:, k, blk(c)], start=k == 0, stop=k == 1)
                    mm.then_inc(mean_done, 1)
                for c in range(NBLK):
                    pe.wait_ge(squared, NBLK * layer + c + 1)
                    for k in range(KD):
                        mm = pe.matmul(bank[4 + c][:], mean_w[:], square[:, c % 2, k, :], start=k == 0, stop=k == 1)
                    mm.then_inc(var_done, 1)

            def logits(layer):
                n_e, v0 = ((E0, V_ROUTE0), (E1, V_ROUTE1))[layer]
                for t in range(NT):
                    for k in range(KD):
                        mm = pe.matmul(bank[3][:, t * n_e:(t + 1) * n_e], xn[:, k, t * P:(t + 1) * P],
                                       vec[:, v0 + k * n_e:v0 + (k + 1) * n_e], start=k == 0, stop=k == 1)
                mm.then_inc(logits_done, 1)

            def combine_transposes(layer):
                kc = (KC0, KC1)[layer]
                pe.wait_ge(comb_done, layer + 1)
                for c in range(NBLK):
                    if c >= 2:
                        pe.wait_ge(comb_t_done, NBLK * layer + c - 1)
                    for j in range(4):
                        mm = pe.transpose(bank[c % 2][0:kc, j * P:(j + 1) * P],
                                          comb[:, 4 * c + j, 0:kc], cst[:, C_ID:C_ID + P])
                    mm.then_inc(comb_tp, 1)

            norm_stats(0)
            pe.wait_ge(norm_lo, NBLK)
            pe.wait_ge(const_in, 48)
            logits(0)
            pe.wait_ge(small_lo_done, 2)
            pe.wait_ge(score_done, 1)

            def kv_product(t):
                if t >= 2:
                    pe.wait_ge(kv_biased, t - 1)
                for k in range(KD):
                    mm = three(bank[t % 2][:], XN, (everything, k, slice(t * P, t * P + P)),
                               W0, (everything, k, slice(D, 3 * D)), k == 0, k == 1)
                mm.then_inc(kv_mm, 1)

            def query_product(b):
                for m in range(2):
                    u = 2 * b + m
                    if u >= 2:
                        pe.wait_ge(q_biased, u - 1)
                    for k in range(KD):
                        mm = three(bank[2 + m][:], W0, (everything, k, slice(m * P, m * P + P)),
                                   XN, (everything, k, blk(b)), k == 0, k == 1)
                    mm.then_inc(q_mm, 1)

            def state_product(t):
                b, j, r = t // 4, t % 4, t % KV_RING
                pe.wait_ge(kv_lo_done, t + 1)
                if j == 0 and b >= 1:
                    pe.wait_ge(state_masked, 2 * b)
                for hb in range(2):
                    mm = three(bank[4 + hb][:, 0:D + 2], (kv_hi, kv_lo), (everything, r, slice(hb * P, hb * P + P)),
                               (kv_hi, kv_lo), (everything, r, slice(D, 2 * D + 2)), j == 0, j == 3)
                mm.then_inc(state_mm, 1)

            def ratio_product(b):
                for hb in range(2):
                    u = 2 * b + hb
                    pe.wait_ge(state_lo_done, u + 1)
                    pe.wait_ge(q_lo_done, u + 1)
                    if u >= 1:
                        pe.wait_ge(attn_done, u)
                    for r in range(2):
                        mm = three(bank[6 + r][:], (state_hi, state_lo), (everything, hb, slice(r * P, r * P + P)),
                                   (q_hi, q_lo), (everything, hb, everything), True, True)
                    mm.then_inc(ratio_mm, 1)

            pe.wait_ge(const_made, 4)
            for b in range(BATCH):
                for j in range(4):
                    t = 4 * b + j
                    kv_product(t)
                    if t >= 1:
                        state_product(t - 1)
                    if j == 1:
                        if b >= 1:
                            ratio_product(b - 1)
                        query_product(b)
            state_product(NT - 1)
            ratio_product(BATCH - 1)
            pe.wait_ge(kv_biased, NT)
            combine_transposes(0)

            def unit_front(ph, i, tb, ub):
                par, s, u, tile = tb % 2, ub % 2, 4 * i + ub, 2 * i + tb
                toks = blk(2 * ph.half + s)
                pe.wait_ge(gu_lo_done, tile + 1)
                if needed(u):
                    pe.wait_ge(weighted, u)
                pe.matmul(bank[2][:], e_sel[0:ph.kc, par, :], comb_t[0:ph.kc, toks],
                          start=True, stop=True).then_inc(cw_mm, 1)
                if needed(u):
                    pe.wait_ge(silu_done, u)
                for k in range(KD):
                    mm = three(bank[0][:], (w_gu_hi, w_gu_lo), (everything, par, slice(k * P, k * P + P)),
                               XN, (everything, k, toks), k == 0, k == 1)
                mm.then_inc(gate_mm, 1)
                if needed(u):
                    pe.wait_ge(hid_done, u)
                for k in range(KD):
                    mm = three(bank[1][:], (w_gu_hi, w_gu_lo), (everything, par, slice(D + k * P, D + k * P + P)),
                               XN, (everything, k, toks), k == 0, k == 1)
                mm.then_inc(up_mm, 1)

            def unit_down(ph, i, tb, ub, last=False):
                par, s, u, tile = tb % 2, ub % 2, 4 * i + ub, 2 * i + tb
                pe.wait_ge(dn_lo_done, tile + 1)
                pe.wait_ge(h_lo_done, u + 1)
                for m in range(KD):
                    mm = three(bank[4 + 2 * m + s][:], (w_dn_hi, w_dn_lo), (everything, par, slice(m * P, m * P + P)),
                               (h_hi, h_lo), (everything, s, everything), False, last)
                mm.then_inc(down_mm, 1)

            def experts(ph, begin):
                t0 = ph.first
                unit_front(ph, 0, t0, 2 * t0)
                begin()

                def two_tiles(i):
                    for j in range(4):
                        unit_front(ph, i, t0 + (j + 1) // 2, 2 * t0 + j + 1)
                        unit_down(ph, i, t0 + j // 2, 2 * t0 + j)

                if ph.peel:
                    two_tiles(0)
                with pe.Fori(ph.peel, ph.pairs) as i:
                    two_tiles(i)
                for u in range(2 * (t0 + 2 * ph.pairs), 2 * ph.last):
                    if u + 1 < 2 * ph.last:
                        unit_front(ph, 0, (u + 1) // 2, u + 1)
                    unit_down(ph, 0, u // 2, u, last=u // 2 == ph.last - 1)

            def begin0(half):
                def go():
                    pe.wait_ge(attn_lo_done, 2 * half + 2)
                    for m in range(KD):
                        for s in range(2):
                            if half == 1:
                                pe.wait_ge(acc_read, 2 * m + s + 1)
                            for k in range(KD):
                                three(bank[4 + 2 * m + s][:], WO, (everything, k, slice(m * P, m * P + P)),
                                      (a_hi, a_lo), (everything, k, s, everything), k == 0, False)
                return go

            def begin1(half):
                def go():
                    for m in range(KD):
                        for s in range(2):
                            if half == 1:
                                pe.wait_ge(acc_read, 8 + 2 * m + s + 1)
                            pe.matmul(bank[4 + 2 * m + s][:], zero[:], xn_hi[:, 0, blk(0)],
                                      start=True, stop=False, skip_group_check=True)
                return go

            pe.wait_ge(comb_t_done, NBLK)
            pe.wait_ge(attn_done, 2 * BATCH)
            pe.wait_ge(state_masked, 2 * BATCH)
            experts(PHASES[0], begin0(0))
            experts(PHASES[1], begin0(1))

            pe.wait_ge(acc_read, 8)
            norm_stats(1)
            pe.wait_ge(norm_lo, 2 * NBLK)
            logits(1)
            pe.wait_ge(small_lo_done, 3 + BATCH)
            for w in range(2):
                for b in range(BATCH):
                    for k in range(KD):
                        mm = three(bank[w][:], KQ, (everything, k, w, b, everything),
                                   XN, (everything, k, blk(b)), b == 0 and k == 0, b == 3 and k == 1)
                mm.then_inc(gla_kq_mm, 1)
            pe.wait_ge(gla_ready, 1)
            pe.wait_ge(score_done, 2)

            def chunk_front(i):
                pe.wait_ge(chunk_in, i + 1)
                if i >= 1:
                    pe.wait_ge(v_done, i)
                for k in range(KD):
                    mm = pe.transpose(bank[0][:, k * P:(k + 1) * P],
                                      x_chunk[:, i % 2, k].rearrange("p b s -> p (b s)"),
                                      cst[:, C_ID:C_ID + P])
                mm.then_inc(v_tp, 1)
                if i >= 1:
                    pe.wait_ge(ke_done, i)
                pe.transpose(bank[1][:, 0:P], e_bd[:, i].rearrange("p b s -> p (b s)"),
                             cst[:, C_ID:C_ID + P]).then_inc(ke_tp, 1)
                if i >= 1:
                    pe.wait_ge(sc_done, i)
                pe.matmul(bank[2][:, 0:P], k_bd[:, i].rearrange("p b s -> p (b s)"),
                          q_bd[:, i].rearrange("p b s -> p (b s)"), start=True, stop=True).then_inc(sc_mm, 1)

            def chunk_back(i):
                pe.wait_ge(v_done, i + 1)
                pe.wait_ge(ke_done, i + 1)
                if i >= 1:
                    pe.wait_ge(s_done, i)
                pe.matmul(bank[3][:, 0:D], ke[:, i % 2, :], v_nat[:, i % 2, :], start=True, stop=True)\
                    .then_inc(upd_mm, 1)
                pe.wait_ge(sc_done, i + 1)
                if i >= 2:
                    pe.wait_ge(o_done, i - 1)
                ob = bank[4 + i % 2]
                for m in range(KD):
                    o = ob[:, m * P:(m + 1) * P]
                    pe.matmul(o, v_nat[:, i % 2, m * P:(m + 1) * P], sc[:, i % 2, :], start=True, stop=False,
                              skip_group_check=True)
                    mm = pe.matmul(o, s_st[:, i % 2, m * P:(m + 1) * P],
                                   q_bd[:, i].rearrange("p b s -> p (b s)"), start=False, stop=True,
                                   skip_group_check=True)
                mm.then_inc(o_mm, 1)

            chunk_front(0)
            for i in range(NCH):
                if i + 1 < NCH:
                    chunk_front(i + 1)
                chunk_back(i)
            for c in range(NBLK):
                pe.wait_ge(osq_done, c + 1)
                if c == 0:
                    pe.wait_ge(o_done, NCH)
                if c >= 1:
                    pe.wait_ge(rms_std, c)
                for k in range(KD):
                    mm = pe.matmul(bank[6][:], mean_w[:], square[:, c % 2, k, :], start=k == 0, stop=k == 1)
                mm.then_inc(ms_mm, 1)
                pe.wait_ge(o_lo_done, c + 1)
                for m in range(KD):
                    u = 2 * c + m
                    if u >= 2:
                        pe.wait_ge(go_silu, u - 1)
                    for k in range(KD):
                        three(bank[4 + m][:], OG, (everything, k, slice(m * P, m * P + P)),
                              (a_hi, a_lo), (everything, k, c % 2, everything), k == 0, False)
                    for k in range(KD):
                        mm = three(bank[4 + m][:], OG, (everything, k, slice(D + m * P, D + m * P + P)),
                                   XN, (everything, k, blk(c)), False, k == 1)
                    mm.then_inc(go_mm, 1)
            combine_transposes(1)
            pe.wait_ge(comb_t_done, 2 * NBLK)
            pe.wait_ge(go_silu, 2 * NBLK)
            experts(PHASES[2], begin1(0))
            experts(PHASES[3], begin1(1))

        @block.scalar
        def _(act):
            def norm(layer):
                for c in range(NBLK):
                    q = NBLK * layer + c
                    act.wait_ge(centred, q + 1)
                    if c >= 2:
                        act.wait_ge(var_done, q - 1)
                    nc.scalar.activation(square[:, c % 2], xn[:, :, blk(c)], ACT.Square).then_inc(squared, 1)
                    if c >= 1:
                        act_std(layer, c - 1)
                act_std(layer, NBLK - 1)
                for c in range(NBLK):
                    q = NBLK * layer + c
                    act.wait_ge(normed, q + 1)
                    nc.scalar.copy(xn_hi[:, :, blk(c)], xn[:, :, blk(c)]).then_inc(norm_hi, 1)

            def act_std(layer, c):
                q = NBLK * layer + c
                act.wait_ge(var_done, q + 1)
                if q >= 2:
                    act.wait_ge(normed, q - 1)
                nc.scalar.activation(std[:, c % 2, :], bank[4 + c][:], ACT.Sqrt,
                                     bias=cst[:, C_EPS:C_EPS + 1]).then_inc(std_done, 1)

            act.wait_ge(small_in, 16)
            nc.scalar.copy(w0_hi[:], w0_raw[:, :, 0:3 * D]).then_inc(small_hi_done, 1)
            nc.scalar.copy(wo_hi[:], w0_raw[:, :, 3 * D:4 * D]).then_inc(small_hi_done, 1)
            act.wait_ge(const_in, 48)
            norm(0)
            act.wait_ge(logits_done, 1)
            nc.scalar.activation(score[:].rearrange("p t e -> p (t e)"), bank[3][:], ACT.Sigmoid).then_inc(score_done, 1)

            def kv_e(t):
                act.wait_ge(kv_min, t + 1)
                nc.scalar.activation(kv_exp[:, t % 2, :], kv_exp[:, t % 2, :], ACT.Exp).then_inc(kv_exped, 1)

            def kv_h(t):
                act.wait_ge(kv_full, t + 1)
                if t >= KV_RING:
                    act.wait_ge(state_mm, t - KV_RING + 1)
                nc.scalar.copy(kv_hi[:, t % KV_RING, 0:2 * D], kv[:, t % 2, :]).then_inc(kv_hi_done, 1)

            def state_h(u):
                act.wait_ge(state_masked, u + 1)
                if u >= 2:
                    act.wait_ge(ratio_mm, u - 1)
                nc.scalar.copy(state_hi[:, u % 2, :], state[:, u % 2, :]).then_inc(state_hi_done, 1)

            def den_add(u):
                act.wait_ge(ratio_mm, u + 1)
                if u >= 2:
                    act.wait_ge(attn_done, u - 1)
                nc.scalar.activation(den[:, u % 2, :], bank[7][:], ACT.Identity, bias=cst[:, C_TINY:C_TINY + 1]).then_inc(den_done, 1)

            def attn_high(c):
                nc.scalar.copy(a_hi[:, :, c % 2, :], xn[:, :, blk(c)]).then_inc(attn_hi_done, 1)

            def kv_tile(t):
                kv_e(t)
                kv_h(t)

            def queries(b):
                for m in range(2):
                    act.wait_ge(q_min, 2 * b + m + 1)
                    nc.scalar.activation(q_exp[:, m, :], q_exp[:, m, :], ACT.Exp).then_inc(q_exped, 1)
                for m in range(2):
                    act.wait_ge(q_full, 2 * b + m + 1)
                    if b >= 1:
                        act.wait_ge(ratio_mm, 2 * (b - 1) + m + 1)
                    nc.scalar.copy(q_hi[:, m, :], qf[:, m, :]).then_inc(q_hi_done, 1)

            for b in range(BATCH + 1):
                if b < BATCH:
                    kv_tile(4 * b)
                if b >= 1:
                    for hb in range(2):
                        state_h(2 * (b - 1) + hb)
                if b < BATCH:
                    kv_tile(4 * b + 1)
                if b >= 1:
                    for hb in range(2):
                        den_add(2 * (b - 1) + hb)
                if b < BATCH:
                    queries(b)
                    kv_tile(4 * b + 2)
                    kv_tile(4 * b + 3)
            act.wait_ge(attn_done, 2 * BATCH)
            for c in range(2):
                attn_high(c)

            def comb_copy(layer):
                kc = (KC0, KC1)[layer]
                for c in range(NBLK):
                    act.wait_ge(comb_tp, NBLK * layer + c + 1)
                    nc.scalar.copy(comb_t[0:kc, blk(c)], bank[c % 2][0:kc, :]).then_inc(comb_t_done, 1)

            comb_copy(0)

            def split_gu(ph, i, tb):
                par = tb % 2
                act.wait_ge(raw_in[par], 32 * i + 32 * (tb // 2 + 1))
                if needed(4 * i + 2 * tb - 2):
                    act.wait_ge(up_mm, 4 * i + (2 * tb - 2))
                nc.scalar.copy(e_sel[0:ph.kc, par, :], e_raw[0:ph.kc, par, :]).then_inc(gu_hi_done, 1)
                nc.scalar.copy(w_gu_hi[:, par, :], w_raw[:, par, 0:2 * D]).then_inc(gu_hi_done, 1)

            def split_dn(i, tb):
                par = tb % 2
                if needed(4 * i + 2 * tb - 2):
                    act.wait_ge(down_mm, 4 * i + (2 * tb - 2))
                nc.scalar.copy(w_dn_hi[:, par, :], w_raw[:, par, 2 * D:3 * D]).then_inc(dn_hi_done, 1)

            def unit(ph_next, i, tb, ub):
                s = ub % 2
                act.wait_ge(gate_mm, 4 * i + (ub + 1))
                if needed(4 * i + ub - 1):
                    act.wait_ge(h_lo_done, 4 * i + (ub - 1))
                nc.scalar.activation(gate[:, s, :], bank[0][:], ACT.Silu).then_inc(silu_done, 1)
                if ph_next is not None:
                    if s == 0:
                        split_gu(ph_next, i, tb + 1)
                    else:
                        split_dn(i, tb + 1)
                act.wait_ge(hid_done, 4 * i + (ub + 1))
                if needed(4 * i + ub - 1):
                    act.wait_ge(down_mm, 4 * i + (ub - 1))
                nc.scalar.copy(h_hi[:, s, :], gate[:, s, :]).then_inc(h_hi_done, 1)

            def experts(ph):
                t0 = ph.first

                def two_tiles(i):
                    for j in range(4):
                        unit(ph, i, t0 + j // 2, 2 * t0 + j)

                if ph.peel:
                    two_tiles(0)
                with act.Fori(ph.peel, ph.pairs) as i:
                    two_tiles(i)
                for u in range(2 * (t0 + 2 * ph.pairs), 2 * ph.last):
                    tile = u // 2
                    nxt = ph if tile + 1 < ph.last else PHASES[PHASES.index(ph) + 1] if tile + 1 < ALL_TILES else None
                    unit(nxt, 0, tile, u)

            split_gu(PHASES[0], 0, 0)
            split_dn(0, 0)
            experts(PHASES[0])
            act.wait_ge(down_mm, 2 * PHASES[1].first)
            for c in range(2, 4):
                attn_high(c)
            experts(PHASES[1])

            norm(1)
            act.wait_ge(gla_kq_mm, 1)
            nc.scalar.activation(rec_q[:], bank[0][:], ACT.Silu).then_inc(gla_act, 1)
            act.wait_ge(gla_kq_mm, 2)
            nc.scalar.activation(rec_k[:], bank[1][:], ACT.Sigmoid).then_inc(gla_act, 1)
            act.wait_ge(gla_act, 2)
            nc.scalar.activation(std[:, 0, :], rec_k[:], ACT.Sigmoid, scale=-1.0).then_inc(gla_act, 1)
            act.wait_ge(score_done, 2)
            nc.scalar.activation(pick[:, :, 0:E1], score[:, :, 0:E1], ACT.Exp).then_inc(gla_act, 1)

            def chunk_act(i):
                act.wait_ge(v_tp, i + 1)
                if i >= 2:
                    act.wait_ge(o_mm, i - 1)
                nc.scalar.copy(v_nat[:, i % 2, :], bank[0][:, 0:D]).then_inc(v_done, 1)
                act.wait_ge(ke_tp, i + 1)
                if i >= 2:
                    act.wait_ge(upd_mm, i - 1)
                nc.scalar.copy(ke[:, i % 2, :], bank[1][:, 0:P]).then_inc(ke_done, 1)

            def o_out(i):
                act.wait_ge(o_mm, i + 1)
                for m in range(KD):
                    cp = nc.scalar.copy(
                        xn[:, m, :].rearrange("p (b c s) -> p c b s", b=BATCH, s=CH)[:, i],
                        bank[4 + i % 2][:, m * P:(m + 1) * P].rearrange("p (b s) -> p b s", b=BATCH))
                cp.then_inc(o_done, 1)

            for i in range(NCH):
                chunk_act(i)
                if i >= 1:
                    o_out(i - 1)
            o_out(NCH - 1)
            act.wait_ge(o_done, NCH)
            for c in range(NBLK):
                if c >= 2:
                    act.wait_ge(ms_mm, c - 1)
                nc.scalar.activation(square[:, c % 2], xn[:, :, blk(c)], ACT.Square).then_inc(osq_done, 1)
                if c >= 2:
                    act.wait_ge(go_mm, 2 * (c - 1))
                nc.scalar.copy(a_hi[:, :, c % 2, :], xn[:, :, blk(c)]).then_inc(o_hi_done, 1)
                act.wait_ge(ms_mm, c + 1)
                if c >= 2:
                    act.wait_ge(y_done, c - 1)
                nc.scalar.activation(std[:, c % 2, :], bank[6][:], ACT.Sqrt, bias=cst[:, C_EPS:C_EPS + 1]).then_inc(rms_std, 1)
                for m in range(KD):
                    act.wait_ge(go_mm, 2 * c + m + 1)
                    if c >= 1 and m == 0:
                        act.wait_ge(y_done, c)
                    nc.scalar.activation(q_exp[:, m, :], bank[4 + m][:], ACT.Silu).then_inc(go_silu, 1)
            comb_copy(1)
            act.wait_ge(y_done, NBLK)
            experts(PHASES[2])
            experts(PHASES[3])

        @block.vector
        def _(dve):
            links = [0]

            def link(ins):
                links[0] += 1
                ins.then_inc(chain, 1)
                dve.wait_ge(chain, links[0])

            v = nc.vector

            def over_width(ap):
                return ap.unsqueeze(1).to_broadcast([P, KD, BLK])

            def norm(layer):
                for c in range(NBLK):
                    q = NBLK * layer + c
                    dve.wait_ge(mean_done, q + 1)
                    v.tensor_tensor(xn[:, :, blk(c)], x[:, :, blk(c)], over_width(bank[c][:]),
                                    ALU.subtract).then_inc(centred, 1)
                for c in range(NBLK):
                    q = NBLK * layer + c
                    dve.wait_ge(std_done, q + 1)
                    dve.wait_ge(squared, q + 1)
                    link(v.reciprocal(std[:, c % 2, :], std[:, c % 2, :]))
                    v.tensor_tensor(xn[:, :, blk(c)], xn[:, :, blk(c)], over_width(std[:, c % 2, :]),
                                    ALU.mult).then_inc(normed, 1)
                    if c >= 1:
                        norm_low(q - 1, c - 1)
                norm_low(NBLK * layer + NBLK - 1, NBLK - 1)

            def norm_low(q, c):
                dve.wait_ge(norm_hi, q + 1)
                v.tensor_tensor(xn_lo[:, :, blk(c)], xn[:, :, blk(c)], f(xn_hi[:, :, blk(c)]),
                                ALU.subtract).then_inc(norm_lo, 1)

            def rank_below(values, n, tri, limit, out):
                a, b = (c[:, 0:NT * n * n].rearrange("p (t a b) -> p t a b", t=NT, a=n) for c in compare)
                own = values.unsqueeze(3).to_broadcast([P, NT, n, n])
                other = values.unsqueeze(2).to_broadcast([P, NT, n, n])
                v.tensor_tensor(a, other, own, ALU.is_gt)
                link(v.tensor_tensor(b, other, own, ALU.is_equal))
                link(v.tensor_tensor(b, b, tri.rearrange("p (a b) -> p a b", b=n).unsqueeze(1)
                                     .to_broadcast([P, NT, n, n]), ALU.mult))
                link(v.tensor_tensor(a, a, b, ALU.add))
                link(v.tensor_reduce(rank[:, :, 0:n], a, AX_X, ALU.add))
                link(v.tensor_scalar(out, rank[:, :, 0:n], float(limit), None, ALU.is_lt))

            def combine_parts(w, n_e):
                link(v.tensor_copy(comb[:, :, 0:n_e].bitcast(F32R), w))
                v.tensor_tensor(comb[:, :, n_e:2 * n_e], w, comb[:, :, 0:n_e], ALU.subtract)
                v.memset(comb[:, :, 2 * n_e:2 * n_e + 1], 1.0).then_inc(comb_done, 1)

            def route0():
                dve.wait_ge(score_done, 1)
                eb = row[:, R_EB:R_EB + E0].unsqueeze(1).to_broadcast([P, NT, E0])
                link(v.tensor_tensor(pick[:], score[:], eb, ALU.add))
                four = pick[:].rearrange("p t (g a b) -> p t g a b", g=G0, a=2)
                hi, lo = pair[0][:, 0], pair[0][:, 1]
                v.tensor_tensor(hi, four[:, :, :, :, 0], four[:, :, :, :, 1], ALU.max)
                link(v.tensor_tensor(lo, four[:, :, :, :, 0], four[:, :, :, :, 1], ALU.min))
                one, two, three_ = pair[1][:, 0, :, :, 0], pair[1][:, 0, :, :, 1], pair[1][:, 1, :, :, 0]
                v.tensor_tensor(one, hi[:, :, :, 0], hi[:, :, :, 1], ALU.max)
                link(v.tensor_tensor(two, hi[:, :, :, 0], hi[:, :, :, 1], ALU.min))
                link(v.tensor_tensor(three_, lo[:, :, :, 0], lo[:, :, :, 1], ALU.max))
                link(v.tensor_tensor(two, two, three_, ALU.max))
                link(v.tensor_tensor(group[:], one, two, ALU.add))
                rank_below(group[:], G0, cst[:, C_TRI:C_TRI + G0 * G0], TOPG0, group[:])
                link(v.tensor_tensor(pick[:].rearrange("p t (g e) -> p t g e", g=G0),
                                     pick[:].rearrange("p t (g e) -> p t g e", g=G0),
                                     group[:].unsqueeze(3).to_broadcast([P, NT, G0, E0 // G0]), ALU.mult))
                for t in range(NT):
                    m = v.max(top[:, t, :], pick[:, t, :])
                link(m)
                for t in range(NT):
                    m = v.match_replace(rep[:, t, :], top[:, t, :], pick[:, t, :], -3e38)
                link(m)
                link(v.tensor_tensor(rep[:], rep[:], pick[:], ALU.not_equal))
                link(v.tensor_tensor(rep[:], rep[:], score[:], ALU.mult))
                link(v.tensor_reduce(tot[:, :, 0], rep[:], AX_X, ALU.add))
                link(v.tensor_scalar(tot[:], tot[:], 1e-20, None, ALU.add))
                link(v.reciprocal(tot[:], tot[:]))
                link(v.tensor_tensor(rep[:], rep[:], tot[:].to_broadcast([P, NT, E0]), ALU.mult))
                link(v.tensor_scalar(rep[:], rep[:], SCALE0, None, ALU.mult))
                combine_parts(rep[:], E0)

            norm(0)
            dve.wait_ge(const_in, 48)
            route0()

            kv_bias = row[:, R_BKV:R_BKV + 2 * D]

            def kv_bias_min(t):
                dve.wait_ge(kv_mm, t + 1)
                if t >= 2:
                    dve.wait_ge(kv_lo_done, t - 1)
                    dve.wait_ge(kv_hi_done, t - 1)
                v.tensor_tensor(kv[:, t % 2, :], bank[t % 2][:], kv_bias, ALU.add).then_inc(kv_biased, 1)
                dve.wait_ge(kv_biased, t + 1)
                v.tensor_scalar(kv_exp[:, t % 2, :], kv[:, t % 2, 0:D], 0.0, None, ALU.min).then_inc(kv_min, 1)

            def kv_elu(t):
                dve.wait_ge(kv_exped, t + 1)
                v.scalar_tensor_tensor(out=kv[:, t % 2, 0:D], in0=kv[:, t % 2, 0:D], scalar=0.0,
                                       in1=kv_exp[:, t % 2, :], op0=ALU.max, op1=ALU.add).then_inc(kv_full, 1)

            def mask_state(u):
                b, hb = u // 2, u % 2
                heads = cst[:, C_HEADS:C_HEADS + P]
                dve.wait_ge(state_mm, 4 * b + 4)
                if u >= 2:
                    dve.wait_ge(state_lo_done, u - 1)
                v.tensor_tensor(state[:, hb, 0:P], bank[4 + hb][:, hb * P:hb * P + P], heads, ALU.mult)
                v.tensor_scalar(state[:, hb, P:2 * P], heads, bank[4 + hb][:, D:D + 1], None,
                                ALU.mult).then_inc(state_masked, 1)

            def state_low(u):
                dve.wait_ge(state_hi_done, u + 1)
                if u >= 2:
                    dve.wait_ge(ratio_mm, u - 1)
                v.tensor_tensor(state_lo[:, u % 2, :], state[:, u % 2, :], f(state_hi[:, u % 2, :]),
                                ALU.subtract).then_inc(state_lo_done, 1)

            def ratio(u):
                dve.wait_ge(den_done, u + 1)
                link(v.reciprocal(den[:, u % 2, :], den[:, u % 2, :]))
                dve.wait_ge(logits_done, 1)
                v.tensor_tensor(xn[:, u % 2, blk(u // 2)], bank[6][:], den[:, u % 2, :],
                                ALU.mult).then_inc(attn_done, 1)

            def attn_low(c):
                dve.wait_ge(attn_hi_done, c + 1)
                v.tensor_tensor(a_lo[:, :, c % 2, :], xn[:, :, blk(c)], f(a_hi[:, :, c % 2, :]),
                                ALU.subtract).then_inc(attn_lo_done, 1)

            def kv_tile(t):
                kv_bias_min(t)
                kv_elu(t)

            def queries(b):
                for m in range(2):
                    u = 2 * b + m
                    dve.wait_ge(q_mm, u + 1)
                    if b >= 1:
                        dve.wait_ge(q_lo_done, u - 1)
                    v.tensor_scalar(qf[:, m, :], bank[2 + m][:], vec[:, V_BQ + m:V_BQ + m + 1], None,
                                    ALU.add).then_inc(q_biased, 1)
                    dve.wait_ge(q_biased, u + 1)
                    v.tensor_scalar(q_exp[:, m, :], qf[:, m, :], 0.0, None, ALU.min).then_inc(q_min, 1)
                for m in range(2):
                    dve.wait_ge(q_exped, 2 * b + m + 1)
                    v.scalar_tensor_tensor(out=qf[:, m, :], in0=qf[:, m, :], scalar=0.0,
                                           in1=q_exp[:, m, :], op0=ALU.max, op1=ALU.add).then_inc(q_full, 1)

            for b in range(BATCH + 1):
                if b < BATCH:
                    kv_tile(4 * b)
                if b >= 1:
                    for hb in range(2):
                        mask_state(2 * (b - 1) + hb)
                    for hb in range(2):
                        state_low(2 * (b - 1) + hb)
                if b < BATCH:
                    kv_tile(4 * b + 1)
                if b >= 1:
                    for hb in range(2):
                        ratio(2 * (b - 1) + hb)
                if b < BATCH:
                    queries(b)
                    kv_tile(4 * b + 2)
                    kv_tile(4 * b + 3)
            for c in range(2):
                attn_low(c)

            def split_gu(i, tb):
                par = tb % 2
                dve.wait_ge(gu_hi_done, 4 * i + (2 * tb + 2))
                if needed(4 * i + 2 * tb - 2):
                    dve.wait_ge(up_mm, 4 * i + (2 * tb - 2))
                v.tensor_tensor(w_gu_lo[:, par, :], w_raw[:, par, 0:2 * D], f(w_gu_hi[:, par, :]),
                                ALU.subtract).then_inc(gu_lo_done, 1)

            def split_dn(i, tb):
                par = tb % 2
                dve.wait_ge(dn_hi_done, 2 * i + (tb + 1))
                if needed(4 * i + 2 * tb - 2):
                    dve.wait_ge(down_mm, 4 * i + (2 * tb - 2))
                v.tensor_tensor(w_dn_lo[:, par, :], w_raw[:, par, 2 * D:3 * D], f(w_dn_hi[:, par, :]),
                                ALU.subtract).then_inc(dn_lo_done, 1)

            def unit(split, i, tb, ub):
                s = ub % 2
                dve.wait_ge(silu_done, 4 * i + (ub + 1))
                dve.wait_ge(cw_mm, 4 * i + (ub + 1))
                v.tensor_tensor(gate[:, s, :], gate[:, s, :], bank[2][:], ALU.mult).then_inc(weighted, 1)
                dve.wait_ge(up_mm, 4 * i + (ub + 1))
                dve.wait_ge(weighted, 4 * i + (ub + 1))
                v.tensor_tensor(gate[:, s, :], gate[:, s, :], bank[1][:], ALU.mult).then_inc(hid_done, 1)
                if split:
                    if s == 0:
                        split_gu(i, tb + 1)
                    else:
                        split_dn(i, tb + 1)
                dve.wait_ge(h_hi_done, 4 * i + (ub + 1))
                if needed(4 * i + ub - 1):
                    dve.wait_ge(down_mm, 4 * i + (ub - 1))
                v.tensor_tensor(h_lo[:, s, :], gate[:, s, :], f(h_hi[:, s, :]), ALU.subtract).then_inc(h_lo_done, 1)

            def experts(ph):
                t0 = ph.first

                def two_tiles(i):
                    for j in range(4):
                        unit(True, i, t0 + j // 2, 2 * t0 + j)

                if ph.peel:
                    two_tiles(0)
                with dve.Fori(ph.peel, ph.pairs) as i:
                    two_tiles(i)
                for u in range(2 * (t0 + 2 * ph.pairs), 2 * ph.last):
                    unit(u // 2 + 1 < ALL_TILES, 0, u // 2, u)
                dve.wait_ge(down_mm, 2 * ph.last)
                dve.wait_ge(down_mm, 2 * ph.last)
                for a in range(4):
                    kd, c = a // 2, 2 * ph.half + a % 2
                    if ph.layer == 0:
                        v.scalar_tensor_tensor(out=x[:, kd, blk(c)], in0=bank[4 + a][:],
                                               scalar=vec[:, V_BO + kd:V_BO + kd + 1], in1=x[:, kd, blk(c)],
                                               op0=ALU.add, op1=ALU.add).then_inc(acc_read, 1)
                    else:
                        v.tensor_tensor(x[:, kd, blk(c)], bank[4 + a][:], x[:, kd, blk(c)],
                                        ALU.add).then_inc(acc_read, 1)

            split_gu(0, 0)
            split_dn(0, 0)
            experts(PHASES[0])
            for c in range(2, 4):
                attn_low(c)
            experts(PHASES[1])

            dve.wait_ge(acc_read, 8)
            norm(1)

            dve.wait_ge(logits_done, 2)
            lg = bank[3][:, 0:NT * E1].rearrange("p (t e) -> p t e", e=E1)
            w8 = score[:, :, 0:E1]
            link(v.tensor_reduce(tot[:, :, 0], lg, AX_X, ALU.max))
            v.tensor_tensor(w8, lg, tot[:].to_broadcast([P, NT, E1]), ALU.subtract).then_inc(score_done, 1)
            dve.wait_ge(gla_act, 3)
            decay, first = std[:, 0, :], std[:, 1, :]
            starts = cst[:, C_START:C_START + SEQ]
            link(v.tensor_tensor(first, decay, starts, ALU.mult))
            link(v.tensor_tensor(decay, decay, first, ALU.subtract))
            link(v.tensor_tensor_scan(run[:], decay, first, 0.0, ALU.mult, ALU.add))
            link(v.reciprocal(first, run[:]))
            link(v.scalar_tensor_tensor(out=rec_q[:], in0=rec_q[:], scalar=GLA_SCALE, in1=run[:],
                                        op0=ALU.mult, op1=ALU.mult))
            link(v.tensor_tensor(rec_k[:], rec_k[:], first, ALU.mult))
            ends = run[:].rearrange("p (c s) -> p c s", s=CH)[:, :, CH - 1:CH]
            link(v.tensor_tensor(decay.rearrange("p (c s) -> p c s", s=CH),
                                 rec_k[:].rearrange("p (c s) -> p c s", s=CH),
                                 ends.to_broadcast([P, NCH, CH]), ALU.mult))
            dve.wait_ge(pool_chain, 1)
            link(v.memset(s_st[:, 0, :], 0.0))
            for b in range(BATCH):
                r = slice(32 * b, 32 * b + 32)
                for dst, src in ((q_bd, rec_q[:]), (k_bd, rec_k[:]), (e_bd, decay)):
                    cp = v.tensor_copy(dst[r, :, b, :], src[r, :].rearrange("p (c s) -> p c s", s=CH))
            cp.then_inc(gla_ready, 1)

            dve.wait_ge(gla_act, 4)
            ex = pick[:, :, 0:E1]
            link(v.tensor_reduce(tot[:, :, 0], ex, AX_X, ALU.add))
            link(v.reciprocal(tot[:], tot[:]))
            link(v.tensor_tensor(ex, ex, tot[:].to_broadcast([P, NT, E1]), ALU.mult))
            two = ex.rearrange("p t (g e) -> p t g e", g=G1)
            gr = group[:, :, 0:G1]
            link(v.tensor_tensor(gr, two[:, :, :, 0], two[:, :, :, 1], ALU.max))
            t1 = C_TRI + G0 * G0
            rank_below(gr, G1, cst[:, t1:t1 + G1 * G1], TOPG1, gr)
            masked = rep[:, :, 0:E1]
            link(v.tensor_tensor(masked.rearrange("p t (g e) -> p t g e", g=G1), two,
                                 gr.unsqueeze(3).to_broadcast([P, NT, G1, E1 // G1]), ALU.mult))
            t1 += G1 * G1
            sel = rep[:, :, E1:2 * E1]
            rank_below(masked, E1, cst[:, t1:t1 + E1 * E1], TOPK1, sel)
            link(v.tensor_tensor(masked, masked, sel, ALU.mult))
            combine_parts(masked, E1)

            def chunk_scores(i):
                dve.wait_ge(sc_mm, i + 1)
                if i >= 2:
                    dve.wait_ge(o_mm, i - 1)
                v.tensor_tensor(sc[:, i % 2, :], bank[2][:, 0:P], cst[:, C_CAUSAL:C_CAUSAL + P],
                                ALU.mult).then_inc(sc_done, 1)

            def chunk_state(i):
                dve.wait_ge(upd_mm, i + 1)
                if i >= 1:
                    dve.wait_ge(o_mm, i)
                    dve.wait_ge(s_done, i)
                v.scalar_tensor_tensor(out=s_st[:, (i + 1) % 2, :], in0=s_st[:, i % 2, :],
                                       scalar=run[:, (i + 1) * CH - 1:(i + 1) * CH], in1=bank[3][:, 0:D],
                                       op0=ALU.mult, op1=ALU.add).then_inc(s_done, 1)

            chunk_scores(0)
            for i in range(NCH):
                if i + 1 < NCH:
                    chunk_scores(i + 1)
                chunk_state(i)
            for c in range(NBLK):
                dve.wait_ge(o_hi_done, c + 1)
                v.tensor_tensor(a_lo[:, :, c % 2, :], xn[:, :, blk(c)], f(a_hi[:, :, c % 2, :]),
                                ALU.subtract).then_inc(o_lo_done, 1)
                dve.wait_ge(rms_std, c + 1)
                dve.wait_ge(osq_done, c + 1)
                link(v.reciprocal(std[:, c % 2, :], std[:, c % 2, :]))
                link(v.tensor_tensor(xn[:, :, blk(c)], xn[:, :, blk(c)], over_width(std[:, c % 2, :]), ALU.mult))
                dve.wait_ge(go_silu, 2 * c + 2)
                for m in range(KD):
                    g = v.scalar_tensor_tensor(out=xn[:, m, blk(c)], in0=xn[:, m, blk(c)],
                                               scalar=vec[:, V_GW + m:V_GW + m + 1], in1=q_exp[:, m, :],
                                               op0=ALU.mult, op1=ALU.mult)
                g.then_inc(y_done, 1)
                dve.wait_ge(y_done, c + 1)
                link(v.tensor_tensor(x[:, :, blk(c)], x[:, :, blk(c)], xn[:, :, blk(c)], ALU.add))
            experts(PHASES[2])
            experts(PHASES[3])


def _constants():
    c = np.zeros((P, C_ALL), np.float32)
    p = np.arange(P)
    c[:, C_ID:C_ID + P] = np.eye(P)
    c[:, C_HEADS:C_HEADS + P] = p[:, None] // HEAD == p[None] // HEAD
    same = p[:, None] // CH == p[None] // CH
    c[:, C_CAUSAL:C_CAUSAL + P] = same & (p[:, None] <= p[None])
    c[:, C_START:C_START + SEQ] = np.arange(SEQ) % CH == 0
    c[:, C_EPS], c[:, C_TINY] = LN_EPS, TINY
    at = C_TRI
    for n in (G0, G1, E1):
        g = np.arange(n)
        c[:, at:at + n * n] = (g[None] < g[:, None]).reshape(1, -1)
        at += n * n
    return c


def _selectors(tiles, experts, width):
    e = np.zeros((2 * experts + 1, tiles * P), np.float32)
    feature = np.arange(experts * width)
    e[feature // width, feature] = 1
    e[experts + feature // width, feature] = 1
    e[2 * experts, experts * width:experts * width + SHARED] = 1
    return np.ascontiguousarray(e.reshape(-1, tiles, P).transpose(1, 0, 2))


def _by_partition(a):
    return np.ascontiguousarray(a.reshape(KD, P, -1).transpose(1, 0, 2))


def _feature_tiles(tiles, gates, ups, downs, sg, su, sd):
    def rows(w, s):
        a = np.zeros((tiles * P, D), np.float32)
        n = w.shape[0] * w.shape[1]
        a[:n] = w.reshape(n, D)
        a[n:n + s.shape[0]] = s
        return a.reshape(tiles, P, D)

    out = np.empty((tiles, P, 3 * D), np.float32)
    for k, a in ((0, rows(gates, sg)), (1, rows(ups, su))):
        out[:, :, k * D:(k + 1) * D] = a.reshape(tiles, P, KD, P).transpose(0, 3, 2, 1).reshape(tiles, P, D)
    out[:, :, 2 * D:] = rows(downs.transpose(0, 2, 1), sd.T)
    return out


def kernel(**inputs):
    import concourse.bacc as bacc
    from concourse.bass_utils import run_bass_kernel_spmd

    a = {k: np.asarray(v) for k, v in inputs.items()}
    vecs = np.zeros((P, V_ALL), np.float32)
    for at, name in ((V_BQ, "L0_attn_bq"), (V_BO, "L0_attn_bo"), (V_GW, "L1_attn_g_weight")):
        vecs[:, at:at + KD] = a[name].reshape(KD, P).T
    for at, name in ((V_ROUTE0, "L0_ffn_router_weight"), (V_ROUTE1, "L1_ffn_gate_weight")):
        w = _by_partition(a[name].T)
        vecs[:, at:at + w.shape[1] * w.shape[2]] = w.reshape(P, -1)
    data = {
        "x_t": _by_partition(a["L0_attn_x"].reshape(T, D).T),
        "w_attn": _by_partition(np.concatenate([a[f"L0_attn_w{n}"].T for n in "qkvo"], axis=1)),
        "vecs": vecs,
        "rows": np.concatenate([a["L0_attn_bk"], a["L0_attn_bv"], a["L0_ffn_e_bias"]]),
        "consts": _constants(),
        "w_gla": _by_partition(np.concatenate([a[f"L1_attn_{n}"].T for n in ("Wq", "Wk", "Wog", "Wig")], axis=1)),
        "moe0": _feature_tiles(TILES0, *(a[f"L0_ffn_{n}"] for n in ("Wg", "Wu", "Wd", "sWg", "sWu", "sWd"))),
        "moe1": _feature_tiles(TILES1, *(a[f"L1_ffn_{n}"] for n in ("gate_w", "up_w", "down_w", "sh_gate_w",
                                                                  "sh_up_w", "sh_down_w"))),
        "expand0": _selectors(TILES0, E0, F0),
        "expand1": _selectors(TILES1, E1, F1),
    }
    nc = bacc.Bacc("TRN2", target_bir_lowering=False, num_devices=1,
                   dynamic_dma_scratch_size=1024)
    arrays, args = {}, {}
    for name, v in data.items():
        arrays[f"in_{name}"] = v
        args[name] = nc.dram_tensor(f"in_{name}", v.shape, mybir.dt.from_np(v.dtype), kind="ExternalInput").ap()
    args["out_t"] = nc.dram_tensor("out_t", (P, KD, T), F32, kind="ExternalOutput").ap()
    build(nc, **args)
    got = run_bass_kernel_spmd(nc, [arrays], core_ids=[0]).results[0]["out_t"]
    return np.ascontiguousarray(got.transpose(1, 0, 2).reshape(D, T).T).reshape(BATCH, SEQ, D)
```

```python
from contextlib import ExitStack

import numpy as np

import concourse.bass as bass
from concourse import mybir

F32 = mybir.dt.float32
F32R = mybir.dt.float32r
ALU = mybir.AluOpType
ACT = mybir.ActivationFunctionType
AX_X = mybir.AxisListType.X

P = 128
D = 256
KD = D // P
BATCH, SEQ = 4, 512
T = BATCH * SEQ
BLK = 512
NBLK = T // BLK
NT = T // P
HEAD = 16
LN_EPS = 1e-5

E0, G0, F0 = 32, 8, 176
TOPG0, TOPK0, SCALE0 = 4, 8, 2.5
E1, G1, F1 = 8, 4, 176
TOPG1, TOPK1 = 2, 2
SHARED = 2 * F0
TILES0 = -(-(E0 * F0 + SHARED) // P)
TILES1 = -(-(E1 * F1 + SHARED) // P)
KC0, KC1 = 2 * E0 + 1, 2 * E1 + 1

CH = 32
NCH = SEQ // CH
GLA_SCALE = float(HEAD) ** -0.5

C_ID, C_HEADS, C_CAUSAL, C_START, C_TRI = 0, P, 2 * P, 3 * P, 3 * P + SEQ
C_ALL = C_TRI + G0 * G0 + G1 * G1 + E1 * E1 + 2
C_EPS, C_TINY = C_ALL - 2, C_ALL - 1
C_HSEL = C_ALL
C_ALL += 2 * (D // HEAD)
TINY = 1e-8

V_BQ, V_BO, V_GW, V_ROUTE0 = 0, 2, 4, 6
V_ROUTE1 = V_ROUTE0 + KD * P
V_ALL = V_ROUTE1 + KD * P
KV_RING = 4
KV_LAG = 3
SW = D + D // HEAD
R_BKV, R_EB = 0, 2 * D
R_ALL = R_EB + E0


class Phase:

    def __init__(self, layer, half, first):
        self.layer, self.half, self.first = layer, half, first
        self.tiles = (TILES0, TILES1)[layer]
        self.kc = (KC0, KC1)[layer]
        self.pairs = (self.tiles - 1) // 2
        self.rest = self.tiles - 2 * self.pairs
        self.peel = int(first == 0)
        self.last = first + self.tiles


PHASES = []
for _layer in range(2):
    for _half in range(2):
        PHASES.append(Phase(_layer, _half, PHASES[-1].last if PHASES else 0))
ALL_TILES = PHASES[-1].last


def needed(n):
    return not isinstance(n, int) or n > 0


def build(nc, x_t, x_nat, w_attn, vecs, rows, consts, w_gla, moe0, moe1, expand0, expand1, out_t):
    with ExitStack() as ctx:
        def sb(name, shape, dt=F32):
            return ctx.enter_context(nc.sbuf_tensor(name, shape, dt))

        def sem(name):
            return ctx.enter_context(nc.semaphore(name))

        banks = ctx.enter_context(nc.psum_tensor("banks", [P, 8, BLK], F32))
        bank = [banks[:, i, :] for i in range(8)]

        x = sb("x", [P, KD, T])
        xn = sb("xn", [P, KD, T])
        xn_hi = sb("xn_hi", [P, KD, T], F32R)
        xn_lo = sb("xn_lo", [P, KD, T], F32R)
        square = sb("square", [P, 2, KD, BLK])
        std = sb("std", [P, 2, BLK])
        x_tok = x[:].rearrange("p k (c j d) -> p (k c) j d", c=2, d=D)
        turned = square[:].rearrange("p a k (h d) -> p a (k h) d", d=D)

        def nat(layer, c):
            return x_tok[:, c] if layer == 0 else turned[:, c % 2]

        bn = sb("bn", [P, NT, 6])
        mean_var = sb("mean_var", [P, NT, 2])
        rstd = sb("rstd", [P, NT])

        cst = sb("cst", [P, C_ALL])
        vec = sb("vec", [P, V_ALL])
        row = sb("row", [P, R_ALL])
        mean_w = sb("mean_w", [P, P])
        ones = sb("ones", [P, P])

        a_hi = sb("a_hi", [P, KD, 2, BLK], F32R)
        a_lo = sb("a_lo", [P, KD, 2, BLK], F32R)
        wo_hi = sb("wo_hi", [P, KD, D], F32R)
        wo_lo = sb("wo_lo", [P, KD, D], F32R)

        w_raw = sb("w_raw", [P, 2, 3 * D])
        w_gu_hi = sb("w_gu_hi", [P, 2, 2 * D], F32R)
        w_gu_lo = sb("w_gu_lo", [P, 2, 2 * D], F32R)
        w_dn_hi = sb("w_dn_hi", [P, 2, D], F32R)
        w_dn_lo = sb("w_dn_lo", [P, 2, D], F32R)
        e_raw = sb("e_raw", [P, 2, P])
        e_sel = sb("e_sel", [P, 2, P], F32R)
        zero = sb("zero", [P, P], F32R)
        gate = sb("gate", [P, 2, BLK])
        h_hi = sb("h_hi", [P, 2, BLK], F32R)
        h_lo = sb("h_lo", [P, 2, BLK], F32R)
        q_exp = gate
        state_hi, state_lo = (h[:].rearrange("p a n -> p (a n)")[:, 0:2 * SW].rearrange("p (h n) -> p h n", h=2)
                              for h in (h_hi, h_lo))
        a_nat = std[:].rearrange("p u (r n) -> p u r n", r=2)

        score = sb("score", [P, NT, E0])
        pick = sb("pick", [P, NT, E0])
        rep = sb("rep", [P, NT, E0])
        pair = [std[:, n, :].rearrange("p (j t g a) -> p j t g a", j=2, t=NT, g=G0) for n in range(2)]
        group = sb("group", [P, NT, G0])
        compare = [square[:, n].rearrange("p k n -> p (k n)") for n in range(2)]
        rank = sb("rank", [P, NT, G0])
        top = sb("top", [P, NT, 8])
        tot = sb("tot", [P, NT, 1])
        comb = sb("comb", [P, NT, KC0])
        comb_t = sb("comb_t", [KC0, T], F32R)

        with ExitStack() as own0:
            def sb0(name, shape, dt=F32):
                return own0.enter_context(nc.sbuf_tensor(name, shape, dt))

            w0_raw = sb0("w0_raw", [P, KD, 4 * D])
            w0_hi = sb0("w0_hi", [P, KD, 3 * D], F32R)
            w0_lo = sb0("w0_lo", [P, KD, 3 * D], F32R)
            kv = sb0("kv", [P, KV_RING, 2 * D])
            kv_exp = sb0("kv_exp", [P, 2, D])
            kv_hi = sb0("kv_hi", [P, KV_RING, 2 * D + 2], F32R)
            kv_lo = sb0("kv_lo", [P, KV_RING, 2 * D + 2], F32R)
            qf = sb0("qf", [P, 2, BLK])
            q_hi = sb0("q_hi", [P, 2, BLK], F32R)
            q_lo = sb0("q_lo", [P, 2, BLK], F32R)
            state = sb0("state", [P, 2, SW])
            inv = sb0("inv", [P, 2, 2, D // HEAD])

        w1_raw = sb("w1_raw", [P, KD, 2 * HEAD + 2 * D])
        kq_hi = sb("kq_hi", [P, KD, 2, BATCH, P], F32R)
        kq_lo = sb("kq_lo", [P, KD, 2, BATCH, P], F32R)
        og_hi = sb("og_hi", [P, KD, 2 * D], F32R)
        og_lo = sb("og_lo", [P, KD, 2 * D], F32R)
        rec_q = sb("rec_q", [P, SEQ])
        rec_k = sb("rec_k", [P, SEQ])
        run = sb("run", [P, SEQ])
        q_bd = sb("q_bd", [P, NCH, BATCH, CH])
        k_bd = sb("k_bd", [P, NCH, BATCH, CH])
        e_bd = sb("e_bd", [P, NCH, BATCH, CH])
        x_chunk = sb("x_chunk", [P, 2, KD, BATCH, CH])
        sc = sb("sc", [P, 2, P])
        ke = sb("ke", [P, 2, P])
        v_nat = gate[:, 0, :].rearrange("p (j n) -> p j n", j=2)
        s_st = gate[:, 1, :].rearrange("p (j n) -> p j n", j=2)

        def f(ap):
            return ap.bitcast(F32)

        x_in = [sem(f"x_in{c}") for c in range(NBLK)]
        const_in = sem("const_in")
        small_in = sem("small_in")
        const_made = sem("const_made")
        raw_in = [sem(f"raw_in{b}") for b in range(2)]
        x_t_in = sem("x_t_in")
        token_tp = sem("token_tp")
        var_done = sem("var_done")
        std_done = sem("std_done")
        nat_normed = sem("nat_normed")
        norm_tp = sem("norm_tp")
        normed = sem("normed")
        norm_hi = sem("norm_hi")
        norm_lo = sem("norm_lo")
        small_hi_done = sem("small_hi_done")
        small_lo_done = sem("small_lo_done")
        logits_done = sem("logits_done")
        score_done = sem("score_done")
        comb_done = sem("comb_done")
        comb_tp = sem("comb_tp")
        comb_t_done = sem("comb_t_done")
        kv_mm = sem("kv_mm")
        kv_biased = sem("kv_biased")
        kv_min = sem("kv_min")
        kv_exped = sem("kv_exped")
        kv_full = sem("kv_full")
        kv_hi_done = sem("kv_hi_done")
        kv_lo_done = sem("kv_lo_done")
        q_mm = sem("q_mm")
        q_biased = sem("q_biased")
        q_full = sem("q_full")
        q_hi_done = sem("q_hi_done")
        q_lo_done = sem("q_lo_done")
        state_mm = sem("state_mm")
        state_masked = sem("state_masked")
        state_hi_done = sem("state_hi_done")
        state_lo_done = sem("state_lo_done")
        ratio_mm = sem("ratio_mm")
        attn_nat = sem("attn_nat")
        attn_tp = sem("attn_tp")
        state_clear = sem("state_clear")
        attn_done = sem("attn_done")
        attn_hi_done = sem("attn_hi_done")
        attn_lo_done = sem("attn_lo_done")
        gu_hi_done = sem("gu_hi_done")
        gu_lo_done = sem("gu_lo_done")
        dn_hi_done = sem("dn_hi_done")
        dn_lo_done = sem("dn_lo_done")
        cw_mm = sem("cw_mm")
        gate_mm = sem("gate_mm")
        up_mm = sem("up_mm")
        down_mm = sem("down_mm")
        silu_done = sem("silu_done")
        weighted = sem("weighted")
        hid_done = sem("hid_done")
        h_hi_done = sem("h_hi_done")
        h_lo_done = sem("h_lo_done")
        acc_read = sem("acc_read")
        stored = sem("stored")
        gla_kq_mm = sem("gla_kq_mm")
        gla_act = sem("gla_act")
        gla_ready = sem("gla_ready")
        chunk_in = sem("chunk_in")
        v_tp = sem("v_tp")
        v_done = sem("v_done")
        sc_mm = sem("sc_mm")
        sc_done = sem("sc_done")
        ke_tp = sem("ke_tp")
        ke_done = sem("ke_done")
        upd_mm = sem("upd_mm")
        s_done = sem("s_done")
        o_mm = sem("o_mm")
        o_done = sem("o_done")
        o_hi_done = sem("o_hi_done")
        o_lo_done = sem("o_lo_done")
        osq_done = sem("osq_done")
        ms_mm = sem("ms_mm")
        rms_std = sem("rms_std")
        diag_done = sem("diag_done")
        spread_mm = sem("spread_mm")
        y_added = sem("y_added")
        go_mm = sem("go_mm")
        go_silu = sem("go_silu")
        y_done = sem("y_done")
        chain = sem("chain")
        pool_chain = sem("pool_chain")

        block = ctx.enter_context(nc.Block())

        def blk(c):
            return slice(c * BLK, (c + 1) * BLK)

        @block.sync
        def _(sp):
            def tokens_in(c):
                sp.dma_start(x_tok[:, c], x_nat[blk(c), :].rearrange("(j p) d -> p j d", p=P))\
                    .then_inc(x_in[c], 16)

            tokens_in(0)
            sp.dma_start(cst[:], consts).then_inc(const_in, 16)
            tokens_in(1)
            sp.dma_start(vec[:], vecs).then_inc(const_in, 16)
            sp.dma_start(row[:], rows.partition_broadcast(P)).then_inc(const_in, 16)
            for c in range(2, NBLK):
                tokens_in(c)
            sp.dma_start(w0_raw[:], w_attn).then_inc(small_in, 16)
            sp.wait_ge(norm_tp, NBLK)
            sp.dma_start(x[:], x_t).then_inc(x_t_in, 16)

            def load_tile(ph, n, m):
                src, sel = ((moe0, expand0), (moe1, expand1))[ph.layer]
                sp.dma_start(w_raw[:, n % 2, :], src[m]).then_inc(raw_in[n % 2], 16)
                sp.dma_start(e_raw[0:ph.kc, n % 2, :], sel[m]).then_inc(raw_in[n % 2], 16)

            for ph in PHASES:
                if ph.layer == 1 and ph.half == 0:
                    sp.wait_ge(attn_done, BATCH)
                    sp.dma_start(w1_raw[:], w_gla).then_inc(small_in, 16)
                for m in range(2):
                    n = ph.first + m
                    if n >= 2:
                        sp.wait_ge(dn_lo_done, n - 1)
                        sp.wait_ge(gu_lo_done, n - 1)
                    load_tile(ph, n, m)
                with sp.Fori(0, (ph.tiles - 2) // 2) as i:
                    for j in range(2):
                        n = ph.first + 2 + j
                        sp.wait_ge(dn_lo_done, 2 * i + (n - 1))
                        sp.wait_ge(gu_lo_done, 2 * i + (n - 1))
                        src, sel = ((moe0, expand0), (moe1, expand1))[ph.layer]
                        b = n % 2
                        sp.dma_start(w_raw[:, b, :], src[bass.ds(2 * i + (2 + j), 1), :, :]
                                     .rearrange("a p n -> p (a n)")).then_inc(raw_in[b], 16)
                        sp.dma_start(e_raw[0:ph.kc, b, :], sel[bass.ds(2 * i + (2 + j), 1), :, :]
                                     .rearrange("a p n -> p (a n)")).then_inc(raw_in[b], 16)
                if ph.tiles % 2:
                    n = ph.last - 1
                    sp.wait_ge(dn_lo_done, n - 1)
                    sp.wait_ge(gu_lo_done, n - 1)
                    load_tile(ph, n, ph.tiles - 1)
            for half in range(2):
                for a in range(4):
                    kd, c = a // 2, 2 * half + a % 2
                    sp.wait_ge(acc_read, 8 + 4 * half + a + 1)
                    sp.dma_start(out_t[:, kd, blk(c)], x[:, kd, blk(c)]).then_inc(stored, 16)
            sp.wait_ge(stored, 16 * 8)

        @block.gpsimd
        def _(pool):
            nc.gpsimd.memset(mean_w[:], 1.0 / D)
            nc.gpsimd.memset(ones[:], 1.0)
            nc.gpsimd.memset(state[:], 0.0).then_inc(const_made, 1)
            nc.gpsimd.memset(f(kv_hi[:, :, 2 * D:2 * D + 2]), 1.0).then_inc(const_made, 1)
            nc.gpsimd.memset(f(kv_lo[:, :, 2 * D:2 * D + 2]), 0.0).then_inc(const_made, 1)
            nc.gpsimd.memset(f(zero[:]), 0.0).then_inc(const_made, 1)

            pool.wait_ge(small_in, 16)
            parts = ((w0_hi[:, :, D:3 * D], w0_lo[:, :, D:3 * D], w0_raw[:, :, D:3 * D]),
                     (w0_hi[:, :, 0:D], w0_lo[:, :, 0:D], w0_raw[:, :, 0:D]),
                     (wo_hi[:], wo_lo[:], w0_raw[:, :, 3 * D:4 * D]))
            for n, (hi, lo, raw) in enumerate(parts):
                nc.gpsimd.tensor_copy(hi, raw).then_inc(small_hi_done, 1)
                pool.wait_ge(small_hi_done, n + 1)
                nc.gpsimd.tensor_tensor(lo, raw, f(hi), ALU.subtract).then_inc(small_lo_done, 1)

            def kv_low(t):
                pool.wait_ge(kv_hi_done, t + 1)
                if t >= KV_RING:
                    pool.wait_ge(state_mm, t - KV_RING + 1)
                nc.gpsimd.tensor_tensor(kv_lo[:, t % KV_RING, 0:2 * D], kv[:, t % KV_RING, :],
                                        f(kv_hi[:, t % KV_RING, 0:2 * D]), ALU.subtract).then_inc(kv_lo_done, 1)

            def q_low(b):
                for m in range(2):
                    pool.wait_ge(q_hi_done, 2 * b + m + 1)
                    if b >= 1:
                        pool.wait_ge(ratio_mm, 2 * b)
                    nc.gpsimd.tensor_tensor(q_lo[:, m, :], qf[:, m, :], f(q_hi[:, m, :]),
                                            ALU.subtract).then_inc(q_lo_done, 1)

            for t in range(NT + 2):
                if t < NT:
                    kv_low(t)
                if t % 4 == 1 and t >= 4:
                    q_low(t // 4 - 1)

            pool.wait_ge(attn_done, BATCH)
            for z in (q_bd[:], k_bd[:], e_bd[:], f(kq_hi[:]), f(kq_lo[:])):
                last = nc.gpsimd.memset(z, 0.0)
            last.then_inc(pool_chain, 1)
            pool.wait_ge(small_in, 32)
            nc.gpsimd.tensor_copy(og_hi[:], w1_raw[:, :, 2 * HEAD:]).then_inc(pool_chain, 1)
            pool.wait_ge(pool_chain, 2)
            raw = w1_raw[:, :, 0:2 * HEAD].rearrange("p k (w h) -> p k w h", w=2)
            for b in range(BATCH):
                own = (slice(None), slice(None), slice(None), b, slice(32 * b, 32 * b + HEAD))
                nc.gpsimd.tensor_copy(kq_hi[own], raw).then_inc(pool_chain, 1)
            nc.gpsimd.tensor_tensor(og_lo[:], w1_raw[:, :, 2 * HEAD:], f(og_hi[:]), ALU.subtract)\
                .then_inc(small_lo_done, 1)
            pool.wait_ge(pool_chain, 2 + BATCH)
            for b in range(BATCH):
                own = (slice(None), slice(None), slice(None), b, slice(32 * b, 32 * b + HEAD))
                nc.gpsimd.tensor_tensor(kq_lo[own], raw, f(kq_hi[own]), ALU.subtract).then_inc(small_lo_done, 1)

            pool.wait_ge(normed, 2 * NBLK)
            for i in range(NCH):
                if i >= 2:
                    pool.wait_ge(v_tp, i - 1)
                nc.gpsimd.tensor_copy(x_chunk[:, i % 2],
                                      xn[:].rearrange("p k (b c s) -> p c k b s", b=BATCH, s=CH)[:, i])\
                    .then_inc(chunk_in, 1)

            for c in range(NBLK + 1):
                if c < NBLK:
                    pool.wait_ge(o_hi_done, c + 1)
                    if c >= 2:
                        pool.wait_ge(go_mm, 2 * (c - 1))
                    nc.gpsimd.tensor_tensor(a_lo[:, :, c % 2, :], xn[:, :, blk(c)], f(a_hi[:, :, c % 2, :]),
                                            ALU.subtract).then_inc(o_lo_done, 1)
                if c >= 1:
                    pool.wait_ge(y_done, c)
                    nc.gpsimd.tensor_tensor(x[:, :, blk(c - 1)], x[:, :, blk(c - 1)], xn[:, :, blk(c - 1)],
                                            ALU.add).then_inc(y_added, 1)

        @block.tensor
        def _(pe):
            def three(out, w, wsl, m, msl, start, stop):
                (wh, wl), (mh, ml) = w, m
                pe.matmul(out, wh[wsl], mh[msl], start=start, stop=False, skip_group_check=True)
                pe.matmul(out, wh[wsl], ml[msl], start=False, stop=False, skip_group_check=True)
                return pe.matmul(out, wl[wsl], mh[msl], start=False, stop=stop, skip_group_check=True)

            XN = (xn_hi, xn_lo)
            W0, WO = (w0_hi, w0_lo), (wo_hi, wo_lo)
            KQ, OG = (kq_hi, kq_lo), (og_hi, og_lo)
            everything = slice(None)

            def to_tokens(c):
                if c >= 2:
                    pe.wait_ge(nat_normed, NBLK + c - 1)
                for j in range(4):
                    for k in range(KD):
                        mm = pe.transpose(bank[2 * (c % 2) + j // 2][:, (j % 2) * D + k * P:(j % 2) * D + (k + 1) * P],
                                          x[:, k, (4 * c + j) * P:(4 * c + j + 1) * P], cst[:, C_ID:C_ID + P])
                mm.then_inc(token_tp, 1)

            def to_width(layer, c):
                q = NBLK * layer + c
                pe.wait_ge(nat_normed, q + 1)
                if c >= 2:
                    pe.wait_ge(normed, q - 1)
                for k in range(KD):
                    for j in range(4):
                        mm = pe.transpose(bank[4 + 2 * (c % 2) + k][:, j * P:(j + 1) * P],
                                          nat(layer, c)[:, j, k * P:(k + 1) * P], cst[:, C_ID:C_ID + P])
                mm.then_inc(norm_tp, 1)

            def logits(layer, first, c):
                n_e, v0 = ((E0, V_ROUTE0), (E1, V_ROUTE1))[layer]
                pe.wait_ge(normed, NBLK * layer + c + 1)
                for t in range(4 * c, 4 * c + 4):
                    to = bank[first + t // 8]
                    at = t % 8 * n_e
                    for k in range(KD):
                        mm = pe.matmul(to[:, at:at + P], xn[:, k, t * P:(t + 1) * P],
                                       vec[:, v0 + k * P:v0 + (k + 1) * P], start=k == 0, stop=k == 1)
                mm.then_inc(logits_done, 1)

            def combine_transposes(layer):
                kc = (KC0, KC1)[layer]
                pe.wait_ge(comb_done, layer + 1)
                for c in range(NBLK):
                    if c >= 2:
                        pe.wait_ge(comb_t_done, NBLK * layer + c - 1)
                    for j in range(4):
                        mm = pe.transpose(bank[c % 2][0:kc, j * P:(j + 1) * P],
                                          comb[:, 4 * c + j, 0:kc], cst[:, C_ID:C_ID + P])
                    mm.then_inc(comb_tp, 1)

            pe.wait_ge(const_in, 48)
            for c in range(NBLK):
                to_width(0, c)
                if c >= 1:
                    logits(0, 2, c - 1)
            logits(0, 2, NBLK - 1)
            pe.wait_ge(small_lo_done, 1)

            def kv_product(t):
                pe.wait_ge(norm_lo, t // 4 + 1)
                if t >= 2:
                    pe.wait_ge(kv_biased, t - 1)
                for k in range(KD):
                    mm = three(bank[t % 2][:], XN, (everything, k, slice(t * P, t * P + P)),
                               W0, (everything, k, slice(D, 3 * D)), k == 0, k == 1)
                mm.then_inc(kv_mm, 1)

            def query_product(b):
                for m in range(2):
                    u = 2 * b + m
                    if b >= 1:
                        pe.wait_ge(q_biased, u - 1)
                    if b >= 2:
                        pe.wait_ge(attn_done, b - 1)
                    for k in range(KD):
                        mm = three(bank[2 + m][:], W0, (everything, k, slice(m * P, m * P + P)),
                                   XN, (everything, k, blk(b)), k == 0, k == 1)
                    mm.then_inc(q_mm, 1)

            def state_product(t):
                b, j, r = t // 4, t % 4, t % KV_RING
                pe.wait_ge(kv_lo_done, t + 1)
                if t == 0:
                    pe.wait_ge(normed, NBLK)
                if j == 0 and b >= 1:
                    pe.wait_ge(state_masked, 2 * b)
                for hb in range(2):
                    mm = three(bank[4 + hb][:, 0:D + 2], (kv_hi, kv_lo), (everything, r, slice(hb * P, hb * P + P)),
                               (kv_hi, kv_lo), (everything, r, slice(D, 2 * D + 2)), j == 0, j == 3)
                mm.then_inc(state_mm, 1)

            def ratio_product(u):
                pe.wait_ge(state_lo_done, u // 2 * 2 + 2)
                pe.wait_ge(q_lo_done, u // 2 * 2 + 2)
                if u >= 1:
                    pe.wait_ge(attn_nat, u)
                for r in range(2):
                    toks = slice(((2 * u + r) % 4) * P, ((2 * u + r) % 4 + 1) * P)
                    for hb in range(2):
                        mm = three(bank[6 + r][:, 0:SW], (q_hi, q_lo), (everything, hb, toks),
                                   (state_hi, state_lo), (everything, hb, everything), hb == 0, hb == 1)
                mm.then_inc(ratio_mm, 1)

            def attn_turn(b):
                pe.wait_ge(attn_nat, 2 * b + 2)
                pe.wait_ge(q_biased, min(2 * b + 4, 2 * BATCH))
                for k in range(KD):
                    for j in range(4):
                        mm = pe.transpose(bank[2 + k][:, j * P:(j + 1) * P], a_nat[:, j // 2, j % 2, k * P:(k + 1) * P],
                                          cst[:, C_ID:C_ID + P])
                mm.then_inc(attn_tp, 1)

            pe.wait_ge(const_made, 4)
            for t in range(NT + 6):
                b, j = t // 4, t % 4
                if t < NT:
                    kv_product(t)
                if j == 0 and b >= 2:
                    ratio_product(2 * (b - 2) + 1)
                if KV_LAG <= t < NT + KV_LAG:
                    state_product(t - KV_LAG)
                if j == 0 and 1 <= b <= BATCH:
                    if b == 1:
                        pe.wait_ge(score_done, 1)
                        pe.wait_ge(small_lo_done, 2)
                    query_product(b - 1)
                if j == 1 and b >= 2:
                    attn_turn(b - 2)
                if j == 2 and b == BATCH:
                    pe.wait_ge(kv_biased, NT)
                    combine_transposes(0)
                if j == 3 and b >= 1:
                    ratio_product(2 * (b - 1))

            def unit_front(ph, i, tb, ub):
                par, s, u, tile = tb % 2, ub % 2, 4 * i + ub, 2 * i + tb
                toks = blk(2 * ph.half + s)
                pe.wait_ge(gu_lo_done, tile + 1)
                if needed(u):
                    pe.wait_ge(weighted, u)
                pe.matmul(bank[2][:], e_sel[0:ph.kc, par, :], comb_t[0:ph.kc, toks],
                          start=True, stop=True).then_inc(cw_mm, 1)
                if needed(u):
                    pe.wait_ge(silu_done, u)
                for k in range(KD):
                    mm = three(bank[0][:], (w_gu_hi, w_gu_lo), (everything, par, slice(k * P, k * P + P)),
                               XN, (everything, k, toks), k == 0, k == 1)
                mm.then_inc(gate_mm, 1)
                if needed(u):
                    pe.wait_ge(hid_done, u)
                for k in range(KD):
                    mm = three(bank[1][:], (w_gu_hi, w_gu_lo), (everything, par, slice(D + k * P, D + k * P + P)),
                               XN, (everything, k, toks), k == 0, k == 1)
                mm.then_inc(up_mm, 1)

            def unit_down(ph, i, tb, ub, last=False):
                par, s, u, tile = tb % 2, ub % 2, 4 * i + ub, 2 * i + tb
                pe.wait_ge(dn_lo_done, tile + 1)
                pe.wait_ge(h_lo_done, u + 1)
                for m in range(KD):
                    mm = three(bank[4 + 2 * m + s][:], (w_dn_hi, w_dn_lo), (everything, par, slice(m * P, m * P + P)),
                               (h_hi, h_lo), (everything, s, everything), False, last)
                mm.then_inc(down_mm, 1)

            def experts(ph, begin):
                t0 = ph.first
                unit_front(ph, 0, t0, 2 * t0)
                begin()

                def two_tiles(i):
                    for j in range(4):
                        unit_front(ph, i, t0 + (j + 1) // 2, 2 * t0 + j + 1)
                        unit_down(ph, i, t0 + j // 2, 2 * t0 + j)

                if ph.peel:
                    two_tiles(0)
                with pe.Fori(ph.peel, ph.pairs) as i:
                    two_tiles(i)
                for u in range(2 * (t0 + 2 * ph.pairs), 2 * ph.last):
                    if u + 1 < 2 * ph.last:
                        unit_front(ph, 0, (u + 1) // 2, u + 1)
                    unit_down(ph, 0, u // 2, u, last=u // 2 == ph.last - 1)

            def begin0(half):
                def go():
                    pe.wait_ge(small_lo_done, 3)
                    pe.wait_ge(attn_lo_done, 2 * half + 2)
                    for m in range(KD):
                        for s in range(2):
                            if half == 1:
                                pe.wait_ge(acc_read, 2 * m + s + 1)
                            for k in range(KD):
                                three(bank[4 + 2 * m + s][:], WO, (everything, k, slice(m * P, m * P + P)),
                                      (a_hi, a_lo), (everything, k, s, everything), k == 0, False)
                return go

            def begin1(half):
                def go():
                    for m in range(KD):
                        for s in range(2):
                            if half == 1:
                                pe.wait_ge(acc_read, 8 + 2 * m + s + 1)
                            pe.matmul(bank[4 + 2 * m + s][:], zero[:], xn_hi[:, 0, blk(0)],
                                      start=True, stop=False, skip_group_check=True)
                return go

            pe.wait_ge(comb_t_done, NBLK)
            pe.wait_ge(attn_nat, 2 * BATCH)
            experts(PHASES[0], begin0(0))
            experts(PHASES[1], begin0(1))

            pe.wait_ge(acc_read, 8)
            to_tokens(0)
            to_tokens(1)
            for c in range(NBLK):
                to_width(1, c)
                if c + 2 < NBLK:
                    to_tokens(c + 2)
            pe.wait_ge(norm_lo, 2 * NBLK)
            pe.wait_ge(small_lo_done, 4 + BATCH)
            for w in range(2):
                for b in range(BATCH):
                    for k in range(KD):
                        mm = three(bank[w][:], KQ, (everything, k, w, b, everything),
                                   XN, (everything, k, blk(b)), b == 0 and k == 0, b == 3 and k == 1)
                mm.then_inc(gla_kq_mm, 1)
            for c in range(NBLK):
                logits(1, 6, c)
            pe.wait_ge(gla_ready, 1)

            def chunk_front(i):
                pe.wait_ge(chunk_in, i + 1)
                if i >= 1:
                    pe.wait_ge(v_done, i)
                for k in range(KD):
                    mm = pe.transpose(bank[0][:, k * P:(k + 1) * P],
                                      x_chunk[:, i % 2, k].rearrange("p b s -> p (b s)"),
                                      cst[:, C_ID:C_ID + P])
                mm.then_inc(v_tp, 1)
                if i >= 1:
                    pe.wait_ge(ke_done, i)
                pe.transpose(bank[1][:, 0:P], e_bd[:, i].rearrange("p b s -> p (b s)"),
                             cst[:, C_ID:C_ID + P]).then_inc(ke_tp, 1)
                if i >= 1:
                    pe.wait_ge(sc_done, i)
                pe.matmul(bank[2][:, 0:P], k_bd[:, i].rearrange("p b s -> p (b s)"),
                          q_bd[:, i].rearrange("p b s -> p (b s)"), start=True, stop=True).then_inc(sc_mm, 1)

            def chunk_back(i):
                pe.wait_ge(v_done, i + 1)
                pe.wait_ge(ke_done, i + 1)
                if i >= 1:
                    pe.wait_ge(s_done, i)
                pe.matmul(bank[3][:, 0:D], ke[:, i % 2, :], v_nat[:, i % 2, :], start=True, stop=True)\
                    .then_inc(upd_mm, 1)
                pe.wait_ge(sc_done, i + 1)
                if i >= 2:
                    pe.wait_ge(o_done, i - 1)
                ob = bank[4 + i % 2]
                for m in range(KD):
                    o = ob[:, m * P:(m + 1) * P]
                    pe.matmul(o, v_nat[:, i % 2, m * P:(m + 1) * P], sc[:, i % 2, :], start=True, stop=False,
                              skip_group_check=True)
                    mm = pe.matmul(o, s_st[:, i % 2, m * P:(m + 1) * P],
                                   q_bd[:, i].rearrange("p b s -> p (b s)"), start=False, stop=True,
                                   skip_group_check=True)
                mm.then_inc(o_mm, 1)

            chunk_front(0)
            for i in range(NCH):
                if i + 1 < NCH:
                    chunk_front(i + 1)
                chunk_back(i)
            pe.wait_ge(o_done, NCH)

            def mean_square(c):
                pe.wait_ge(osq_done, c + 1)
                if c >= 1:
                    pe.wait_ge(rms_std, c)
                for j in range(4):
                    for k in range(KD):
                        mm = pe.matmul(bank[6][:, j * P:(j + 1) * P], square[:, c % 2, k, j * P:(j + 1) * P],
                                       mean_w[:], start=k == 0, stop=k == 1)
                mm.then_inc(ms_mm, 1)

            def gate_product(c, m):
                u, to = 2 * c + m, bank[4 + m - 2 * (c % 2)]
                if u >= 4:
                    pe.wait_ge(go_silu, u - 3)
                for k in range(KD):
                    three(to[:], OG, (everything, k, slice(D + m * P, D + m * P + P)),
                          XN, (everything, k, blk(c)), k == 0, False)
                pe.wait_ge(o_lo_done, c + 1)
                for k in range(KD):
                    mm = three(to[:], OG, (everything, k, slice(m * P, m * P + P)),
                               (a_hi, a_lo), (everything, k, c % 2, everything), False, k == 1)
                mm.then_inc(go_mm, 1)

            pe.wait_ge(score_done, 2)
            mean_square(0)
            for c in range(NBLK):
                gate_product(c, 0)
                pe.wait_ge(diag_done, c + 1)
                if c >= 1:
                    pe.wait_ge(y_done, c)
                pe.matmul(bank[7][:], ones[:], std[:, c % 2, :], start=True, stop=True).then_inc(spread_mm, 1)
                gate_product(c, 1)
                if c == 1:
                    combine_transposes(1)
                if c + 1 < NBLK:
                    mean_square(c + 1)
            pe.wait_ge(comb_t_done, 2 * NBLK)
            pe.wait_ge(go_silu, 2 * NBLK)
            pe.wait_ge(y_done, NBLK)
            experts(PHASES[2], begin1(0))
            experts(PHASES[3], begin1(1))

        @block.scalar
        def _(act):
            def norm_std(layer, c):
                q = NBLK * layer + c
                act.wait_ge(var_done, q + 1)
                nc.scalar.activation(rstd[:, 4 * c:4 * c + 4], mean_var[:, 4 * c:4 * c + 4, 1], ACT.Sqrt,
                                     bias=cst[:, C_EPS:C_EPS + 1]).then_inc(std_done, 1)

            def norm_parts(layer, c):
                q = NBLK * layer + c
                act.wait_ge(norm_tp, q + 1)
                nc.scalar.copy(xn[:, :, blk(c)], banks[:, 4 + 2 * (c % 2):6 + 2 * (c % 2), :]).then_inc(normed, 1)
                act.wait_ge(normed, q + 1)
                nc.scalar.copy(xn_hi[:, :, blk(c)], xn[:, :, blk(c)]).then_inc(norm_hi, 1)

            def norm(layer):
                norm_std(layer, 0)
                norm_std(layer, 1)
                for c in range(NBLK):
                    norm_parts(layer, c)
                    if c + 2 < NBLK:
                        norm_std(layer, c + 2)

            act.wait_ge(const_in, 48)
            norm(0)
            act.wait_ge(logits_done, NBLK)
            nc.scalar.activation(score[:].rearrange("p (b t) e -> p b (t e)", b=2),
                                 banks[:, 2:4, 0:8 * E0], ACT.Sigmoid).then_inc(score_done, 1)

            def kv_e(t):
                act.wait_ge(kv_min, t + 1)
                nc.scalar.activation(kv_exp[:, t % 2, :], kv_exp[:, t % 2, :], ACT.Exp).then_inc(kv_exped, 1)

            def kv_h(t):
                act.wait_ge(kv_full, t + 1)
                if t >= KV_RING:
                    act.wait_ge(state_mm, t - KV_RING + 1)
                nc.scalar.copy(kv_hi[:, t % KV_RING, 0:2 * D], kv[:, t % KV_RING, :]).then_inc(kv_hi_done, 1)

            def state_h(u):
                act.wait_ge(state_masked, u + 1)
                if u >= 2:
                    act.wait_ge(ratio_mm, u // 2 * 2)
                nc.scalar.copy(state_hi[:, u % 2, :], state[:, u % 2, :]).then_inc(state_hi_done, 1)

            def attn_evac(b):
                act.wait_ge(attn_tp, b + 1)
                nc.scalar.copy(xn[:, :, blk(b)], banks[:, 2:4, :]).then_inc(attn_done, 1)

            def attn_high(c):
                nc.scalar.copy(a_hi[:, :, c % 2, :], xn[:, :, blk(c)]).then_inc(attn_hi_done, 1)

            def queries_elu(b):
                for m in range(2):
                    act.wait_ge(q_mm, 2 * b + m + 1)
                    if b >= 1:
                        act.wait_ge(q_lo_done, 2 * b + m - 1)
                    bq = vec[:, V_BQ + m:V_BQ + m + 1]
                    nc.scalar.activation(q_exp[:, m, :], bank[2 + m][:], ACT.Exp, bias=bq)
                    nc.scalar.activation(qf[:, m, :], bank[2 + m][:], ACT.Relu, bias=bq).then_inc(q_biased, 1)

            def queries_high(b):
                for m in range(2):
                    act.wait_ge(q_full, 2 * b + m + 1)
                    if b >= 1:
                        act.wait_ge(ratio_mm, 2 * b)
                    nc.scalar.copy(q_hi[:, m, :], qf[:, m, :]).then_inc(q_hi_done, 1)

            def comb_copy(layer):
                kc = (KC0, KC1)[layer]
                for c in range(NBLK):
                    act.wait_ge(comb_tp, NBLK * layer + c + 1)
                    nc.scalar.copy(comb_t[0:kc, blk(c)], bank[c % 2][0:kc, :]).then_inc(comb_t_done, 1)

            for t in range(NT + 6):
                b, j = t // 4, t % 4
                if j == 3 and b >= 1:
                    for hb in range(2):
                        state_h(2 * (b - 1) + hb)
                if t < NT:
                    kv_e(t)
                if 1 <= t <= NT:
                    kv_h(t - 1)
                if j == 0 and 1 <= b <= BATCH:
                    queries_elu(b - 1)
                if j == 1 and 1 <= b <= BATCH:
                    queries_high(b - 1)
                if j == 1 and b >= 2:
                    attn_evac(b - 2)
                if j == 2 and b == BATCH:
                    comb_copy(0)
            act.wait_ge(attn_done, BATCH)
            for c in range(2):
                attn_high(c)


            def split_gu(ph, i, tb):
                par = tb % 2
                act.wait_ge(raw_in[par], 32 * i + 32 * (tb // 2 + 1))
                if needed(4 * i + 2 * tb - 2):
                    act.wait_ge(up_mm, 4 * i + (2 * tb - 2))
                nc.scalar.copy(e_sel[0:ph.kc, par, :], e_raw[0:ph.kc, par, :]).then_inc(gu_hi_done, 1)
                nc.scalar.copy(w_gu_hi[:, par, :], w_raw[:, par, 0:2 * D]).then_inc(gu_hi_done, 1)

            def split_dn(i, tb):
                par = tb % 2
                if needed(4 * i + 2 * tb - 2):
                    act.wait_ge(down_mm, 4 * i + (2 * tb - 2))
                nc.scalar.copy(w_dn_hi[:, par, :], w_raw[:, par, 2 * D:3 * D]).then_inc(dn_hi_done, 1)

            def unit(ph_next, i, tb, ub):
                s = ub % 2
                act.wait_ge(gate_mm, 4 * i + (ub + 1))
                if needed(4 * i + ub - 1):
                    act.wait_ge(h_lo_done, 4 * i + (ub - 1))
                nc.scalar.activation(gate[:, s, :], bank[0][:], ACT.Silu).then_inc(silu_done, 1)
                if ph_next is not None:
                    if s == 0:
                        split_gu(ph_next, i, tb + 1)
                    else:
                        split_dn(i, tb + 1)
                act.wait_ge(hid_done, 4 * i + (ub + 1))
                if needed(4 * i + ub - 1):
                    act.wait_ge(down_mm, 4 * i + (ub - 1))
                nc.scalar.copy(h_hi[:, s, :], gate[:, s, :]).then_inc(h_hi_done, 1)

            def experts(ph):
                t0 = ph.first

                def two_tiles(i):
                    for j in range(4):
                        unit(ph, i, t0 + j // 2, 2 * t0 + j)

                if ph.peel:
                    two_tiles(0)
                with act.Fori(ph.peel, ph.pairs) as i:
                    two_tiles(i)
                for u in range(2 * (t0 + 2 * ph.pairs), 2 * ph.last):
                    tile = u // 2
                    nxt = ph if tile + 1 < ph.last else PHASES[PHASES.index(ph) + 1] if tile + 1 < ALL_TILES else None
                    unit(nxt, 0, tile, u)

            split_gu(PHASES[0], 0, 0)
            split_dn(0, 0)
            experts(PHASES[0])
            act.wait_ge(down_mm, 2 * PHASES[1].first)
            for c in range(2, 4):
                attn_high(c)
            experts(PHASES[1])

            norm(1)
            act.wait_ge(gla_kq_mm, 1)
            nc.scalar.activation(rec_q[:], bank[0][:], ACT.Silu).then_inc(gla_act, 1)
            act.wait_ge(gla_kq_mm, 2)
            nc.scalar.activation(rec_k[:], bank[1][:], ACT.Sigmoid).then_inc(gla_act, 1)
            act.wait_ge(gla_act, 2)
            nc.scalar.activation(std[:, 0, :], rec_k[:], ACT.Sigmoid, scale=-1.0).then_inc(gla_act, 1)
            def chunk_act(i):
                act.wait_ge(v_tp, i + 1)
                if i >= 2:
                    act.wait_ge(o_mm, i - 1)
                nc.scalar.copy(v_nat[:, i % 2, :], bank[0][:, 0:D]).then_inc(v_done, 1)
                act.wait_ge(ke_tp, i + 1)
                if i >= 2:
                    act.wait_ge(upd_mm, i - 1)
                nc.scalar.copy(ke[:, i % 2, :], bank[1][:, 0:P]).then_inc(ke_done, 1)

            def o_out(i):
                act.wait_ge(o_mm, i + 1)
                for m in range(KD):
                    cp = nc.scalar.copy(
                        xn[:, m, :].rearrange("p (b c s) -> p c b s", b=BATCH, s=CH)[:, i],
                        bank[4 + i % 2][:, m * P:(m + 1) * P].rearrange("p (b s) -> p b s", b=BATCH))
                cp.then_inc(o_done, 1)

            for i in range(NCH):
                chunk_act(i)
                if i >= 1:
                    o_out(i - 1)
                if i == 1:
                    act.wait_ge(score_done, 2)
                    nc.scalar.activation(pick[:, :, 0:E1], score[:, :, 0:E1], ACT.Exp).then_inc(gla_act, 1)
            o_out(NCH - 1)
            act.wait_ge(o_done, NCH)
            for c in range(NBLK):
                if c >= 2:
                    act.wait_ge(ms_mm, c - 1)
                nc.scalar.activation(square[:, c % 2], xn[:, :, blk(c)], ACT.Square).then_inc(osq_done, 1)
                if c >= 2:
                    act.wait_ge(go_mm, 2 * (c - 1))
                nc.scalar.copy(a_hi[:, :, c % 2, :], xn[:, :, blk(c)]).then_inc(o_hi_done, 1)
                act.wait_ge(ms_mm, c + 1)
                nc.scalar.activation(rstd[:, 4 * c:4 * c + 4], bank[6].rearrange("p (j n) -> p j n", j=4)[:, :, 0], ACT.Sqrt,
                                     bias=cst[:, C_EPS:C_EPS + 1]).then_inc(rms_std, 1)
                for m in range(KD):
                    act.wait_ge(go_mm, 2 * c + m + 1)
                    if c >= 1 and m == 0:
                        act.wait_ge(y_done, c)
                    nc.scalar.activation(q_exp[:, m, :], bank[4 + m - 2 * (c % 2)][:], ACT.Silu).then_inc(go_silu, 1)
                if c == 1:
                    comb_copy(1)
            act.wait_ge(y_done, NBLK)
            experts(PHASES[2])
            experts(PHASES[3])

        @block.vector
        def _(dve):
            links = [0]

            def link(ins):
                links[0] += 1
                ins.then_inc(chain, 1)
                dve.wait_ge(chain, links[0])

            v = nc.vector

            def over_width(ap):
                return ap.unsqueeze(1).to_broadcast([P, KD, BLK])

            def norm_stats(layer, c):
                q = NBLK * layer + c
                if layer == 0:
                    dve.wait_ge(x_in[c], 16)
                else:
                    dve.wait_ge(token_tp, c + 1)
                for j in range(4):
                    last = v.bn_stats(bn[:, 4 * c + j, :], tokens(layer, c, j))
                link(last)
                for j in range(4):
                    last = v.bn_aggr(mean_var[:, 4 * c + j, :], bn[:, 4 * c + j, :])
                last.then_inc(var_done, 1)

            def tokens(layer, c, j):
                if layer == 0:
                    return nat(0, c)[:, j, :]
                return bank[2 * (c % 2) + j // 2][:, (j % 2) * D:(j % 2 + 1) * D]

            def norm_apply(layer, c):
                q = NBLK * layer + c
                dve.wait_ge(std_done, q + 1)
                link(v.reciprocal(rstd[:, 4 * c:4 * c + 4], rstd[:, 4 * c:4 * c + 4]))
                if layer == 1 and c >= 2:
                    dve.wait_ge(norm_tp, q - 1)
                for j in range(4):
                    last = v.tensor_scalar(nat(layer, c)[:, j, :], tokens(layer, c, j), mean_var[:, 4 * c + j, 0:1],
                                           rstd[:, 4 * c + j:4 * c + j + 1], ALU.subtract, ALU.mult)
                last.then_inc(nat_normed, 1)

            def norm(layer):
                norm_stats(layer, 0)
                norm_stats(layer, 1)
                for c in range(NBLK):
                    norm_apply(layer, c)
                    if c >= 1:
                        norm_low(NBLK * layer + c - 1, c - 1)
                    if c + 2 < NBLK:
                        norm_stats(layer, c + 2)
                norm_low(NBLK * layer + NBLK - 1, NBLK - 1)

            def norm_low(q, c):
                dve.wait_ge(norm_hi, q + 1)
                v.tensor_tensor(xn_lo[:, :, blk(c)], xn[:, :, blk(c)], f(xn_hi[:, :, blk(c)]),
                                ALU.subtract).then_inc(norm_lo, 1)

            def wide(n, values=None):
                a, b = (c[:, 0:NT * n * n].rearrange("p (t a b) -> p t a b", t=NT, a=n) for c in compare)
                if values is None:
                    return a, b
                return a, b, values.unsqueeze(3).to_broadcast([P, NT, n, n]), \
                    values.unsqueeze(2).to_broadcast([P, NT, n, n])

            def rank_compare(values, n, tri):
                a, b, own, other = wide(n, values)
                v.tensor_tensor(a, other, own, ALU.is_gt)
                link(v.tensor_tensor(b, other, own, ALU.is_equal))

            def rank_ties(values, n, tri):
                a, b = wide(n)
                link(v.tensor_tensor(b, b, tri.rearrange("p (a b) -> p a b", b=n).unsqueeze(1)
                                     .to_broadcast([P, NT, n, n]), ALU.mult))
                link(v.tensor_tensor(a, a, b, ALU.add))

            def rank_count(n, limit, out):
                link(v.tensor_reduce(rank[:, :, 0:n], wide(n)[0], AX_X, ALU.add))
                link(v.tensor_scalar(out, rank[:, :, 0:n], float(limit), None, ALU.is_lt))

            def rank_below(values, n, tri, limit, out):
                rank_compare(values, n, tri)
                rank_ties(values, n, tri)
                rank_count(n, limit, out)

            def combine_parts(w, n_e):
                link(v.tensor_copy(comb[:, :, 0:n_e].bitcast(F32R), w))
                v.tensor_tensor(comb[:, :, n_e:2 * n_e], w, comb[:, :, 0:n_e], ALU.subtract)
                v.memset(comb[:, :, 2 * n_e:2 * n_e + 1], 1.0).then_inc(comb_done, 1)

            def route_groups():
                dve.wait_ge(score_done, 1)
                eb = row[:, R_EB:R_EB + E0].unsqueeze(1).to_broadcast([P, NT, E0])
                link(v.tensor_tensor(pick[:], score[:], eb, ALU.add))
                four = pick[:].rearrange("p t (g a b) -> p t g a b", g=G0, a=2)
                hi, lo = pair[0][:, 0], pair[0][:, 1]
                v.tensor_tensor(hi, four[:, :, :, :, 0], four[:, :, :, :, 1], ALU.max)
                link(v.tensor_tensor(lo, four[:, :, :, :, 0], four[:, :, :, :, 1], ALU.min))
                one, two, three_ = pair[1][:, 0, :, :, 0], pair[1][:, 0, :, :, 1], pair[1][:, 1, :, :, 0]
                v.tensor_tensor(one, hi[:, :, :, 0], hi[:, :, :, 1], ALU.max)
                v.tensor_tensor(two, hi[:, :, :, 0], hi[:, :, :, 1], ALU.min)
                link(v.tensor_tensor(three_, lo[:, :, :, 0], lo[:, :, :, 1], ALU.max))
                link(v.tensor_tensor(two, two, three_, ALU.max))
                link(v.tensor_tensor(group[:], one, two, ALU.add))

            def route_mask():
                link(v.tensor_tensor(pick[:].rearrange("p t (g e) -> p t g e", g=G0),
                                     pick[:].rearrange("p t (g e) -> p t g e", g=G0),
                                     group[:].unsqueeze(3).to_broadcast([P, NT, G0, E0 // G0]), ALU.mult))
                for t in range(NT):
                    m = v.max(top[:, t, :], pick[:, t, :])
                link(m)

            def route_pick():
                for t in range(NT):
                    m = v.match_replace(rep[:, t, :], top[:, t, :], pick[:, t, :], -3e38)
                link(m)

            def route_choose():
                link(v.tensor_tensor(rep[:], rep[:], pick[:], ALU.not_equal))
                link(v.tensor_tensor(rep[:], rep[:], score[:], ALU.mult))
                link(v.tensor_reduce(tot[:, :, 0], rep[:], AX_X, ALU.add))

            def route_scale():
                link(v.tensor_scalar(tot[:], tot[:], 1e-20, None, ALU.add))
                link(v.reciprocal(tot[:], tot[:]))
                link(v.tensor_tensor(rep[:], rep[:], tot[:].to_broadcast([P, NT, E0]), ALU.mult))
                link(v.tensor_scalar(rep[:], rep[:], SCALE0, None, ALU.mult))

            group_order = (group[:], G0, cst[:, C_TRI:C_TRI + G0 * G0])
            route0 = {
                0: route_groups,
                1: lambda: rank_compare(*group_order),
                2: lambda: rank_ties(*group_order),
                3: lambda: rank_count(G0, TOPG0, group[:]),
                5: route_mask,
                6: route_pick,
                7: route_choose,
                9: route_scale,
                10: lambda: combine_parts(rep[:], E0),
            }

            norm(0)
            dve.wait_ge(const_in, 48)

            kv_bias = row[:, R_BKV:R_BKV + 2 * D]

            def kv_bias_min(t):
                dve.wait_ge(kv_mm, t + 1)
                if t >= KV_RING:
                    dve.wait_ge(kv_lo_done, t - KV_RING + 1)
                v.tensor_tensor(kv[:, t % KV_RING, :], bank[t % 2][:], kv_bias, ALU.add).then_inc(kv_biased, 1)
                dve.wait_ge(kv_biased, t + 1)
                v.tensor_scalar(kv_exp[:, t % 2, :], kv[:, t % KV_RING, 0:D], 0.0, None, ALU.min).then_inc(kv_min, 1)

            def kv_elu(t):
                dve.wait_ge(kv_exped, t + 1)
                v.scalar_tensor_tensor(out=kv[:, t % KV_RING, 0:D], in0=kv[:, t % KV_RING, 0:D], scalar=0.0,
                                       in1=kv_exp[:, t % 2, :], op0=ALU.max, op1=ALU.add).then_inc(kv_full, 1)

            def mask_state(u):
                b, hb = u // 2, u % 2
                heads = cst[:, C_HEADS:C_HEADS + P]
                dve.wait_ge(state_mm, 4 * b + 4)
                if u >= 2:
                    dve.wait_ge(state_lo_done, u - 1)
                v.tensor_tensor(state[:, hb, hb * P:hb * P + P], bank[4 + hb][:, hb * P:hb * P + P], heads, ALU.mult)
                own = C_HSEL + hb * (D // HEAD)
                v.tensor_scalar(state[:, hb, D:SW], cst[:, own:own + D // HEAD], bank[4 + hb][:, D:D + 1], None,
                                ALU.mult).then_inc(state_masked, 1)

            def state_low(u):
                dve.wait_ge(state_hi_done, u + 1)
                if u >= 2:
                    dve.wait_ge(ratio_mm, u // 2 * 2)
                v.tensor_tensor(state_lo[:, u % 2, :], state[:, u % 2, :], f(state_hi[:, u % 2, :]),
                                ALU.subtract).then_inc(state_lo_done, 1)

            def ratio(u):
                nh = D // HEAD
                dve.wait_ge(ratio_mm, u + 1)
                link(v.tensor_scalar(inv[:, u % 2], banks[:, 6:8, D:SW], TINY, None, ALU.add))
                link(v.reciprocal(inv[:, u % 2], inv[:, u % 2]))
                if u >= 2:
                    dve.wait_ge(attn_tp, u // 2)
                for r in range(2):
                    last = v.tensor_tensor(a_nat[:, u % 2, r].rearrange("p (h e) -> p h e", h=nh),
                                           bank[6 + r][:, 0:D].rearrange("p (h e) -> p h e", h=nh),
                                           inv[:, u % 2, r].unsqueeze(2).to_broadcast([P, nh, HEAD]), ALU.mult)
                last.then_inc(attn_nat, 1)

            def attn_low(c):
                dve.wait_ge(attn_hi_done, c + 1)
                v.tensor_tensor(a_lo[:, :, c % 2, :], xn[:, :, blk(c)], f(a_hi[:, :, c % 2, :]),
                                ALU.subtract).then_inc(attn_lo_done, 1)

            def queries_elu(b):
                for m in range(2):
                    dve.wait_ge(q_biased, 2 * b + m + 1)
                    v.scalar_tensor_tensor(out=qf[:, m, :], in0=q_exp[:, m, :], scalar=1.0,
                                           in1=qf[:, m, :], op0=ALU.min, op1=ALU.add).then_inc(q_full, 1)

            for t in range(NT + 6):
                b, j = t // 4, t % 4
                if j == 3 and b >= 1:
                    for hb in range(2):
                        state_low(2 * (b - 1) + hb)
                if j == 0 and b >= 2:
                    ratio(2 * (b - 2))
                if t < NT:
                    kv_bias_min(t)
                if 1 <= t <= NT:
                    kv_elu(t - 1)
                if j == 0 and b >= 2:
                    ratio(2 * (b - 2) + 1)
                if j == 1 and 1 <= b <= BATCH:
                    queries_elu(b - 1)
                if j == 2 and b >= 1:
                    for hb in range(2):
                        mask_state(2 * (b - 1) + hb)
                if t in route0:
                    route0[t]()
            for c in range(2):
                attn_low(c)

            def split_gu(i, tb):
                par = tb % 2
                dve.wait_ge(gu_hi_done, 4 * i + (2 * tb + 2))
                if needed(4 * i + 2 * tb - 2):
                    dve.wait_ge(up_mm, 4 * i + (2 * tb - 2))
                v.tensor_tensor(w_gu_lo[:, par, :], w_raw[:, par, 0:2 * D], f(w_gu_hi[:, par, :]),
                                ALU.subtract).then_inc(gu_lo_done, 1)

            def split_dn(i, tb):
                par = tb % 2
                dve.wait_ge(dn_hi_done, 2 * i + (tb + 1))
                if needed(4 * i + 2 * tb - 2):
                    dve.wait_ge(down_mm, 4 * i + (2 * tb - 2))
                v.tensor_tensor(w_dn_lo[:, par, :], w_raw[:, par, 2 * D:3 * D], f(w_dn_hi[:, par, :]),
                                ALU.subtract).then_inc(dn_lo_done, 1)

            def unit(split, i, tb, ub):
                s = ub % 2
                dve.wait_ge(silu_done, 4 * i + (ub + 1))
                dve.wait_ge(cw_mm, 4 * i + (ub + 1))
                v.tensor_tensor(gate[:, s, :], gate[:, s, :], bank[2][:], ALU.mult).then_inc(weighted, 1)
                dve.wait_ge(up_mm, 4 * i + (ub + 1))
                dve.wait_ge(weighted, 4 * i + (ub + 1))
                v.tensor_tensor(gate[:, s, :], gate[:, s, :], bank[1][:], ALU.mult).then_inc(hid_done, 1)
                if split:
                    if s == 0:
                        split_gu(i, tb + 1)
                    else:
                        split_dn(i, tb + 1)
                dve.wait_ge(h_hi_done, 4 * i + (ub + 1))
                if needed(4 * i + ub - 1):
                    dve.wait_ge(down_mm, 4 * i + (ub - 1))
                v.tensor_tensor(h_lo[:, s, :], gate[:, s, :], f(h_hi[:, s, :]), ALU.subtract).then_inc(h_lo_done, 1)

            def experts(ph):
                t0 = ph.first

                def two_tiles(i):
                    for j in range(4):
                        unit(True, i, t0 + j // 2, 2 * t0 + j)

                if ph.peel:
                    two_tiles(0)
                with dve.Fori(ph.peel, ph.pairs) as i:
                    two_tiles(i)
                for u in range(2 * (t0 + 2 * ph.pairs), 2 * ph.last):
                    unit(u // 2 + 1 < ALL_TILES, 0, u // 2, u)
                dve.wait_ge(down_mm, 2 * ph.last)
                dve.wait_ge(down_mm, 2 * ph.last)
                if ph.half == 0:
                    if ph.layer == 0:
                        dve.wait_ge(x_t_in, 16)
                    else:
                        dve.wait_ge(y_added, NBLK)
                for a in range(4):
                    kd, c = a // 2, 2 * ph.half + a % 2
                    if ph.layer == 0:
                        v.scalar_tensor_tensor(out=x[:, kd, blk(c)], in0=bank[4 + a][:],
                                               scalar=vec[:, V_BO + kd:V_BO + kd + 1], in1=x[:, kd, blk(c)],
                                               op0=ALU.add, op1=ALU.add).then_inc(acc_read, 1)
                    else:
                        v.tensor_tensor(x[:, kd, blk(c)], bank[4 + a][:], x[:, kd, blk(c)],
                                        ALU.add).then_inc(acc_read, 1)

            split_gu(0, 0)
            split_dn(0, 0)
            experts(PHASES[0])
            for c in range(2, 4):
                attn_low(c)
            experts(PHASES[1])

            norm(1)

            dve.wait_ge(gla_act, 3)
            decay, first = std[:, 0, :], std[:, 1, :]
            starts = cst[:, C_START:C_START + SEQ]
            link(v.tensor_tensor(first, decay, starts, ALU.mult))
            link(v.tensor_tensor(decay, decay, first, ALU.subtract))
            link(v.tensor_tensor_scan(run[:], decay, first, 0.0, ALU.mult, ALU.add))
            link(v.reciprocal(first, run[:]))
            link(v.scalar_tensor_tensor(out=rec_q[:], in0=rec_q[:], scalar=GLA_SCALE, in1=run[:],
                                        op0=ALU.mult, op1=ALU.mult))
            link(v.tensor_tensor(rec_k[:], rec_k[:], first, ALU.mult))
            ends = run[:].rearrange("p (c s) -> p c s", s=CH)[:, :, CH - 1:CH]
            link(v.tensor_tensor(decay.rearrange("p (c s) -> p c s", s=CH),
                                 rec_k[:].rearrange("p (c s) -> p c s", s=CH),
                                 ends.to_broadcast([P, NCH, CH]), ALU.mult))
            dve.wait_ge(pool_chain, 1)
            link(v.memset(s_st[:, 0, :], 0.0))
            for b in range(BATCH):
                r = slice(32 * b, 32 * b + 32)
                for dst, src in ((q_bd, rec_q[:]), (k_bd, rec_k[:]), (e_bd, decay)):
                    cp = v.tensor_copy(dst[r, :, b, :], src[r, :].rearrange("p (c s) -> p c s", s=CH))
            cp.then_inc(gla_ready, 1)

            ex = pick[:, :, 0:E1]
            two = ex.rearrange("p t (g e) -> p t g e", g=G1)
            gr, masked, sel = group[:, :, 0:G1], rep[:, :, 0:E1], rep[:, :, E1:2 * E1]
            t1 = C_TRI + G0 * G0
            group_order1 = (gr, G1, cst[:, t1:t1 + G1 * G1])
            expert_order1 = (masked, E1, cst[:, t1 + G1 * G1:t1 + G1 * G1 + E1 * E1])

            def softmax_less_max():
                dve.wait_ge(logits_done, 2 * NBLK)
                w8 = score[:, :, 0:E1]
                for h in range(2):
                    last = v.tensor_copy(w8[:, 8 * h:8 * h + 8],
                                         bank[6 + h][:, 0:8 * E1].rearrange("p (t e) -> p t e", e=E1))
                link(last)
                link(v.tensor_reduce(tot[:, :, 0], w8, AX_X, ALU.max))
                v.tensor_tensor(w8, w8, tot[:].to_broadcast([P, NT, E1]), ALU.subtract).then_inc(score_done, 1)

            def softmax_divide():
                dve.wait_ge(gla_act, 4)
                link(v.tensor_reduce(tot[:, :, 0], ex, AX_X, ALU.add))
                link(v.reciprocal(tot[:], tot[:]))
                link(v.tensor_tensor(ex, ex, tot[:].to_broadcast([P, NT, E1]), ALU.mult))
                link(v.tensor_tensor(gr, two[:, :, :, 0], two[:, :, :, 1], ALU.max))

            def mask_groups():
                link(v.tensor_tensor(masked.rearrange("p t (g e) -> p t g e", g=G1), two,
                                     gr.unsqueeze(3).to_broadcast([P, NT, G1, E1 // G1]), ALU.mult))

            def mask_experts():
                rank_count(E1, TOPK1, sel)
                link(v.tensor_tensor(masked, masked, sel, ALU.mult))

            route1 = {
                0: softmax_less_max,
                2: softmax_divide,
                3: lambda: rank_compare(*group_order1),
                4: lambda: rank_ties(*group_order1),
                5: lambda: rank_count(G1, TOPG1, gr),
                6: mask_groups,
                7: lambda: rank_compare(*expert_order1),
                8: lambda: rank_ties(*expert_order1),
                9: mask_experts,
                10: lambda: combine_parts(masked, E1),
            }

            def chunk_scores(i):
                dve.wait_ge(sc_mm, i + 1)
                if i >= 2:
                    dve.wait_ge(o_mm, i - 1)
                v.tensor_tensor(sc[:, i % 2, :], bank[2][:, 0:P], cst[:, C_CAUSAL:C_CAUSAL + P],
                                ALU.mult).then_inc(sc_done, 1)

            def chunk_state(i):
                dve.wait_ge(upd_mm, i + 1)
                if i >= 1:
                    dve.wait_ge(o_mm, i)
                    dve.wait_ge(s_done, i)
                v.scalar_tensor_tensor(out=s_st[:, (i + 1) % 2, :], in0=s_st[:, i % 2, :],
                                       scalar=run[:, (i + 1) * CH - 1:(i + 1) * CH], in1=bank[3][:, 0:D],
                                       op0=ALU.mult, op1=ALU.add).then_inc(s_done, 1)

            chunk_scores(0)
            for i in range(NCH):
                if i + 1 < NCH:
                    chunk_scores(i + 1)
                chunk_state(i)
                if i in route1:
                    route1[i]()
            for c in range(NBLK):
                dve.wait_ge(rms_std, c + 1)
                r = rstd[:, 4 * c:4 * c + 4]
                link(v.reciprocal(r, r))
                if c >= 2:
                    dve.wait_ge(spread_mm, c - 1)
                for j in range(4):
                    last = v.tensor_scalar(std[:, c % 2, j * P:(j + 1) * P], cst[:, C_ID:C_ID + P],
                                           rstd[:, 4 * c + j:4 * c + j + 1], None, ALU.mult)
                last.then_inc(diag_done, 1)
                dve.wait_ge(spread_mm, c + 1)
                dve.wait_ge(o_lo_done, c + 1)
                link(v.tensor_tensor(xn[:, :, blk(c)], xn[:, :, blk(c)], over_width(bank[7][:]), ALU.mult))
                dve.wait_ge(go_silu, 2 * c + 2)
                for m in range(KD):
                    last = v.scalar_tensor_tensor(out=xn[:, m, blk(c)], in0=xn[:, m, blk(c)],
                                                  scalar=vec[:, V_GW + m:V_GW + m + 1], in1=q_exp[:, m, :],
                                                  op0=ALU.mult, op1=ALU.mult)
                last.then_inc(y_done, 1)
            experts(PHASES[2])
            experts(PHASES[3])


def _constants():
    c = np.zeros((P, C_ALL), np.float32)
    p = np.arange(P)
    c[:, C_ID:C_ID + P] = np.eye(P)
    c[:, C_HEADS:C_HEADS + P] = p[:, None] // HEAD == p[None] // HEAD
    same = p[:, None] // CH == p[None] // CH
    c[:, C_CAUSAL:C_CAUSAL + P] = same & (p[:, None] <= p[None])
    c[:, C_START:C_START + SEQ] = np.arange(SEQ) % CH == 0
    for hb in range(2):
        heads = np.arange(D // HEAD)
        c[:, C_HSEL + hb * len(heads):C_HSEL + (hb + 1) * len(heads)] = heads[None] == (hb * P + p[:, None]) // HEAD
    c[:, C_EPS], c[:, C_TINY] = LN_EPS, TINY
    at = C_TRI
    for n in (G0, G1, E1):
        g = np.arange(n)
        c[:, at:at + n * n] = (g[None] < g[:, None]).reshape(1, -1)
        at += n * n
    return c


def _selectors(tiles, experts, width):
    e = np.zeros((2 * experts + 1, tiles * P), np.float32)
    feature = np.arange(experts * width)
    e[feature // width, feature] = 1
    e[experts + feature // width, feature] = 1
    e[2 * experts, experts * width:experts * width + SHARED] = 1
    return np.ascontiguousarray(e.reshape(-1, tiles, P).transpose(1, 0, 2))


def _by_partition(a):
    return np.ascontiguousarray(a.reshape(KD, P, -1).transpose(1, 0, 2))


def _feature_tiles(tiles, gates, ups, downs, sg, su, sd):
    def rows(w, s):
        a = np.zeros((tiles * P, D), np.float32)
        n = w.shape[0] * w.shape[1]
        a[:n] = w.reshape(n, D)
        a[n:n + s.shape[0]] = s
        return a.reshape(tiles, P, D)

    out = np.empty((tiles, P, 3 * D), np.float32)
    for k, a in ((0, rows(gates, sg)), (1, rows(ups, su))):
        out[:, :, k * D:(k + 1) * D] = a.reshape(tiles, P, KD, P).transpose(0, 3, 2, 1).reshape(tiles, P, D)
    out[:, :, 2 * D:] = rows(downs.transpose(0, 2, 1), sd.T)
    return out


def kernel(**inputs):
    import concourse.bacc as bacc
    from concourse.bass_utils import run_bass_kernel_spmd

    a = {k: np.asarray(v) for k, v in inputs.items()}
    vecs = np.zeros((P, V_ALL), np.float32)
    for at, name in ((V_BQ, "L0_attn_bq"), (V_BO, "L0_attn_bo"), (V_GW, "L1_attn_g_weight")):
        vecs[:, at:at + KD] = a[name].reshape(KD, P).T
    for at, name in ((V_ROUTE0, "L0_ffn_router_weight"), (V_ROUTE1, "L1_ffn_gate_weight")):
        w = _by_partition(a[name].T)
        for k in range(KD):
            vecs[:, at + k * P:at + k * P + w.shape[2]] = w[:, k]
    data = {
        "x_nat": a["L0_attn_x"].reshape(T, D),
        "x_t": _by_partition(a["L0_attn_x"].reshape(T, D).T),
        "w_attn": _by_partition(np.concatenate([a[f"L0_attn_w{n}"].T for n in "qkvo"], axis=1)),
        "vecs": vecs,
        "rows": np.concatenate([a["L0_attn_bk"], a["L0_attn_bv"], a["L0_ffn_e_bias"]]),
        "consts": _constants(),
        "w_gla": _by_partition(np.concatenate([a[f"L1_attn_{n}"].T for n in ("Wq", "Wk", "Wog", "Wig")], axis=1)),
        "moe0": _feature_tiles(TILES0, *(a[f"L0_ffn_{n}"] for n in ("Wg", "Wu", "Wd", "sWg", "sWu", "sWd"))),
        "moe1": _feature_tiles(TILES1, *(a[f"L1_ffn_{n}"] for n in ("gate_w", "up_w", "down_w", "sh_gate_w",
                                                                  "sh_up_w", "sh_down_w"))),
        "expand0": _selectors(TILES0, E0, F0),
        "expand1": _selectors(TILES1, E1, F1),
    }
    nc = bacc.Bacc("TRN2", target_bir_lowering=False, num_devices=1,
                   dynamic_dma_scratch_size=1024)
    arrays, args = {}, {}
    for name, v in data.items():
        arrays[f"in_{name}"] = v
        args[name] = nc.dram_tensor(f"in_{name}", v.shape, mybir.dt.from_np(v.dtype), kind="ExternalInput").ap()
    args["out_t"] = nc.dram_tensor("out_t", (P, KD, T), F32, kind="ExternalOutput").ap()
    build(nc, **args)
    got = run_bass_kernel_spmd(nc, [arrays], core_ids=[0]).results[0]["out_t"]
    return np.ascontiguousarray(got.transpose(1, 0, 2).reshape(D, T).T).reshape(BATCH, SEQ, D)
```

```python
from contextlib import ExitStack

import numpy as np

import concourse.bass as bass
from concourse import mybir

F32 = mybir.dt.float32
F32R = mybir.dt.float32r
ALU = mybir.AluOpType
ACT = mybir.ActivationFunctionType
AX_X = mybir.AxisListType.X


P = 128
D = 256
KD = D // P
BATCH, SEQ = 4, 512
T = BATCH * SEQ
BLK = 512
NBLK = T // BLK
NT = T // P
HEAD = 16
LN_EPS = 1e-5

E0, G0, F0 = 32, 8, 176
TOPG0, TOPK0, SCALE0 = 4, 8, 2.5
E1, G1, F1 = 8, 4, 176
TOPG1, TOPK1 = 2, 2
SHARED = 2 * F0
TILES0 = -(-(E0 * F0 + SHARED) // P)
TILES1 = -(-(E1 * F1 + SHARED) // P)
KC0, KC1 = 2 * E0 + 1, 2 * E1 + 1

CH = 32
NCH = SEQ // CH
GLA_SCALE = float(HEAD) ** -0.5

C_ID, C_HEADS, C_CAUSAL, C_START, C_TRI = 0, P, 2 * P, 3 * P, 3 * P + SEQ
C_EPS = C_TRI + G1 * G1
C_HSEL = C_EPS + 1
C_ALL = C_HSEL + 2 * (D // HEAD)
SW = D + D // HEAD
TINY = 1e-8

V_BQ, V_BO, V_GW, V_ROUTE0 = 0, 2, 4, 6
V_ROUTE1 = V_ROUTE0 + KD * P
V_ALL = V_ROUTE1 + KD * P
R_BKV, R_EB = 0, 2 * D
R_ALL = R_EB + E0

FRAME = 8
KV_AT, QUERY_AT, EXP_AT, STATE_AT = 0, 2, 3, 6
RATIO_AT, TURN_AT, OUT_PARTS_AT = 3, 5, 7
ROUTE0_AT = (7, 15, 23, 31, 32, 33, 34)
COMB0_AT = BATCH * FRAME + FRAME - 1

WIDTH0_AT, LOGITS0_AT = RATIO_AT, TURN_AT
NORMS0 = 2 + 4

QUARTERS = 4
TOKENS_AT = 1
STD_AT = TOKENS_AT + QUARTERS
WIDTH_AT = STD_AT + 1
LOGITS_AT = WIDTH_AT + QUARTERS
ROUTE_AT = LOGITS_AT + 1
COMB_AT = ROUTE_AT + 7
HALF_DONE = COMB_AT + 2
KQ_AT = ROUTE_AT
DECAY_AT = ROUTE_AT + 4
CHUNKS_AT = DECAY_AT + 7
MEAN_AT = CHUNKS_AT + NCH
OUT_AT = MEAN_AT + NBLK


class Phase:

    def __init__(self, layer, half, first):
        self.layer, self.half, self.first = layer, half, first
        self.tiles = (TILES0, TILES1)[layer]
        self.kc = (KC0, KC1)[layer]
        self.pairs = (self.tiles - 1) // 2
        self.peel = {0: COMB0_AT // 4 + 1, 1: HALF_DONE // 4 + 1}.get(2 * layer + half, self.pairs)
        self.last = first + self.tiles


PHASES = []
for _layer in range(2):
    for _half in range(2):
        PHASES.append(Phase(_layer, _half, PHASES[-1].last if PHASES else 0))
ALL_TILES = PHASES[-1].last


FIRST_ASIDE = (2 * PHASES[1].first, 2 * PHASES[2].first)


def aside(ph, u):
    half = int(ph.layer == 1)
    return half, u - FIRST_ASIDE[half]


def needed(n):
    return not isinstance(n, int) or n > 0


def build(nc, x_t, x_nat, w_attn, vecs, rows, consts, w_gla, moe0, moe1, expand0, expand1, out_t):
    with ExitStack() as ctx:
        def sb(name, shape, dt=F32):
            return ctx.enter_context(nc.sbuf_tensor(name, shape, dt))

        def sem(name):
            return ctx.enter_context(nc.semaphore(name))

        def f(ap):
            return ap.bitcast(F32)

        banks = ctx.enter_context(nc.psum_tensor("banks", [P, 8, BLK], F32))
        bank = [banks[:, i, :] for i in range(8)]

        x = sb("x", [P, KD, T])
        xn = sb("xn", [P, KD, T])
        xn_hi = sb("xn_hi", [P, KD, T], F32R)
        xn_lo = sb("xn_lo", [P, KD, T], F32R)
        square = sb("square", [P, 2, KD, BLK])
        std = sb("std", [P, 2, BLK])
        x_tok = x[:].rearrange("p k (c j d) -> p (k c) j d", c=2, d=D)
        turned = square[:].rearrange("p a k n -> p (a k n)").rearrange("p (q j d) -> p q j d", j=2, d=D)

        bn = sb("bn", [P, NT, 6])
        mean_var = sb("mean_var", [P, NT, 2])
        rstd = sb("rstd", [P, NT])

        cst = sb("cst", [P, C_ALL])
        vec = sb("vec", [P, V_ALL])
        row = sb("row", [P, R_ALL])
        mean_w = sb("mean_w", [P, P])
        ones = sb("ones", [P, P])

        a_hi = sb("a_hi", [P, KD, 2, BLK], F32R)
        a_lo = sb("a_lo", [P, KD, 2, BLK], F32R)
        wo_hi = sb("wo_hi", [P, KD, D], F32R)
        wo_lo = sb("wo_lo", [P, KD, D], F32R)

        w_raw = sb("w_raw", [P, 2, 3 * D])
        w_gu_hi = sb("w_gu_hi", [P, 2, 2 * D], F32R)
        w_gu_lo = sb("w_gu_lo", [P, 2, 2 * D], F32R)
        w_dn_hi = sb("w_dn_hi", [P, 2, D], F32R)
        w_dn_lo = sb("w_dn_lo", [P, 2, D], F32R)
        e_raw = sb("e_raw", [P, 2, P])
        e_sel = sb("e_sel", [P, 2, P], F32R)
        gate = sb("gate", [P, 2, BLK])
        h_hi = sb("h_hi", [P, 2, BLK], F32R)
        h_lo = sb("h_lo", [P, 2, BLK], F32R)
        a_nat = std[:].rearrange("p u (r n) -> p (u r) n", n=D)

        score = sb("score", [P, NT, E0])
        pick = sb("pick", [P, NT, E0])
        rep = sb("rep", [P, NT, E0])
        group = sb("group", [P, NT, G0])
        compare = [square[:, n].rearrange("p k n -> p (k n)") for n in range(2)]
        pair = [c[:, 0:2 * NT * G0].rearrange("p (j t g a) -> p j t g a", j=2, t=NT // 2, g=G0) for c in compare]
        rank = sb("rank", [P, NT, G0])
        top = sb("top", [P, NT, 8])
        tot = sb("tot", [P, NT, 1])
        comb = sb("comb", [P, NT, KC0])
        comb_t = sb("comb_t", [KC0, T], F32R)

        with ExitStack() as own0:
            def sb0(name, shape, dt=F32):
                return own0.enter_context(nc.sbuf_tensor(name, shape, dt))

            w0_raw = sb0("w0_raw", [P, KD, 4 * D])
            w0_hi = sb0("w0_hi", [P, KD, 3 * D], F32R)
            w0_lo = sb0("w0_lo", [P, KD, 3 * D], F32R)
            kv = sb0("kv", [P, 4, 2 * D])
            kv_hi = sb0("kv_hi", [P, 4, 2 * D + 2], F32R)
            kv_lo = sb0("kv_lo", [P, 4, 2 * D + 2], F32R)
            qf = sb0("qf", [P, 2, BLK])
            q_hi = sb0("q_hi", [P, 2, BLK], F32R)
            q_lo = sb0("q_lo", [P, 2, BLK], F32R)
            state = sb0("state", [P, 2, SW])
            state_hi = sb0("state_hi", [P, 2, SW], F32R)
            state_lo = sb0("state_lo", [P, 2, SW], F32R)
            inv = sb0("inv", [P, D // HEAD])
            kv_exp = w0_raw[:, 0, :].rearrange("p (t n) -> p t n", t=4)
            q_exp = w0_raw[:, 1, :].rearrange("p (m n) -> p m n", m=2)

        w1_raw = sb("w1_raw", [P, KD, 2 * HEAD + 2 * D])
        kq_hi = sb("kq_hi", [P, KD, 2, BATCH, P], F32R)
        kq_lo = sb("kq_lo", [P, KD, 2, BATCH, P], F32R)
        og_hi = sb("og_hi", [P, KD, 2 * D], F32R)
        og_lo = sb("og_lo", [P, KD, 2 * D], F32R)
        rec_q = sb("rec_q", [P, SEQ])
        rec_k = sb("rec_k", [P, SEQ])
        run = sb("run", [P, SEQ])
        q_bd = sb("q_bd", [P, NCH, BATCH, CH])
        k_bd = sb("k_bd", [P, NCH, BATCH, CH])
        e_bd = sb("e_bd", [P, NCH, BATCH, CH])
        x_chunk = sb("x_chunk", [P, 2, KD, BATCH, CH])
        sc = sb("sc", [P, 2, P])
        ke = sb("ke", [P, 2, P])
        v_nat = vec[:, V_ROUTE0:V_ROUTE0 + 2 * D].rearrange("p (j n) -> p j n", j=2)
        s_st = row[:, 0:2 * D].rearrange("p (j n) -> p j n", j=2)
        og_gate = w1_raw[:].rearrange("p k n -> p (k n)")[:, 0:KD * BLK].rearrange("p (k n) -> p k n", k=KD)


        x_in = [sem(f"x_in{c}") for c in range(NBLK)]
        const_in = sem("const_in")
        rows_in = sem("rows_in")
        small_in = sem("small_in")
        const_made = sem("const_made")
        raw_in = [sem(f"raw_in{b}") for b in range(2)]
        x_t_in = sem("x_t_in")
        token_tp = sem("token_tp")
        var_done = sem("var_done")
        std_done = sem("std_done")
        nat_normed = sem("nat_normed")
        norm_tp = sem("norm_tp")
        normed = sem("normed")
        norm_hi = sem("norm_hi")
        norm_lo = sem("norm_lo")
        small_hi_done = sem("small_hi_done")
        small_lo_done = sem("small_lo_done")
        logits_done = sem("logits_done")
        score_done = sem("score_done")
        comb_done = sem("comb_done")
        comb_tp = sem("comb_tp")
        comb_t_done = sem("comb_t_done")
        kv_mm = sem("kv_mm")
        kv_biased = sem("kv_biased")
        kv_min = sem("kv_min")
        kv_exped = sem("kv_exped")
        kv_full = sem("kv_full")
        kv_hi_done = sem("kv_hi_done")
        kv_lo_done = sem("kv_lo_done")
        q_mm = sem("q_mm")
        q_biased = sem("q_biased")
        q_min = sem("q_min")
        q_exped = sem("q_exped")
        q_full = sem("q_full")
        q_hi_done = sem("q_hi_done")
        q_lo_done = sem("q_lo_done")
        state_mm = sem("state_mm")
        state_masked = sem("state_masked")
        state_hi_done = sem("state_hi_done")
        state_lo_done = sem("state_lo_done")
        ratio_mm = sem("ratio_mm")
        attn_nat = sem("attn_nat")
        attn_tp = sem("attn_tp")
        projected = sem("projected")
        value_hi_done = sem("value_hi_done")
        state_clear = sem("state_clear")
        attn_done = sem("attn_done")
        attn_hi_done = sem("attn_hi_done")
        attn_lo_done = sem("attn_lo_done")
        gu_hi_done = sem("gu_hi_done")
        gu_lo_done = sem("gu_lo_done")
        dn_hi_done = sem("dn_hi_done")
        dn_lo_done = sem("dn_lo_done")
        cw_mm = sem("cw_mm")
        gate_mm = sem("gate_mm")
        up_mm = sem("up_mm")
        down_mm = sem("down_mm")
        silu_done = sem("silu_done")
        weighted = sem("weighted")
        hid_done = sem("hid_done")
        h_hi_done = sem("h_hi_done")
        h_lo_done = sem("h_lo_done")
        acc_read = sem("acc_read")
        stored = sem("stored")
        gla_kq_mm = sem("gla_kq_mm")
        gla_act = sem("gla_act")
        gla_ready = sem("gla_ready")
        tokens_out = sem("tokens_out")
        softmax_exp = sem("softmax_exp")
        decays_done = sem("decays_done")
        rms_used = sem("rms_used")
        chunk_in = sem("chunk_in")
        v_tp = sem("v_tp")
        v_done = sem("v_done")
        sc_mm = sem("sc_mm")
        sc_done = sem("sc_done")
        upd_mm = sem("upd_mm")
        s_done = sem("s_done")
        o_mm = sem("o_mm")
        o_done = sem("o_done")
        o_hi_done = sem("o_hi_done")
        o_lo_done = sem("o_lo_done")
        osq_done = sem("osq_done")
        ms_mm = sem("ms_mm")
        rms_std = sem("rms_std")
        diag_done = sem("diag_done")
        spread_mm = sem("spread_mm")
        y_added = sem("y_added")
        go_mm = sem("go_mm")
        go_silu = sem("go_silu")
        y_done = sem("y_done")
        chain = sem("chain")
        pool_chain = sem("pool_chain")

        block = ctx.enter_context(nc.Block())

        def blk(c):
            return slice(c * BLK, (c + 1) * BLK)

        @block.sync
        def _(sp):
            def tokens_in(c):
                sp.dma_start(x_tok[:, c], x_nat[blk(c), :].rearrange("(j p) d -> p j d", p=P))\
                    .then_inc(x_in[c], 16)

            tokens_in(0)
            sp.dma_start(cst[:], consts).then_inc(const_in, 16)
            tokens_in(1)
            sp.dma_start(vec[:], vecs).then_inc(rows_in, 16)
            sp.dma_start(row[:], rows.partition_broadcast(P)).then_inc(rows_in, 16)
            for c in range(2, NBLK):
                tokens_in(c)
            sp.dma_start(w0_raw[:], w_attn).then_inc(small_in, 16)

            def load_tile(ph, n, m):
                src, sel = ((moe0, expand0), (moe1, expand1))[ph.layer]
                sp.dma_start(w_raw[:, n % 2, :], src[m]).then_inc(raw_in[n % 2], 16)
                sp.dma_start(e_raw[0:ph.kc, n % 2, :], sel[m]).then_inc(raw_in[n % 2], 16)

            def load_pairs(ph, first, last):
                with sp.Fori(first, last) as i:
                    for j in range(2):
                        n = ph.first + 2 + j
                        sp.wait_ge(dn_lo_done, 2 * i + (n - 1))
                        sp.wait_ge(gu_lo_done, 2 * i + (n - 1))
                        src, sel = ((moe0, expand0), (moe1, expand1))[ph.layer]
                        b = n % 2
                        sp.dma_start(w_raw[:, b, :], src[bass.ds(2 * i + (2 + j), 1), :, :]
                                     .rearrange("a p n -> p (a n)")).then_inc(raw_in[b], 16)
                        sp.dma_start(e_raw[0:ph.kc, b, :], sel[bass.ds(2 * i + (2 + j), 1), :, :]
                                     .rearrange("a p n -> p (a n)")).then_inc(raw_in[b], 16)

            for ph in PHASES:
                if ph.layer == 1 and ph.half == 0:
                    sp.wait_ge(attn_nat, NT)
                    sp.dma_start(w1_raw[:], w_gla).then_inc(small_in, 16)
                for m in range(2):
                    n = ph.first + m
                    if n >= 2:
                        sp.wait_ge(dn_lo_done, n - 1)
                        sp.wait_ge(gu_lo_done, n - 1)
                    load_tile(ph, n, m)
                pairs = (ph.tiles - 2) // 2
                if ph is PHASES[0]:
                    load_pairs(ph, 0, FRAME)
                    sp.wait_ge(norm_tp, NORMS0)
                    sp.dma_start(x[:], x_t).then_inc(x_t_in, 16)
                    load_pairs(ph, FRAME, pairs)
                else:
                    load_pairs(ph, 0, pairs)
                if ph.tiles % 2:
                    n = ph.last - 1
                    sp.wait_ge(dn_lo_done, n - 1)
                    sp.wait_ge(gu_lo_done, n - 1)
                    load_tile(ph, n, ph.tiles - 1)
            for half in range(2):
                for a in range(4):
                    kd, c = a // 2, 2 * half + a % 2
                    sp.wait_ge(acc_read, 8 + 4 * half + a + 1)
                    if half == 0:
                        sp.wait_ge(y_added, c + 1)
                    sp.dma_start(out_t[:, kd, blk(c)], x[:, kd, blk(c)]).then_inc(stored, 16)
            sp.wait_ge(stored, 16 * 8)

        @block.gpsimd
        def _(pool):
            nc.gpsimd.memset(mean_w[:], 1.0 / D)
            nc.gpsimd.memset(ones[:], 1.0)
            nc.gpsimd.memset(state[:], 0.0).then_inc(const_made, 1)
            nc.gpsimd.memset(f(kv_hi[:, :, 2 * D:2 * D + 2]), 1.0).then_inc(const_made, 1)
            nc.gpsimd.memset(f(kv_lo[:, :, 2 * D:2 * D + 2]), 0.0).then_inc(const_made, 1)

            pool.wait_ge(small_in, 16)
            parts = ((w0_hi[:, :, D:3 * D], w0_lo[:, :, D:3 * D], w0_raw[:, :, D:3 * D]),
                     (w0_hi[:, :, 0:D], w0_lo[:, :, 0:D], w0_raw[:, :, 0:D]),
                     (wo_hi[:], wo_lo[:], w0_raw[:, :, 3 * D:4 * D]))
            for n, (hi, lo, raw) in enumerate(parts):
                nc.gpsimd.tensor_copy(hi, raw).then_inc(small_hi_done, 1)
                pool.wait_ge(small_hi_done, n + 1)
                nc.gpsimd.tensor_tensor(lo, raw, f(hi), ALU.subtract).then_inc(small_lo_done, 1)

            def split(hi, lo, whole, hi_done, n):
                nc.gpsimd.tensor_copy(hi, whole).then_inc(hi_done, 1)
                pool.wait_ge(hi_done, n)
                return nc.gpsimd.tensor_tensor(lo, whole, f(hi), ALU.subtract)

            def attention_parts(b):
                if b >= 1:
                    pool.wait_ge(state_mm, 2 * b)
                for t in range(4 * b, 4 * b + 4):
                    pool.wait_ge(kv_biased, t + 1)
                    v = (slice(None), t % 4, slice(D, 2 * D))
                    split(kv_hi[v], kv_lo[v], kv[v], value_hi_done, t + 1)
                k = (slice(None), slice(None), slice(0, D))
                pool.wait_ge(kv_full, b + 1)
                split(kv_hi[k], kv_lo[k], kv[k], kv_hi_done, b + 1).then_inc(kv_lo_done, 1)
                pool.wait_ge(q_full, b + 1)
                if b >= 1:
                    pool.wait_ge(ratio_mm, 4 * b)
                split(q_hi[:], q_lo[:], qf[:], q_hi_done, b + 1).then_inc(q_lo_done, 1)
                if b == 0:
                    for q in range(QUARTERS):
                        cols = slice((8 + 2 * q) * P, (8 + 2 * q + 2) * P)
                        pool.wait_ge(norm_hi, 2 + q + 1)
                        nc.gpsimd.tensor_tensor(xn_lo[:, :, cols], xn[:, :, cols], f(xn_hi[:, :, cols]),
                                                ALU.subtract).then_inc(norm_lo, 1)
                pool.wait_ge(state_masked, 2 * b + 2)
                split(state_hi[:], state_lo[:], state[:], state_hi_done, b + 1).then_inc(state_lo_done, 1)

            def output_low(b):
                pool.wait_ge(attn_hi_done, b + 1)
                nc.gpsimd.tensor_tensor(a_lo[:, :, b % 2, :], xn[:, :, blk(b)], f(a_hi[:, :, b % 2, :]),
                                        ALU.subtract).then_inc(attn_lo_done, 1)

            for b in range(BATCH):
                attention_parts(b)
                if b >= 1:
                    output_low(b - 1)
            output_low(BATCH - 1)

            def norm_parts(half):
                for q in range(QUARTERS):
                    n = NORMS0 + QUARTERS * half + q + 1
                    cols = slice((8 * half + 2 * q) * P, (8 * half + 2 * q + 2) * P)
                    pool.wait_ge(normed, n)
                    nc.gpsimd.tensor_copy(xn_hi[:, :, cols], xn[:, :, cols]).then_inc(norm_hi, 1)
                    pool.wait_ge(norm_hi, n)
                    nc.gpsimd.tensor_tensor(xn_lo[:, :, cols], xn[:, :, cols], f(xn_hi[:, :, cols]),
                                            ALU.subtract).then_inc(norm_lo, 1)

            pool.wait_ge(attn_nat, NT)
            for z in (q_bd[:], k_bd[:], e_bd[:], f(kq_hi[:]), f(kq_lo[:])):
                last = nc.gpsimd.memset(z, 0.0)
            last.then_inc(pool_chain, 1)
            norm_parts(0)
            pool.wait_ge(small_in, 32)
            nc.gpsimd.tensor_copy(og_hi[:], w1_raw[:, :, 2 * HEAD:]).then_inc(pool_chain, 1)
            pool.wait_ge(pool_chain, 2)
            raw = w1_raw[:, :, 0:2 * HEAD].rearrange("p k (w h) -> p k w h", w=2)
            for b in range(BATCH):
                own = (slice(None), slice(None), slice(None), b, slice(32 * b, 32 * b + HEAD))
                nc.gpsimd.tensor_copy(kq_hi[own], raw).then_inc(pool_chain, 1)
            nc.gpsimd.tensor_tensor(og_lo[:], w1_raw[:, :, 2 * HEAD:], f(og_hi[:]), ALU.subtract)\
                .then_inc(small_lo_done, 1)
            pool.wait_ge(pool_chain, 2 + BATCH)
            for b in range(BATCH):
                own = (slice(None), slice(None), slice(None), b, slice(32 * b, 32 * b + HEAD))
                nc.gpsimd.tensor_tensor(kq_lo[own], raw, f(kq_hi[own]), ALU.subtract).then_inc(small_lo_done, 1)

            norm_parts(1)

            def chunk_values(i):
                if i >= 2:
                    pool.wait_ge(v_tp, i - 1)
                nc.gpsimd.tensor_copy(x_chunk[:, i % 2],
                                      xn[:].rearrange("p k (b c s) -> p c k b s", b=BATCH, s=CH)[:, i])\
                    .then_inc(chunk_in, 1)

            chunk_values(0)
            chunk_values(1)
            pool.wait_ge(decays_done, 1)
            nc.gpsimd.memset(s_st[:, 0, :], 0.0).then_inc(state_clear, 1)
            for i in range(2, NCH):
                chunk_values(i)

            for c in range(NBLK + 1):
                if c < NBLK:
                    pool.wait_ge(o_hi_done, c + 1)
                    if c >= 2:
                        pool.wait_ge(go_mm, 2 * (c - 1))
                    nc.gpsimd.tensor_tensor(a_lo[:, :, c % 2, :], xn[:, :, blk(c)], f(a_hi[:, :, c % 2, :]),
                                            ALU.subtract).then_inc(o_lo_done, 1)
                if c >= 1:
                    pool.wait_ge(y_done, c)
                    nc.gpsimd.tensor_tensor(x[:, :, blk(c - 1)], x[:, :, blk(c - 1)], xn[:, :, blk(c - 1)],
                                            ALU.add).then_inc(y_added, 1)

        @block.tensor
        def _(pe):
            def three(out, w, wsl, m, msl, start, stop):
                (wh, wl), (mh, ml) = w, m
                pe.matmul(out, wh[wsl], mh[msl], start=start, stop=False, skip_group_check=True)
                pe.matmul(out, wh[wsl], ml[msl], start=False, stop=False, skip_group_check=True)
                return pe.matmul(out, wl[wsl], mh[msl], start=False, stop=stop, skip_group_check=True)

            XN = (xn_hi, xn_lo)
            W0, WO = (w0_hi, w0_lo), (wo_hi, wo_lo)
            KQ, OG = (kq_hi, kq_lo), (og_hi, og_lo)
            everything = slice(None)

            def to_width(c):
                pe.wait_ge(nat_normed, c + 1)
                for k in range(KD):
                    for j in range(4):
                        mm = pe.transpose(bank[4 + 2 * (c % 2) + k][:, j * P:(j + 1) * P],
                                          x_tok[:, c, j, k * P:(k + 1) * P], cst[:, C_ID:C_ID + P])
                mm.then_inc(norm_tp, 1)

            def logits(tiles, to, n_e, v0):
                for t in tiles:
                    at = t % 8 * n_e
                    for k in range(KD):
                        mm = pe.matmul(to[:, at:at + P], xn[:, k, t * P:(t + 1) * P],
                                       vec[:, v0 + k * P:v0 + (k + 1) * P], start=k == 0, stop=k == 1)
                mm.then_inc(logits_done, 1)

            def logits0(c):
                pe.wait_ge(rows_in, 32)
                pe.wait_ge(normed, c + 1)
                logits(range(4 * c, 4 * c + 4), bank[2], E0, V_ROUTE0)

            def combine_turn(c, kc, to):
                for j in range(4):
                    mm = pe.transpose(to[0:kc, j * P:(j + 1) * P], comb[:, 4 * c + j, 0:kc], cst[:, C_ID:C_ID + P])
                mm.then_inc(comb_tp, 1)

            pe.wait_ge(const_in, 16)
            for c in range(2):
                to_width(c)
            for c in range(2):
                logits0(c)
            side = bank[3]

            def turn_width0(q):
                pe.wait_ge(nat_normed, 2 + q + 1)
                if q == 0:
                    pe.wait_ge(q_biased, 2)
                else:
                    pe.wait_ge(norm_hi, 2 + q)
                for k in range(KD):
                    for j in range(2):
                        t = 8 + 2 * q + j
                        mm = pe.transpose(side[:, (2 * k + j) * P:(2 * k + j + 1) * P],
                                          x_tok[:, t // 4, t % 4, k * P:(k + 1) * P], cst[:, C_ID:C_ID + P])
                mm.then_inc(norm_tp, 1)

            def kv_product(t):
                b = t // 4
                pe.wait_ge(norm_lo, b + 1 if b < 2 else NORMS0)
                pe.wait_ge(small_lo_done, 3)
                if t % 4:
                    pe.wait_ge(kv_biased, t)
                elif b >= 1:
                    pe.wait_ge(state_masked, 2 * b)
                for k in range(KD):
                    mm = three(side, XN, (everything, k, slice(t * P, t * P + P)),
                               W0, (everything, k, slice(D, 3 * D)), k == 0, k == 1)
                mm.then_inc(kv_mm, 1)

            def query_product(b, m):
                if m == 0:
                    pe.wait_ge(kv_biased, 4 * b + 4)
                else:
                    pe.wait_ge(q_biased, 2 * b + 1)
                for k in range(KD):
                    mm = three(side, W0, (everything, k, slice(m * P, m * P + P)),
                               XN, (everything, k, blk(b)), k == 0, k == 1)
                mm.then_inc(q_mm, 1)

            def state_product(b, hb):
                pe.wait_ge(kv_lo_done, b + 1)
                if hb == 1:
                    pe.wait_ge(state_masked, 2 * b + 1)
                elif b == 0:
                    pe.wait_ge(const_made, 3)
                    pe.wait_ge(score_done, 2)
                else:
                    pe.wait_ge(attn_done, 2 * b)
                for j in range(4):
                    mm = three(side[:, 0:D + 2], (kv_hi, kv_lo), (everything, j, slice(hb * P, hb * P + P)),
                               (kv_hi, kv_lo), (everything, j, slice(D, 2 * D + 2)), j == 0, j == 3)
                mm.then_inc(state_mm, 1)

            def ratio_product(t):
                b, j = t // 4, t % 4
                pe.wait_ge(state_lo_done, b + 1)
                pe.wait_ge(q_lo_done, b + 1)
                if j:
                    pe.wait_ge(attn_nat, t)
                elif b + 1 < BATCH:
                    pe.wait_ge(q_biased, 2 * (b + 1) + 2)
                else:
                    pe.wait_ge(state_masked, 2 * BATCH)
                for hb in range(2):
                    mm = three(side[:, 0:SW], (q_hi, q_lo), (everything, hb, slice(j * P, j * P + P)),
                               (state_hi, state_lo), (everything, hb, everything), hb == 0, hb == 1)
                mm.then_inc(ratio_mm, 1)

            def attn_turn(b, k):
                pe.wait_ge(attn_nat, 4 * b + 4)
                if k == 1:
                    pe.wait_ge(attn_done, 2 * b + 1)
                for j in range(4):
                    mm = pe.transpose(side[:, j * P:(j + 1) * P], a_nat[:, j, k * P:(k + 1) * P],
                                      cst[:, C_ID:C_ID + P])
                mm.then_inc(attn_tp, 1)

            def out_product(b, m, start):
                pe.wait_ge(attn_lo_done, b + 1)
                for k in range(KD):
                    mm = three(bank[4 + 2 * m + b % 2][:], WO, (everything, k, slice(m * P, m * P + P)),
                               (a_hi, a_lo), (everything, k, b % 2, everything), start and k == 0, False)
                mm.then_inc(projected, 1)

            def step0(n, end):
                b, m = n // FRAME, n % FRAME
                if b < BATCH and m < QUERY_AT:
                    kv_product(4 * b + 2 * (m - KV_AT) + end)
                elif b < BATCH and m == QUERY_AT:
                    query_product(b, end)
                elif b == 0 and WIDTH0_AT <= m < WIDTH0_AT + 2:
                    turn_width0(2 * (m - WIDTH0_AT) + end)
                elif b == 0 and m == LOGITS0_AT:
                    pe.wait_ge(normed, NORMS0)
                    logits(range(8 + 4 * end, 12 + 4 * end), side, E0, V_ROUTE0)
                elif b >= 1 and RATIO_AT <= m < RATIO_AT + 2:
                    ratio_product(4 * (b - 1) + 2 * (m - RATIO_AT) + end)
                elif b < BATCH and m == STATE_AT:
                    state_product(b, end)
                elif b >= 1 and m == TURN_AT:
                    attn_turn(b - 1, end)
                elif 2 <= b < BATCH and m == OUT_PARTS_AT:
                    out_product(b - 2, end, False)
                elif n == COMB0_AT:
                    pe.wait_ge(comb_done, 2)
                    if end == 0:
                        pe.wait_ge(attn_done, 2 * BATCH)
                    else:
                        pe.wait_ge(comb_t_done, 3)
                    combine_turn(2 + end, KC0, side)

            def turn_tokens(half, q):
                if q == 0:
                    pe.wait_ge(acc_read, 4 * (half + 1))
                    if half == 1:
                        pe.wait_ge(comb_t_done, NBLK + 2)
                else:
                    pe.wait_ge(tokens_out, QUARTERS * half + q)
                for j in range(2):
                    t = 8 * half + 2 * q + j
                    for k in range(KD):
                        mm = pe.transpose(side[:, j * D + k * P:j * D + (k + 1) * P],
                                          x[:, k, t * P:(t + 1) * P], cst[:, C_ID:C_ID + P])
                mm.then_inc(token_tp, 1)

            def turn_width(half, q):
                n = NORMS0 + QUARTERS * half + q
                pe.wait_ge(nat_normed, n + 1)
                if q == 0:
                    pe.wait_ge(tokens_out, QUARTERS * (half + 1))
                else:
                    pe.wait_ge(normed, n)
                for k in range(KD):
                    for j in range(2):
                        mm = pe.transpose(side[:, (2 * k + j) * P:(2 * k + j + 1) * P],
                                          turned[:, q, j, k * P:(k + 1) * P], cst[:, C_ID:C_ID + P])
                mm.then_inc(norm_tp, 1)

            def recurrence_product(w):
                pe.wait_ge(norm_lo, NORMS0 + 2 * QUARTERS)
                pe.wait_ge(small_lo_done, 4 + BATCH)
                if w == 0:
                    pe.wait_ge(score_done, 4)
                else:
                    pe.wait_ge(gla_act, 1)
                for b in range(BATCH):
                    for k in range(KD):
                        mm = three(side[:], KQ, (everything, k, w, b, everything),
                                   XN, (everything, k, blk(b)), b == 0 and k == 0, b == 3 and k == 1)
                mm.then_inc(gla_kq_mm, 1)

            def combine1(half, s):
                c = 2 * half + s
                pe.wait_ge(comb_done, 3 + half)
                if s == 1:
                    pe.wait_ge(comb_t_done, NBLK + c)
                elif half == 1:
                    pe.wait_ge(gla_act, 2)
                combine_turn(c, KC1, side)

            def chunk_front(i):
                pe.wait_ge(chunk_in, i + 1)
                if i == 0:
                    pe.wait_ge(gla_ready, 1)
                    pe.wait_ge(comb_t_done, 2 * NBLK)
                else:
                    pe.wait_ge(o_done, i)
                    pe.wait_ge(s_done, i)
                for k in range(KD):
                    pe.transpose(side[:, k * P:(k + 1) * P], x_chunk[:, i % 2, k].rearrange("p b s -> p (b s)"),
                                 cst[:, C_ID:C_ID + P])
                pe.transpose(side[:, D:D + P], e_bd[:, i].rearrange("p b s -> p (b s)"),
                             cst[:, C_ID:C_ID + P]).then_inc(v_tp, 1)
                pe.matmul(side[:, D + P:D + 2 * P], k_bd[:, i].rearrange("p b s -> p (b s)"),
                          q_bd[:, i].rearrange("p b s -> p (b s)"), start=True, stop=True).then_inc(sc_mm, 1)

            def chunk_back(i):
                pe.wait_ge(v_done, i + 1)
                pe.wait_ge(sc_done, i + 1)
                if i == 0:
                    pe.wait_ge(state_clear, 1)
                pe.matmul(side[:, 0:D], ke[:, i % 2, :], v_nat[:, i % 2, :], start=True, stop=True,
                          skip_group_check=True).then_inc(upd_mm, 1)
                for m in range(KD):
                    o = side[:, D + m * P:D + (m + 1) * P]
                    pe.matmul(o, v_nat[:, i % 2, m * P:(m + 1) * P], sc[:, i % 2, :], start=True, stop=False,
                              skip_group_check=True)
                    mm = pe.matmul(o, s_st[:, i % 2, m * P:(m + 1) * P],
                                   q_bd[:, i].rearrange("p b s -> p (b s)"), start=False, stop=True,
                                   skip_group_check=True)
                mm.then_inc(o_mm, 1)

            def mean_square(c):
                pe.wait_ge(osq_done, c + 1)
                if c == 0:
                    pe.wait_ge(s_done, NCH)
                for t in range(4 * c, 4 * c + 4):
                    j = t % 4
                    for k in range(KD):
                        mm = pe.matmul(side[:, t:t + P], square[:, c % 2, k, j * P:(j + 1) * P],
                                       mean_w[:], start=k == 0, stop=k == 1)
                mm.then_inc(ms_mm, 1)

            def spread(c):
                pe.wait_ge(diag_done, c + 1)
                if c == 0:
                    pe.wait_ge(rms_std, 1)
                else:
                    pe.wait_ge(go_silu, 2 * c)
                pe.matmul(side[:], ones[:], std[:, c % 2, :], start=True, stop=True).then_inc(spread_mm, 1)

            def gate_product(c, m):
                pe.wait_ge(o_lo_done, c + 1)
                if m == 0:
                    pe.wait_ge(rms_used, c + 1)
                else:
                    pe.wait_ge(go_silu, 2 * c + 1)
                for k in range(KD):
                    three(side[:], OG, (everything, k, slice(D + m * P, D + m * P + P)),
                          XN, (everything, k, blk(c)), k == 0, False)
                for k in range(KD):
                    mm = three(side[:], OG, (everything, k, slice(m * P, m * P + P)),
                               (a_hi, a_lo), (everything, k, c % 2, everything), False, k == 1)
                mm.then_inc(go_mm, 1)

            def step1(half, n):
                if TOKENS_AT <= n < STD_AT:
                    turn_tokens(half, n - TOKENS_AT)
                elif WIDTH_AT <= n < LOGITS_AT:
                    turn_width(half, n - WIDTH_AT)
                elif n == LOGITS_AT:
                    pe.wait_ge(normed, NORMS0 + QUARTERS * (half + 1))
                    logits(range(8 * half, 8 * half + 8), side, E1, V_ROUTE1)
                elif COMB_AT <= n < HALF_DONE:
                    combine1(half, n - COMB_AT)
                elif half == 1 and KQ_AT <= n < KQ_AT + 2:
                    recurrence_product(n - KQ_AT)
                elif half == 1 and CHUNKS_AT <= n < MEAN_AT:
                    chunk_front(n - CHUNKS_AT)
                elif half == 1 and MEAN_AT <= n < OUT_AT:
                    mean_square(n - MEAN_AT)
                elif half == 1 and OUT_AT <= n < OUT_AT + 3 * NBLK:
                    c, part = (n - OUT_AT) // 3, (n - OUT_AT) % 3
                    if part == 0:
                        spread(c)
                    else:
                        gate_product(c, part - 1)

            def step1_end(half, n):
                if half == 1 and CHUNKS_AT <= n < MEAN_AT:
                    chunk_back(n - CHUNKS_AT)

            def combine_product(ph, par, toks):
                pe.matmul(bank[2][:], e_sel[0:ph.kc, par, :], comb_t[0:ph.kc, toks],
                          start=True, stop=True).then_inc(cw_mm, 1)

            def unit_front(ph, i, tb, ub, beside=False):
                par, s, u, tile = tb % 2, ub % 2, 4 * i + ub, 2 * i + tb
                toks = blk(2 * ph.half + s)
                pe.wait_ge(gu_lo_done, tile + 1)
                if needed(u):
                    pe.wait_ge(weighted, u)
                    combine_product(ph, par, toks)
                if needed(u):
                    pe.wait_ge(silu_done, u)
                for k in range(KD):
                    mm = three(bank[0][:], (w_gu_hi, w_gu_lo), (everything, par, slice(k * P, k * P + P)),
                               XN, (everything, k, toks), k == 0, k == 1)
                mm.then_inc(gate_mm, 1)
                if beside:
                    step(ph, ub, 0)
                if needed(u):
                    pe.wait_ge(hid_done, u)
                for k in range(KD):
                    mm = three(bank[1][:], (w_gu_hi, w_gu_lo), (everything, par, slice(D + k * P, D + k * P + P)),
                               XN, (everything, k, toks), k == 0, k == 1)
                mm.then_inc(up_mm, 1)

            def unit_down(ph, i, tb, ub, first=False, last=False):
                par, s, u, tile = tb % 2, ub % 2, 4 * i + ub, 2 * i + tb
                pe.wait_ge(dn_lo_done, tile + 1)
                pe.wait_ge(h_lo_done, u + 1)
                for m in range(KD):
                    if first and ph.first:
                        pe.wait_ge(acc_read, 4 * PHASES.index(ph) - 4 + 2 * m + s + 1)
                    mm = three(bank[4 + 2 * m + s][:], (w_dn_hi, w_dn_lo), (everything, par, slice(m * P, m * P + P)),
                               (h_hi, h_lo), (everything, s, everything), first, last)
                mm.then_inc(down_mm, 1)

            def step(ph, u, end):
                n = aside(ph, u)
                if ph is PHASES[0]:
                    step0(u, end)
                elif end == 0:
                    step1(*n)
                else:
                    step1_end(*n)

            def experts(ph):
                t0 = ph.first

                def two_tiles(i, tb, ub, beside=False):
                    for j in range(4):
                        unit_front(ph, i, tb + (j + 1) // 2, ub + j + 1, beside)
                        if ph is PHASES[1] and beside and ub + j == 2 * t0:
                            begin_half1()
                        unit_down(ph, i, tb + j // 2, ub + j,
                                  first=beside and ub + j < 2 * t0 + 2 and ph is not PHASES[1])
                        if beside:
                            step(ph, ub + j + 1, 1)

                if ph is PHASES[0]:
                    begin_half0()
                step(ph, 2 * t0, 1)
                for i in range(ph.peel):
                    two_tiles(0, t0 + 2 * i, 2 * t0 + 4 * i, True)
                if ph.peel < ph.pairs:
                    with pe.Fori(ph.peel, ph.pairs) as i:
                        two_tiles(i, t0, 2 * t0)
                beside = ph.layer == 1
                for u in range(2 * (t0 + 2 * ph.pairs), 2 * ph.last):
                    if u + 1 < 2 * ph.last:
                        unit_front(ph, 0, (u + 1) // 2, u + 1, beside)
                    elif ph is not PHASES[-1]:
                        first_front(PHASES[PHASES.index(ph) + 1])
                    unit_down(ph, 0, u // 2, u, last=u // 2 == ph.last - 1)
                    if beside and u + 1 < 2 * ph.last:
                        step(ph, u + 1, 1)

            def first_front(ph):
                if ph.layer == 0:
                    pe.wait_ge(norm_lo, (2, NORMS0)[ph.half])
                else:
                    pe.wait_ge(norm_lo, NORMS0 + QUARTERS * (ph.half + 1))
                if ph.first:
                    pe.wait_ge(comb_t_done, NBLK * ph.layer + 2 * ph.half + 2)
                unit_front(ph, 0, ph.first, 2 * ph.first, True)

            def begin_half0():
                pe.wait_ge(comb_done, 1)
                for c in range(2):
                    combine_turn(c, KC0, bank[4 + c])
                pe.wait_ge(comb_t_done, 2)
                pe.wait_ge(score_done, 1)
                combine_product(PHASES[0], 0, blk(0))

            def begin_half1():
                for m in range(KD):
                    for s in range(2):
                        pe.wait_ge(acc_read, 2 * m + s + 1)
                        out_product(2 + s, m, True)

            first_front(PHASES[0])
            for ph in PHASES:
                experts(ph)

        @block.scalar
        def _(act):
            def norm_std(c):
                act.wait_ge(var_done, c + 1)
                nc.scalar.activation(rstd[:, 4 * c:4 * c + 4], mean_var[:, 4 * c:4 * c + 4, 1], ACT.Sqrt,
                                     bias=cst[:, C_EPS:C_EPS + 1]).then_inc(std_done, 1)

            def scores(half, source):
                act.wait_ge(logits_done, 2 * half + 2)
                nc.scalar.activation(score[:, 8 * half:8 * half + 8].rearrange("p t e -> p (t e)"),
                                     source[:, 0:8 * E0], ACT.Sigmoid).then_inc(score_done, 1)

            act.wait_ge(const_in, 16)
            norm_std(0)
            norm_std(1)
            for c in range(2):
                act.wait_ge(norm_tp, c + 1)
                nc.scalar.copy(xn[:, :, blk(c)], banks[:, 4 + 2 * c:6 + 2 * c, :]).then_inc(normed, 1)
            scores(0, bank[2])
            for c in range(2):
                act.wait_ge(normed, c + 1)
                nc.scalar.copy(xn_hi[:, :, blk(c)], xn[:, :, blk(c)]).then_inc(norm_hi, 1)
            norm_std(2)
            norm_std(3)

            def comb_copy(c, n, kc, source):
                act.wait_ge(comb_tp, n + 1)
                nc.scalar.copy(comb_t[0:kc, blk(c)], source[0:kc, :]).then_inc(comb_t_done, 1)

            side = bank[3]

            def norm_quarter(q):
                n = 2 + q + 1
                cols = slice((8 + 2 * q) * P, (8 + 2 * q + 2) * P)
                act.wait_ge(norm_tp, n)
                nc.scalar.copy(xn[:, :, cols], side.rearrange("p (k n) -> p k n", k=KD)).then_inc(normed, 1)
                act.wait_ge(normed, n)
                nc.scalar.copy(xn_hi[:, :, cols], xn[:, :, cols]).then_inc(norm_hi, 1)

            def exponentials(b):
                act.wait_ge(kv_min, 4 * b + 4)
                nc.scalar.activation(kv_exp, kv_exp, ACT.Exp).then_inc(kv_exped, 1)
                act.wait_ge(q_min, 2 * b + 2)
                nc.scalar.activation(q_exp, q_exp, ACT.Exp).then_inc(q_exped, 1)

            def attn_evac(b, k):
                act.wait_ge(attn_tp, 2 * b + k + 1)
                nc.scalar.copy(xn[:, k, blk(b)], side).then_inc(attn_done, 1)

            def attn_high(b):
                act.wait_ge(attn_done, 2 * b + 2)
                if b >= 2:
                    act.wait_ge(projected, 2 * (b - 1))
                nc.scalar.copy(a_hi[:, :, b % 2, :], xn[:, :, blk(b)]).then_inc(attn_hi_done, 1)

            def step0(n, end):
                b, m = n // FRAME, n % FRAME
                if n == 0 and end == 0:
                    for c in range(2):
                        comb_copy(c, c, KC0, bank[4 + c])
                if b == 0 and WIDTH0_AT <= m < WIDTH0_AT + 2:
                    norm_quarter(2 * (m - WIDTH0_AT) + end)
                if b == 0 and m == LOGITS0_AT and end == 1:
                    scores(1, side)
                if b < BATCH and m == EXP_AT and end == 0:
                    exponentials(b)
                if b >= 1 and m == TURN_AT:
                    attn_evac(b - 1, end)
                if n == COMB0_AT:
                    comb_copy(2 + end, 2 + end, KC0, side)
                if b >= 1 and m == OUT_PARTS_AT and end == 1:
                    attn_high(b - 1)

            def chunk_act(i):
                act.wait_ge(sc_mm, i + 1)
                if i >= 2:
                    act.wait_ge(o_mm, i - 1)
                nc.scalar.copy(v_nat[:, i % 2, :], side[:, 0:D])
                nc.scalar.copy(ke[:, i % 2, :], side[:, D:D + P]).then_inc(v_done, 1)

            def o_out(i):
                act.wait_ge(o_mm, i + 1)
                act.wait_ge(s_done, i + 1)
                for m in range(KD):
                    cp = nc.scalar.copy(
                        xn[:, m, :].rearrange("p (b c s) -> p c b s", b=BATCH, s=CH)[:, i],
                        side[:, D + m * P:D + (m + 1) * P].rearrange("p (b s) -> p b s", b=BATCH))
                cp.then_inc(o_done, 1)

            def o_square(c):
                act.wait_ge(o_done, NCH)
                if c >= 2:
                    act.wait_ge(ms_mm, c - 1)
                nc.scalar.activation(square[:, c % 2], xn[:, :, blk(c)], ACT.Square).then_inc(osq_done, 1)

            def o_high(c):
                if c >= 2:
                    act.wait_ge(go_mm, 2 * (c - 1))
                nc.scalar.copy(a_hi[:, :, c % 2, :], xn[:, :, blk(c)]).then_inc(o_hi_done, 1)

            def step1(half, n):
                eps = cst[:, C_EPS:C_EPS + 1]
                tiles = slice(8 * half, 8 * half + 8)
                if n < TOKENS_AT:
                    return
                if n < STD_AT:
                    q = n - TOKENS_AT
                    act.wait_ge(token_tp, QUARTERS * half + q + 1)
                    nc.scalar.copy(turned[:, q], side.rearrange("p (j d) -> p j d", d=D)).then_inc(tokens_out, 1)
                elif n == STD_AT:
                    act.wait_ge(var_done, NBLK + half + 1)
                    nc.scalar.activation(rstd[:, tiles], mean_var[:, tiles, 1], ACT.Sqrt, bias=eps)\
                        .then_inc(std_done, 1)
                elif n < LOGITS_AT:
                    q = n - WIDTH_AT
                    act.wait_ge(norm_tp, NORMS0 + QUARTERS * half + q + 1)
                    nc.scalar.copy(xn[:, :, (8 * half + 2 * q) * P:(8 * half + 2 * q + 2) * P],
                                   side.rearrange("p (k n) -> p k n", k=KD)).then_inc(normed, 1)
                elif n == ROUTE_AT:
                    if half == 1:
                        act.wait_ge(gla_kq_mm, 1)
                        nc.scalar.activation(rec_q[:], side[:], ACT.Silu).then_inc(gla_act, 1)
                    act.wait_ge(score_done, 3 + half)
                    nc.scalar.activation(pick[:, tiles, 0:E1], score[:, tiles, 0:E1], ACT.Exp)\
                        .then_inc(softmax_exp, 1)
                elif COMB_AT <= n < HALF_DONE:
                    c = 2 * half + n - COMB_AT
                    comb_copy(c, NBLK + c, KC1, side)
                elif half == 1 and n == KQ_AT + 1:
                    act.wait_ge(gla_kq_mm, 2)
                    nc.scalar.activation(rec_k[:], side[:], ACT.Sigmoid).then_inc(gla_act, 1)
                    act.wait_ge(gla_act, 2)
                    nc.scalar.activation(std[:, 0, :], rec_k[:], ACT.Sigmoid, scale=-1.0).then_inc(gla_act, 1)
                elif half == 1 and CHUNKS_AT <= n < MEAN_AT:
                    chunk_act(n - CHUNKS_AT)
                elif half == 1 and n == OUT_AT - 1:
                    act.wait_ge(ms_mm, NBLK)
                    nc.scalar.activation(rstd[:], side[:, 0:NT], ACT.Sqrt, bias=eps).then_inc(rms_std, 1)
                elif half == 1 and OUT_AT <= n < OUT_AT + 3 * NBLK and (n - OUT_AT) % 3:
                    c, m = (n - OUT_AT) // 3, (n - OUT_AT) % 3 - 1
                    act.wait_ge(go_mm, 2 * c + m + 1)
                    if c >= 1:
                        act.wait_ge(y_done, c)
                    nc.scalar.activation(og_gate[:, m, :], side[:], ACT.Silu).then_inc(go_silu, 1)

            def step1_end(half, n):
                if half == 0:
                    return
                if CHUNKS_AT <= n < MEAN_AT:
                    o_out(n - CHUNKS_AT)
                if MEAN_AT - 1 <= n < OUT_AT - 1:
                    o_square(n - MEAN_AT + 1)
                for c, at in enumerate((OUT_AT - 2, OUT_AT - 1, OUT_AT + 3, OUT_AT + 6)):
                    if n == at:
                        o_high(c)

            def step(ph, u, end):
                n = aside(ph, u)
                if ph is PHASES[0]:
                    step0(u, end)
                elif end == 0:
                    step1(*n)
                else:
                    step1_end(*n)

            def split_gu(ph, i, tb):
                par = tb % 2
                act.wait_ge(raw_in[par], 32 * i + 32 * (tb // 2 + 1))
                if needed(4 * i + 2 * tb - 2):
                    act.wait_ge(up_mm, 4 * i + (2 * tb - 2))
                nc.scalar.copy(e_sel[0:ph.kc, par, :], e_raw[0:ph.kc, par, :]).then_inc(gu_hi_done, 1)
                nc.scalar.copy(w_gu_hi[:, par, :], w_raw[:, par, 0:2 * D]).then_inc(gu_hi_done, 1)

            def split_dn(i, tb):
                par = tb % 2
                if needed(4 * i + 2 * tb - 2):
                    act.wait_ge(down_mm, 4 * i + (2 * tb - 2))
                nc.scalar.copy(w_dn_hi[:, par, :], w_raw[:, par, 2 * D:3 * D]).then_inc(dn_hi_done, 1)

            def unit(ph, ph_next, i, tb, ub, beside=False):
                s = ub % 2
                act.wait_ge(gate_mm, 4 * i + (ub + 1))
                if needed(4 * i + ub - 1):
                    act.wait_ge(h_lo_done, 4 * i + (ub - 1))
                nc.scalar.activation(gate[:, s, :], bank[0][:], ACT.Silu).then_inc(silu_done, 1)
                if beside:
                    step(ph, ub, 0)
                if ph_next is not None:
                    if s == 0:
                        split_gu(ph_next, i, tb + 1)
                    else:
                        split_dn(i, tb + 1)
                act.wait_ge(hid_done, 4 * i + (ub + 1))
                if needed(4 * i + ub - 1):
                    act.wait_ge(down_mm, 4 * i + (ub - 1))
                nc.scalar.copy(h_hi[:, s, :], gate[:, s, :]).then_inc(h_hi_done, 1)
                if beside:
                    step(ph, ub, 1)

            def experts(ph):
                t0 = ph.first

                def two_tiles(i, tb, ub, beside=False):
                    for j in range(4):
                        unit(ph, ph, i, tb + j // 2, ub + j, beside)

                for i in range(ph.peel):
                    two_tiles(0, t0 + 2 * i, 2 * t0 + 4 * i, True)
                if ph.peel < ph.pairs:
                    with act.Fori(ph.peel, ph.pairs) as i:
                        two_tiles(i, t0, 2 * t0)
                for u in range(2 * (t0 + 2 * ph.pairs), 2 * ph.last):
                    tile = u // 2
                    nxt = ph if tile + 1 < ph.last else PHASES[PHASES.index(ph) + 1] if tile + 1 < ALL_TILES else None
                    unit(ph, nxt, 0, tile, u, ph.layer == 1)

            split_gu(PHASES[0], 0, 0)
            split_dn(0, 0)
            experts(PHASES[0])
            experts(PHASES[1])

            for half in range(2):
                experts(PHASES[2 + half])

        @block.vector
        def _(dve):
            links = [0]

            def link(ins):
                links[0] += 1
                ins.then_inc(chain, 1)
                dve.wait_ge(chain, links[0])

            v = nc.vector

            def over_width(ap):
                return ap.unsqueeze(1).to_broadcast([P, KD, BLK])

            def stats(tiles, tokens):
                for n, t in enumerate(tiles):
                    last = v.bn_stats(bn[:, t, :], tokens(n))
                link(last)
                for t in tiles:
                    last = v.bn_aggr(mean_var[:, t, :], bn[:, t, :])
                return last

            def normalise(tiles, tokens):
                for n, t in enumerate(tiles):
                    last = v.tensor_scalar(tokens(n), tokens(n), mean_var[:, t, 0:1], rstd[:, t:t + 1],
                                           ALU.subtract, ALU.mult)
                last.then_inc(nat_normed, 1)

            def norm_stats(c):
                dve.wait_ge(x_in[c], 16)
                stats(range(4 * c, 4 * c + 4), lambda j: x_tok[:, c, j, :]).then_inc(var_done, 1)

            def norm_apply(c):
                dve.wait_ge(std_done, c + 1)
                link(v.reciprocal(rstd[:, 4 * c:4 * c + 4], rstd[:, 4 * c:4 * c + 4]))
                normalise(range(4 * c, 4 * c + 4), lambda j: x_tok[:, c, j, :])

            def norm():
                norm_stats(0)
                norm_stats(1)
                norm_apply(0)
                norm_apply(1)
                norm_stats(2)
                norm_stats(3)

            def norm_quarter(q):
                t = 8 + 2 * q
                normalise(range(t, t + 2), lambda j: x_tok[:, (t + j) // 4, (t + j) % 4, :])

            def norm_low(c):
                dve.wait_ge(norm_hi, c + 1)
                v.tensor_tensor(xn_lo[:, :, blk(c)], xn[:, :, blk(c)], f(xn_hi[:, :, blk(c)]),
                                ALU.subtract).then_inc(norm_lo, 1)

            def wide(nt, n):
                return tuple(c[:, 0:nt * n * n].rearrange("p (t a b) -> p t a b", t=nt, a=n) for c in compare)

            def rank_compare(values, nt, n, tri):
                a, b = wide(nt, n)
                own = values.unsqueeze(3).to_broadcast([P, nt, n, n])
                other = values.unsqueeze(2).to_broadcast([P, nt, n, n])
                v.tensor_tensor(a, other, own, ALU.is_gt)
                link(v.tensor_tensor(b, other, own, ALU.is_equal))

            def rank_ties(values, nt, n, tri):
                a, b = wide(nt, n)
                link(v.tensor_tensor(b, b, tri.rearrange("p (a b) -> p a b", b=n).unsqueeze(1)
                                     .to_broadcast([P, nt, n, n]), ALU.mult))
                link(v.tensor_tensor(a, a, b, ALU.add))

            def rank_count(nt, n, limit, out):
                link(v.tensor_reduce(rank[:, 0:nt, 0:n], wide(nt, n)[0], AX_X, ALU.add))
                link(v.tensor_scalar(out, rank[:, 0:nt, 0:n], float(limit), None, ALU.is_lt))

            def combine_parts(tiles, w, n_e):
                link(v.tensor_copy(comb[:, tiles, 0:n_e].bitcast(F32R), w))
                v.tensor_tensor(comb[:, tiles, n_e:2 * n_e], w, comb[:, tiles, 0:n_e], ALU.subtract)
                v.memset(comb[:, tiles, 2 * n_e:2 * n_e + 1], 1.0).then_inc(comb_done, 1)

            def route0(half, piece):
                nt = NT // 2
                tiles = slice(nt * half, nt * half + nt)
                sc, pk, rp, gr, total = (t[:, tiles] for t in (score, pick, rep, group, tot))
                best, rest = top[:, tiles], rank[:, tiles]
                if piece == 0:
                    dve.wait_ge(score_done, half + 1)
                    eb = row[:, R_EB:R_EB + E0].unsqueeze(1).to_broadcast([P, nt, E0])
                    link(v.tensor_tensor(pk, sc, eb, ALU.add))
                    four = pk.rearrange("p t (g a b) -> p t g a b", g=G0, a=2)
                    hi, lo = pair[0][:, 0], pair[0][:, 1]
                    v.tensor_tensor(hi, four[:, :, :, :, 0], four[:, :, :, :, 1], ALU.max)
                    link(v.tensor_tensor(lo, four[:, :, :, :, 0], four[:, :, :, :, 1], ALU.min))
                    one, two, three_ = pair[1][:, 0, :, :, 0], pair[1][:, 0, :, :, 1], pair[1][:, 1, :, :, 0]
                    v.tensor_tensor(one, hi[:, :, :, 0], hi[:, :, :, 1], ALU.max)
                    v.tensor_tensor(two, hi[:, :, :, 0], hi[:, :, :, 1], ALU.min)
                    link(v.tensor_tensor(three_, lo[:, :, :, 0], lo[:, :, :, 1], ALU.max))
                    link(v.tensor_tensor(two, two, three_, ALU.max))
                    link(v.tensor_tensor(gr, one, two, ALU.add))
                elif piece == 1:
                    for t in range(nt):
                        m = v.max(best[:, t, :], gr[:, t, :])
                    link(m)
                    link(v.memset(best[:, :, TOPG0:8], 3e38))
                    for t in range(nt):
                        m = v.match_replace(rest[:, t, :], best[:, t, :], gr[:, t, :], -3e38)
                    link(m)
                elif piece == 2:
                    link(v.tensor_tensor(gr, rest, gr, ALU.not_equal))
                    link(v.tensor_tensor(pk.rearrange("p t (g e) -> p t g e", g=G0),
                                         pk.rearrange("p t (g e) -> p t g e", g=G0),
                                         gr.unsqueeze(3).to_broadcast([P, nt, G0, E0 // G0]), ALU.mult))
                elif piece == 3:
                    for t in range(nt):
                        m = v.max(top[:, nt * half + t, :], pk[:, t, :])
                    link(m)
                elif piece == 4:
                    for t in range(nt):
                        m = v.match_replace(rp[:, t, :], top[:, nt * half + t, :], pk[:, t, :], -3e38)
                    link(m)
                elif piece == 5:
                    link(v.tensor_tensor(rp, rp, pk, ALU.not_equal))
                    link(v.tensor_tensor(rp, rp, sc, ALU.mult))
                    link(v.tensor_reduce(total[:, :, 0], rp, AX_X, ALU.add))
                elif piece == 6:
                    link(v.tensor_scalar(total, total, 1e-20, None, ALU.add))
                    link(v.reciprocal(total, total))
                    link(v.tensor_tensor(rp, rp, total.to_broadcast([P, nt, E0]), ALU.mult))
                    link(v.tensor_scalar(rp, rp, SCALE0, None, ALU.mult))
                    combine_parts(tiles, rp, E0)

            def split_gu(i, tb):
                par = tb % 2
                dve.wait_ge(gu_hi_done, 4 * i + (2 * tb + 2))
                if needed(4 * i + 2 * tb - 2):
                    dve.wait_ge(up_mm, 4 * i + (2 * tb - 2))
                v.tensor_tensor(w_gu_lo[:, par, :], w_raw[:, par, 0:2 * D], f(w_gu_hi[:, par, :]),
                                ALU.subtract).then_inc(gu_lo_done, 1)

            def split_dn(i, tb):
                par = tb % 2
                dve.wait_ge(dn_hi_done, 2 * i + (tb + 1))
                if needed(4 * i + 2 * tb - 2):
                    dve.wait_ge(down_mm, 4 * i + (2 * tb - 2))
                v.tensor_tensor(w_dn_lo[:, par, :], w_raw[:, par, 2 * D:3 * D], f(w_dn_hi[:, par, :]),
                                ALU.subtract).then_inc(dn_lo_done, 1)

            norm()
            dve.wait_ge(const_in, 16)
            dve.wait_ge(rows_in, 32)
            for piece in range(len(ROUTE0_AT)):
                route0(0, piece)
                if piece < 2:
                    norm_low(piece)
                if piece == 2:
                    split_gu(0, 0)
                    split_dn(0, 0)

            side = bank[3]

            def kv_bias(t):
                b, j = t // 4, t % 4
                dve.wait_ge(kv_mm, t + 1)
                if t == 0:
                    dve.wait_ge(small_lo_done, 3)
                if b >= 1:
                    dve.wait_ge(kv_lo_done, b)
                v.tensor_tensor(kv[:, j, :], side, row[:, R_BKV:R_BKV + 2 * D], ALU.add).then_inc(kv_biased, 1)
                dve.wait_ge(kv_biased, t + 1)
                v.tensor_scalar(kv_exp[:, j, :], kv[:, j, 0:D], 0.0, None, ALU.min).then_inc(kv_min, 1)

            def query_bias(b, m):
                u = 2 * b + m
                dve.wait_ge(q_mm, u + 1)
                if b >= 1:
                    dve.wait_ge(q_lo_done, b)
                v.tensor_scalar(qf[:, m, :], side, vec[:, V_BQ + m:V_BQ + m + 1], None, ALU.add).then_inc(q_biased, 1)
                dve.wait_ge(q_biased, u + 1)
                v.tensor_scalar(q_exp[:, m, :], qf[:, m, :], 0.0, None, ALU.min).then_inc(q_min, 1)

            def elu_plus_one(values, exps):
                return v.scalar_tensor_tensor(out=values, in0=values, scalar=0.0, in1=exps,
                                              op0=ALU.max, op1=ALU.add)

            def mask_state(u):
                b, hb = u // 2, u % 2
                dve.wait_ge(state_mm, u + 1)
                if b >= 1:
                    dve.wait_ge(state_lo_done, b)
                v.tensor_tensor(state[:, hb, hb * P:hb * P + P], side[:, hb * P:hb * P + P],
                                cst[:, C_HEADS:C_HEADS + P], ALU.mult)
                own = C_HSEL + hb * (D // HEAD)
                v.tensor_scalar(state[:, hb, D:SW], cst[:, own:own + D // HEAD], side[:, D:D + 1], None,
                                ALU.mult).then_inc(state_masked, 1)

            def ratio(t):
                nh = D // HEAD
                dve.wait_ge(ratio_mm, t + 1)
                link(v.tensor_scalar(inv[:], side[:, D:SW], TINY, None, ALU.add))
                link(v.reciprocal(inv[:], inv[:]))
                if t >= 4:
                    dve.wait_ge(attn_tp, t // 4 * 2)
                v.tensor_tensor(a_nat[:, t % 4].rearrange("p (h e) -> p h e", h=nh),
                                side[:, 0:D].rearrange("p (h e) -> p h e", h=nh),
                                inv[:].unsqueeze(2).to_broadcast([P, nh, HEAD]), ALU.mult).then_inc(attn_nat, 1)

            def step0(n, end):
                b, m = n // FRAME, n % FRAME
                if b < BATCH and m < QUERY_AT:
                    kv_bias(4 * b + 2 * (m - KV_AT) + end)
                if b < BATCH and m == QUERY_AT:
                    query_bias(b, end)
                if b >= 1 and RATIO_AT <= m < RATIO_AT + 2:
                    ratio(4 * (b - 1) + 2 * (m - RATIO_AT) + end)
                if b < BATCH and m == EXP_AT and end == 1:
                    dve.wait_ge(kv_exped, b + 1)
                    elu_plus_one(kv[:, :, 0:D], kv_exp).then_inc(kv_full, 1)
                if b < BATCH and m == EXP_AT + 1 and end == 1:
                    dve.wait_ge(q_exped, b + 1)
                    elu_plus_one(qf[:], q_exp).then_inc(q_full, 1)
                if b < BATCH and m == STATE_AT:
                    mask_state(2 * b + end)
                if n == 0 and end == 1:
                    dve.wait_ge(std_done, NBLK)
                    link(v.reciprocal(rstd[:, 8:NT], rstd[:, 8:NT]))
                if n < 2 and end == 1:
                    norm_quarter(2 * n)
                    norm_quarter(2 * n + 1)
                if n in ROUTE0_AT and end == 1:
                    route0(1, ROUTE0_AT.index(n))

            def route1(half, n):
                nt = NT // 2
                tiles = slice(nt * half, nt * half + nt)
                w8, ex, total = score[:, tiles, 0:E1], pick[:, tiles, 0:E1], tot[:, tiles]
                two = ex.rearrange("p t (g e) -> p t g e", g=G1)
                gr, masked = group[:, tiles, 0:G1], rep[:, tiles, 0:E1]
                best, rest = top[:, tiles], rank[:, tiles]
                group_order = (gr, nt, G1, cst[:, C_TRI:C_TRI + G1 * G1])
                if n == LOGITS_AT:
                    dve.wait_ge(logits_done, NBLK + half + 1)
                    link(v.tensor_copy(w8, side[:, 0:nt * E1].rearrange("p (t e) -> p t e", e=E1)))
                    link(v.tensor_reduce(total[:, :, 0], w8, AX_X, ALU.max))
                    v.tensor_tensor(w8, w8, total.to_broadcast([P, nt, E1]), ALU.subtract).then_inc(score_done, 1)
                elif n == ROUTE_AT:
                    dve.wait_ge(softmax_exp, half + 1)
                    link(v.tensor_reduce(total[:, :, 0], ex, AX_X, ALU.add))
                    link(v.reciprocal(total, total))
                    link(v.tensor_tensor(ex, ex, total.to_broadcast([P, nt, E1]), ALU.mult))
                    link(v.tensor_tensor(gr, two[:, :, :, 0], two[:, :, :, 1], ALU.max))
                elif n == ROUTE_AT + 1:
                    rank_compare(*group_order)
                    rank_ties(*group_order)
                elif n == ROUTE_AT + 2:
                    rank_count(nt, G1, TOPG1, gr)
                    link(v.tensor_tensor(masked.rearrange("p t (g e) -> p t g e", g=G1), two,
                                         gr.unsqueeze(3).to_broadcast([P, nt, G1, E1 // G1]), ALU.mult))
                elif n == ROUTE_AT + 3:
                    for t in range(nt):
                        last = v.max(best[:, t, :], masked[:, t, :])
                    link(last)
                    link(v.memset(best[:, :, TOPK1:8], 3e38))
                elif n == ROUTE_AT + 4:
                    for t in range(nt):
                        last = v.match_replace(rest[:, t, :], best[:, t, :], masked[:, t, :], -3e38)
                    link(last)
                elif n == ROUTE_AT + 5:
                    link(v.tensor_tensor(rest, rest, masked, ALU.not_equal))
                    link(v.tensor_tensor(masked, masked, rest, ALU.mult))
                    combine_parts(tiles, masked, E1)

            def decays(part):
                decay, first = std[:, 0, :], std[:, 1, :]
                starts = cst[:, C_START:C_START + SEQ]
                h = SEQ // 2
                if part == 0:
                    dve.wait_ge(gla_act, 3)
                    link(v.tensor_tensor(first, decay, starts, ALU.mult))
                    link(v.tensor_tensor(decay, decay, first, ALU.subtract))
                    link(v.tensor_tensor_scan(run[:], decay, first, 0.0, ALU.mult, ALU.add))
                elif part == 1:
                    link(v.reciprocal(first[:, 0:h], run[:, 0:h]))
                elif part == 2:
                    link(v.reciprocal(first[:, h:SEQ], run[:, h:SEQ]))
                elif part == 3:
                    v.scalar_tensor_tensor(out=rec_q[:], in0=rec_q[:], scalar=GLA_SCALE, in1=run[:],
                                           op0=ALU.mult, op1=ALU.mult)
                    link(v.tensor_tensor(rec_k[:], rec_k[:], first, ALU.mult))
                    ends = run[:].rearrange("p (c s) -> p c s", s=CH)[:, :, CH - 1:CH]
                    v.tensor_tensor(decay.rearrange("p (c s) -> p c s", s=CH),
                                    rec_k[:].rearrange("p (c s) -> p c s", s=CH),
                                    ends.to_broadcast([P, NCH, CH]), ALU.mult).then_inc(decays_done, 1)
                else:
                    dve.wait_ge(decays_done, 1)
                    dve.wait_ge(pool_chain, 1)
                    for b in range(2 * (part - 4), 2 * (part - 4) + 2):
                        r = slice(32 * b, 32 * b + 32)
                        for dst, src in ((q_bd, rec_q[:]), (k_bd, rec_k[:]), (e_bd, decay)):
                            cp = v.tensor_copy(dst[r, :, b, :], src[r, :].rearrange("p (c s) -> p c s", s=CH))
                    if part == 5:
                        cp.then_inc(gla_ready, 1)

            def chunk_scores(i):
                dve.wait_ge(sc_mm, i + 1)
                dve.wait_ge(v_done, i + 1)
                if i >= 2:
                    dve.wait_ge(o_mm, i - 1)
                v.tensor_tensor(sc[:, i % 2, :], side[:, D + P:D + 2 * P], cst[:, C_CAUSAL:C_CAUSAL + P],
                                ALU.mult).then_inc(sc_done, 1)

            def chunk_state(i):
                dve.wait_ge(upd_mm, i + 1)
                dve.wait_ge(o_mm, i + 1)
                if i == 0:
                    dve.wait_ge(state_clear, 1)
                else:
                    dve.wait_ge(s_done, i)
                v.scalar_tensor_tensor(out=s_st[:, (i + 1) % 2, :], in0=s_st[:, i % 2, :],
                                       scalar=run[:, (i + 1) * CH - 1:(i + 1) * CH], in1=side[:, 0:D],
                                       op0=ALU.mult, op1=ALU.add).then_inc(s_done, 1)

            def diagonal(c):
                if c >= 2:
                    dve.wait_ge(spread_mm, c - 1)
                for j in range(4):
                    last = v.tensor_scalar(std[:, c % 2, j * P:(j + 1) * P], cst[:, C_ID:C_ID + P],
                                           rstd[:, 4 * c + j:4 * c + j + 1], None, ALU.mult)
                last.then_inc(diag_done, 1)

            def output(c, part):
                if part == 0:
                    dve.wait_ge(spread_mm, c + 1)
                    dve.wait_ge(o_lo_done, c + 1)
                    v.tensor_tensor(xn[:, :, blk(c)], xn[:, :, blk(c)], over_width(side), ALU.mult)\
                        .then_inc(rms_used, 1)
                    return
                m = part - 1
                dve.wait_ge(rms_used, c + 1)
                dve.wait_ge(go_silu, 2 * c + m + 1)
                last = v.scalar_tensor_tensor(out=xn[:, m, blk(c)], in0=xn[:, m, blk(c)],
                                              scalar=vec[:, V_GW + m:V_GW + m + 1], in1=og_gate[:, m, :],
                                              op0=ALU.mult, op1=ALU.mult)
                if m == 1:
                    last.then_inc(y_done, 1)

            def step1(half, n):
                if half == 1 and CHUNKS_AT <= n < MEAN_AT:
                    chunk_scores(n - CHUNKS_AT)
                if half == 1 and OUT_AT <= n < OUT_AT + 3 * NBLK and (n - OUT_AT) % 3 == 0:
                    output((n - OUT_AT) // 3, 0)

            def step1_end(half, n):
                if TOKENS_AT <= n < STD_AT:
                    q = n - TOKENS_AT
                    t = 8 * half + 2 * q
                    dve.wait_ge(tokens_out, QUARTERS * half + q + 1)
                    last = stats(range(t, t + 2), lambda j: turned[:, q, j, :])
                    if n == STD_AT - 1:
                        last.then_inc(var_done, 1)
                if STD_AT <= n < STD_AT + 2:
                    if n == STD_AT:
                        dve.wait_ge(std_done, NBLK + half + 1)
                        own = rstd[:, 8 * half:8 * half + 8]
                        link(v.reciprocal(own, own))
                    for q in range(2 * (n - STD_AT), 2 * (n - STD_AT) + 2):
                        t = 8 * half + 2 * q
                        normalise(range(t, t + 2), lambda j: turned[:, q, j, :])
                route1(half, n)
                if half == 0:
                    return
                if DECAY_AT <= n < DECAY_AT + 6:
                    decays(n - DECAY_AT)
                if CHUNKS_AT <= n < MEAN_AT:
                    chunk_state(n - CHUNKS_AT)
                if n == OUT_AT - 1:
                    dve.wait_ge(rms_std, 1)
                    link(v.reciprocal(rstd[:], rstd[:]))
                    diagonal(0)
                    diagonal(1)
                if OUT_AT <= n < OUT_AT + 3 * NBLK and (n - OUT_AT) % 3:
                    output((n - OUT_AT) // 3, (n - OUT_AT) % 3)
                for c, at in ((2, OUT_AT + 1), (3, OUT_AT + 4)):
                    if n == at:
                        diagonal(c)

            def step(ph, u, end):
                n = aside(ph, u)
                if ph is PHASES[0]:
                    step0(u, end)
                elif end == 0:
                    step1(*n)
                else:
                    step1_end(*n)

            def sums(ph):
                dve.wait_ge(down_mm, 2 * ph.last)
                if ph is PHASES[0]:
                    dve.wait_ge(x_t_in, 16)
                if ph is PHASES[3]:
                    dve.wait_ge(y_added, NBLK)
                for a in range(4):
                    kd, c = a // 2, 2 * ph.half + a % 2
                    if ph.layer == 0:
                        v.scalar_tensor_tensor(out=x[:, kd, blk(c)], in0=bank[4 + a][:],
                                               scalar=vec[:, V_BO + kd:V_BO + kd + 1], in1=x[:, kd, blk(c)],
                                               op0=ALU.add, op1=ALU.add).then_inc(acc_read, 1)
                    else:
                        v.tensor_tensor(x[:, kd, blk(c)], bank[4 + a][:], x[:, kd, blk(c)],
                                        ALU.add).then_inc(acc_read, 1)

            def unit(split, i, tb, ub, ph=None):
                s = ub % 2
                dve.wait_ge(silu_done, 4 * i + (ub + 1))
                dve.wait_ge(cw_mm, 4 * i + (ub + 1))
                v.tensor_tensor(gate[:, s, :], gate[:, s, :], bank[2][:], ALU.mult).then_inc(weighted, 1)
                if ph is not None:
                    step(ph, ub, 0)
                dve.wait_ge(up_mm, 4 * i + (ub + 1))
                dve.wait_ge(weighted, 4 * i + (ub + 1))
                v.tensor_tensor(gate[:, s, :], gate[:, s, :], bank[1][:], ALU.mult).then_inc(hid_done, 1)
                if ph is not None and ph.first and ub == 2 * ph.first:
                    sums(PHASES[PHASES.index(ph) - 1])
                if split:
                    if s == 0:
                        split_gu(i, tb + 1)
                    else:
                        split_dn(i, tb + 1)
                dve.wait_ge(h_hi_done, 4 * i + (ub + 1))
                if needed(4 * i + ub - 1):
                    dve.wait_ge(down_mm, 4 * i + (ub - 1))
                v.tensor_tensor(h_lo[:, s, :], gate[:, s, :], f(h_hi[:, s, :]), ALU.subtract).then_inc(h_lo_done, 1)
                if ph is not None:
                    step(ph, ub, 1)

            def experts(ph):
                t0 = ph.first

                def two_tiles(i, tb, ub, beside=None):
                    for j in range(4):
                        unit(True, i, tb + j // 2, ub + j, beside)

                for i in range(ph.peel):
                    two_tiles(0, t0 + 2 * i, 2 * t0 + 4 * i, ph)
                if ph.peel < ph.pairs:
                    with dve.Fori(ph.peel, ph.pairs) as i:
                        two_tiles(i, t0, 2 * t0)
                for u in range(2 * (t0 + 2 * ph.pairs), 2 * ph.last):
                    unit(u // 2 + 1 < ALL_TILES, 0, u // 2, u, ph if ph.layer == 1 else None)

            experts(PHASES[0])
            experts(PHASES[1])

            experts(PHASES[2])
            experts(PHASES[3])
            sums(PHASES[3])


def _constants():
    c = np.zeros((P, C_ALL), np.float32)
    p = np.arange(P)
    c[:, C_ID:C_ID + P] = np.eye(P)
    c[:, C_HEADS:C_HEADS + P] = p[:, None] // HEAD == p[None] // HEAD
    same = p[:, None] // CH == p[None] // CH
    c[:, C_CAUSAL:C_CAUSAL + P] = same & (p[:, None] <= p[None])
    c[:, C_START:C_START + SEQ] = np.arange(SEQ) % CH == 0
    for hb in range(2):
        heads = np.arange(D // HEAD)
        c[:, C_HSEL + hb * len(heads):C_HSEL + (hb + 1) * len(heads)] = heads[None] == (hb * P + p[:, None]) // HEAD
    c[:, C_EPS] = LN_EPS
    g = np.arange(G1)
    c[:, C_TRI:C_TRI + G1 * G1] = (g[None] < g[:, None]).reshape(1, -1)
    return c


def _selectors(tiles, experts, width):
    e = np.zeros((2 * experts + 1, tiles * P), np.float32)
    feature = np.arange(experts * width)
    e[feature // width, feature] = 1
    e[experts + feature // width, feature] = 1
    e[2 * experts, experts * width:experts * width + SHARED] = 1
    return np.ascontiguousarray(e.reshape(-1, tiles, P).transpose(1, 0, 2))


def _by_partition(a):
    return np.ascontiguousarray(a.reshape(KD, P, -1).transpose(1, 0, 2))


def _feature_tiles(tiles, gates, ups, downs, sg, su, sd):
    def rows(w, s):
        a = np.zeros((tiles * P, D), np.float32)
        n = w.shape[0] * w.shape[1]
        a[:n] = w.reshape(n, D)
        a[n:n + s.shape[0]] = s
        return a.reshape(tiles, P, D)

    out = np.empty((tiles, P, 3 * D), np.float32)
    for k, a in ((0, rows(gates, sg)), (1, rows(ups, su))):
        out[:, :, k * D:(k + 1) * D] = a.reshape(tiles, P, KD, P).transpose(0, 3, 2, 1).reshape(tiles, P, D)
    out[:, :, 2 * D:] = rows(downs.transpose(0, 2, 1), sd.T)
    return out


def kernel(**inputs):
    import concourse.bacc as bacc
    from concourse.bass_utils import run_bass_kernel_spmd

    a = {k: np.asarray(v) for k, v in inputs.items()}
    vecs = np.zeros((P, V_ALL), np.float32)
    for at, name in ((V_BQ, "L0_attn_bq"), (V_BO, "L0_attn_bo"), (V_GW, "L1_attn_g_weight")):
        vecs[:, at:at + KD] = a[name].reshape(KD, P).T
    for at, name in ((V_ROUTE0, "L0_ffn_router_weight"), (V_ROUTE1, "L1_ffn_gate_weight")):
        w = _by_partition(a[name].T)
        for k in range(KD):
            vecs[:, at + k * P:at + k * P + w.shape[2]] = w[:, k]
    data = {
        "x_nat": a["L0_attn_x"].reshape(T, D),
        "x_t": _by_partition(a["L0_attn_x"].reshape(T, D).T),
        "w_attn": _by_partition(np.concatenate([a[f"L0_attn_w{n}"].T for n in "qkvo"], axis=1)),
        "vecs": vecs,
        "rows": np.concatenate([a["L0_attn_bk"], a["L0_attn_bv"], a["L0_ffn_e_bias"]]),
        "consts": _constants(),
        "w_gla": _by_partition(np.concatenate([a[f"L1_attn_{n}"].T for n in ("Wq", "Wk", "Wog", "Wig")], axis=1)),
        "moe0": _feature_tiles(TILES0, *(a[f"L0_ffn_{n}"] for n in ("Wg", "Wu", "Wd", "sWg", "sWu", "sWd"))),
        "moe1": _feature_tiles(TILES1, *(a[f"L1_ffn_{n}"] for n in ("gate_w", "up_w", "down_w", "sh_gate_w",
                                                                  "sh_up_w", "sh_down_w"))),
        "expand0": _selectors(TILES0, E0, F0),
        "expand1": _selectors(TILES1, E1, F1),
    }
    nc = bacc.Bacc("TRN2", target_bir_lowering=False, num_devices=1,
                   dynamic_dma_scratch_size=1024)
    arrays, args = {}, {}
    for name, v in data.items():
        arrays[f"in_{name}"] = v
        args[name] = nc.dram_tensor(f"in_{name}", v.shape, mybir.dt.from_np(v.dtype), kind="ExternalInput").ap()
    args["out_t"] = nc.dram_tensor("out_t", (P, KD, T), F32, kind="ExternalOutput").ap()
    build(nc, **args)
    got = run_bass_kernel_spmd(nc, [arrays], core_ids=[0]).results[0]["out_t"]
    return np.ascontiguousarray(got.transpose(1, 0, 2).reshape(D, T).T).reshape(BATCH, SEQ, D)
```
